# Optimizing a Trainium2 kernel written in Bass

```python
import numpy as np
import jax
import jax.numpy as jnp

def _softmax(x, axis=-1):
    return jax.nn.softmax(x, axis=axis)

def _gelu(x):
    return jax.nn.gelu(x, approximate=True)

def _silu(x):
    return jax.nn.silu(x)

def _sigmoid(x):
    return jax.nn.sigmoid(x)

def _layernorm(x, axis=-1, eps=1e-05):
    m = jnp.mean(x, axis=axis, keepdims=True)
    v = jnp.var(x, axis=axis, keepdims=True)
    return (x - m) / jnp.sqrt(v + eps)

def _scatter_add(tgt, idx, src, axis=0):
    return tgt.at[idx].add(src)

def _segment_sum(src, seg, n):
    return jax.ops.segment_sum(src, seg, n)
kernel_name = 'mk_gps_d1_gnn_r32_f9f635'

def setup_inputs(seed: int=0):
    np.random.seed(seed)
    _w = jnp.asarray

    def _rec_inputs():
        import jax
        import jax.numpy as jnp
        _gk = jax.random.key(seed)
        x = 0.0009128 + 1.001 * jax.random.normal(jax.random.fold_in(_gk, 1), (3125, 256), jnp.float32)
        _s = jax.random.randint(jax.random.fold_in(_gk, 2), (25000,), 0, 3125, jnp.int32)
        _d = jax.random.randint(jax.random.fold_in(_gk, 3), (25000,), 0, 3125, jnp.int32)
        _loop = jnp.arange(3125, dtype=jnp.int32)
        src = jnp.concatenate([_s, _d, _loop])
        dst = jnp.concatenate([_d, _s, _loop])
        _o = jnp.argsort(dst, stable=True)
        src = src[_o]
        dst = dst[_o]
        edge_attr_3 = -0.000563758 + 1.00031 * jax.random.normal(jax.random.fold_in(_gk, 11), (53125, 3), jnp.float32)
        return (x, src, dst, edge_attr_3)
    x, src, dst, edge_attr_3 = _rec_inputs()

    def _L0_gnn_setup():
        import jax, jax.numpy as jnp
        import numpy as np
        MUL = 64
        N_NODES = 10000
        N_EDGES = 10000
        DIM = MUL + 3 * MUL
        SQ3 = float(np.sqrt(3.0))
        INV_MUL = float(1.0 / np.sqrt(MUL))
        INV_TP = float(1.0 / np.sqrt(2 * MUL))

        def _split(f):
            return (f[:, :MUL], f[:, MUL:].reshape(f.shape[0], MUL, 3))

        def _lin(x0, x1, w0, w1):
            return (x0 @ w0 * INV_MUL, jnp.einsum('eum,uv->evm', x1, w1) * INV_MUL)

        def _fctp(x0, x1, sh1, w00, w11, w01, w10):
            dot = jnp.einsum('eum,em->eu', x1, sh1) / SQ3
            out0 = (x0 @ w00 + dot @ w11) * INV_TP
            out1 = (jnp.einsum('eu,uv->ev', x0, w01)[:, :, None] * sh1[:, None, :] + jnp.einsum('eum,uv->evm', x1, w10)) * INV_TP
            return (out0, out1)

        def _forward(atom_feature, edge_vector, weights, edge_index):
            ls0, ls1, ld0, ld1, t1_00, t1_11, t1_01, t1_10, t2_00, t2_11, t2_01, t2_10, lh0, lh1, lsc = weights
            src, dst = (edge_index[0], edge_index[1])
            r = edge_vector / (jnp.linalg.norm(edge_vector, axis=-1, keepdims=True) + 1e-12)
            sh1 = SQ3 * r
            x0, x1 = _split(atom_feature)
            s0, s1 = _lin(x0[src], x1[src], ls0, ls1)
            d0, d1 = _lin(x0[dst], x1[dst], ld0, ld1)
            h0, h1 = _fctp(s0, s1, sh1, t1_00, t1_11, t1_01, t1_10)
            h0, h1 = _lin(h0, h1, lh0, lh1)
            sc = jax.nn.leaky_relu(h0) @ lsc * INV_MUL
            full = jnp.concatenate([sc, jnp.zeros((sc.shape[0], 3 * MUL), sc.dtype)], axis=-1)
            act = jax.nn.softmax(full, axis=-1)
            o0, o1 = _fctp(h0, h1, sh1, t2_00, t2_11, t2_01, t2_10)
            tp2_flat = jnp.concatenate([o0, o1.reshape(o1.shape[0], 3 * MUL)], axis=-1)
            msgs = act * tp2_flat
            agg = jax.ops.segment_sum(msgs, dst, num_segments=atom_feature.shape[0])
            return atom_feature + agg
        _WNAMES = ['lin_src_w0', 'lin_src_w1', 'lin_dst_w0', 'lin_dst_w1', 'tp1_w00', 'tp1_w11', 'tp1_w01', 'tp1_w10', 'tp2_w00', 'tp2_w11', 'tp2_w01', 'tp2_w10', 'lin_hidden_w0', 'lin_hidden_w1', 'lin_scalar_w']
        key = jax.random.key(seed)
        ks = jax.random.split(key, 18)
        inp = {n: jax.random.normal(ks[i], (MUL, MUL), jnp.float32) for i, n in enumerate(_WNAMES)}
        inp['atom_feature'] = jax.random.normal(ks[15], (N_NODES, DIM), jnp.float32)
        inp['edge_vector'] = jax.random.normal(ks[16], (N_EDGES, 3), jnp.float32)
        inp['edge_index'] = jax.random.randint(ks[17], (2, N_EDGES), 0, N_NODES, dtype=jnp.int32)
        return inp
    _L0_gnn_all = _L0_gnn_setup()
    _L0_gnn_in = {k: v for k, v in _L0_gnn_all.items() if k in ('lin_src_w0', 'lin_src_w1', 'lin_dst_w0', 'lin_dst_w1', 'tp1_w00', 'tp1_w11', 'tp1_w01', 'tp1_w10', 'tp2_w00', 'tp2_w11', 'tp2_w01', 'tp2_w10', 'lin_hidden_w0', 'lin_hidden_w1', 'lin_scalar_w')}
    del _L0_gnn_all

    def _L0_mix_setup():
        import jax, jax.numpy as jnp
        import numpy as np
        EPS = 1e-05

        def _layernorm(x, weight, bias):
            mean = jnp.mean(x, axis=-1, keepdims=True)
            std = jnp.std(x, axis=-1, keepdims=True, ddof=1)
            out = (x - mean) / (std + EPS)
            return weight * out + bias
        key = jax.random.key(seed)
        B, N, C = (4, 1024, 256)
        H, hc = (8, C // 8)
        kx, = jax.random.split(key, 1)
        x = jax.random.normal(kx, (B, N, C), dtype=jnp.float32)
        return {'x': x, 'kln_weight': jnp.ones((H, 1, hc), dtype=jnp.float32), 'kln_bias': jnp.zeros((H, 1, hc), dtype=jnp.float32), 'vln_weight': jnp.ones((H, 1, hc), dtype=jnp.float32), 'vln_bias': jnp.zeros((H, 1, hc), dtype=jnp.float32)}
    _L0_mix_all = _L0_mix_setup()
    _L0_mix_in = {k: v for k, v in _L0_mix_all.items() if k in ('kln_weight', 'kln_bias', 'vln_weight', 'vln_bias')}
    del _L0_mix_all

    def _L0_ffn_setup():
        import jax, jax.numpy as jnp
        import numpy as np
        TOP_K = 2
        key = jax.random.key(seed)
        ks = jax.random.split(key, 4)
        B, L, D, H, E = (8, 128, 256, 1024, 8)
        s = 0.02
        return {'x': jax.random.normal(ks[0], (B, L, D), jnp.float32), 'Wg': jax.random.normal(ks[1], (D, E), jnp.float32) * s, 'bg': jnp.zeros((E,), jnp.float32), 'W1': jax.random.normal(ks[2], (E, D, H), jnp.float32) * s, 'b1': jnp.zeros((E, H), jnp.float32), 'W2': jax.random.normal(ks[3], (E, H, D), jnp.float32) * s, 'b2': jnp.zeros((E, D), jnp.float32)}
    _L0_ffn_all = _L0_ffn_setup()
    _L0_ffn_in = {k: v for k, v in _L0_ffn_all.items() if k in ('Wg', 'bg', 'W1', 'b1', 'W2', 'b2')}
    del _L0_ffn_all
    return {'x': x, 'src': src, 'dst': dst, 'edge_attr_3': edge_attr_3, 'L0_gnn_lin_src_w0': _L0_gnn_in['lin_src_w0'], 'L0_gnn_lin_src_w1': _L0_gnn_in['lin_src_w1'], 'L0_gnn_lin_dst_w0': _L0_gnn_in['lin_dst_w0'], 'L0_gnn_lin_dst_w1': _L0_gnn_in['lin_dst_w1'], 'L0_gnn_tp1_w00': _L0_gnn_in['tp1_w00'], 'L0_gnn_tp1_w11': _L0_gnn_in['tp1_w11'], 'L0_gnn_tp1_w01': _L0_gnn_in['tp1_w01'], 'L0_gnn_tp1_w10': _L0_gnn_in['tp1_w10'], 'L0_gnn_tp2_w00': _L0_gnn_in['tp2_w00'], 'L0_gnn_tp2_w11': _L0_gnn_in['tp2_w11'], 'L0_gnn_tp2_w01': _L0_gnn_in['tp2_w01'], 'L0_gnn_tp2_w10': _L0_gnn_in['tp2_w10'], 'L0_gnn_lin_hidden_w0': _L0_gnn_in['lin_hidden_w0'], 'L0_gnn_lin_hidden_w1': _L0_gnn_in['lin_hidden_w1'], 'L0_gnn_lin_scalar_w': _L0_gnn_in['lin_scalar_w'], 'L0_mix_kln_weight': _L0_mix_in['kln_weight'], 'L0_mix_kln_bias': _L0_mix_in['kln_bias'], 'L0_mix_vln_weight': _L0_mix_in['vln_weight'], 'L0_mix_vln_bias': _L0_mix_in['vln_bias'], 'L0_ffn_Wg': _L0_ffn_in['Wg'], 'L0_ffn_bg': _L0_ffn_in['bg'], 'L0_ffn_W1': _L0_ffn_in['W1'], 'L0_ffn_b1': _L0_ffn_in['b1'], 'L0_ffn_W2': _L0_ffn_in['W2'], 'L0_ffn_b2': _L0_ffn_in['b2']}

def reference(x, src, dst, edge_attr_3, L0_gnn_lin_src_w0, L0_gnn_lin_src_w1, L0_gnn_lin_dst_w0, L0_gnn_lin_dst_w1, L0_gnn_tp1_w00, L0_gnn_tp1_w11, L0_gnn_tp1_w01, L0_gnn_tp1_w10, L0_gnn_tp2_w00, L0_gnn_tp2_w11, L0_gnn_tp2_w01, L0_gnn_tp2_w10, L0_gnn_lin_hidden_w0, L0_gnn_lin_hidden_w1, L0_gnn_lin_scalar_w, L0_mix_kln_weight, L0_mix_kln_bias, L0_mix_vln_weight, L0_mix_vln_bias, L0_ffn_Wg, L0_ffn_bg, L0_ffn_W1, L0_ffn_b1, L0_ffn_W2, L0_ffn_b2):
    import jax
    import jax.numpy as jnp

    def _L0_gnn_ref(atom_feature, edge_vector, lin_src_w0, lin_src_w1, lin_dst_w0, lin_dst_w1, tp1_w00, tp1_w11, tp1_w01, tp1_w10, tp2_w00, tp2_w11, tp2_w01, tp2_w10, lin_hidden_w0, lin_hidden_w1, lin_scalar_w, edge_index):
        import jax, jax.numpy as jnp
        import numpy as np
        MUL = 64
        N_NODES = 10000
        N_EDGES = 10000
        DIM = MUL + 3 * MUL
        SQ3 = float(np.sqrt(3.0))
        INV_MUL = float(1.0 / np.sqrt(MUL))
        INV_TP = float(1.0 / np.sqrt(2 * MUL))

        def _split(f):
            return (f[:, :MUL], f[:, MUL:].reshape(f.shape[0], MUL, 3))

        def _lin(x0, x1, w0, w1):
            return (x0 @ w0 * INV_MUL, jnp.einsum('eum,uv->evm', x1, w1) * INV_MUL)

        def _fctp(x0, x1, sh1, w00, w11, w01, w10):
            dot = jnp.einsum('eum,em->eu', x1, sh1) / SQ3
            out0 = (x0 @ w00 + dot @ w11) * INV_TP
            out1 = (jnp.einsum('eu,uv->ev', x0, w01)[:, :, None] * sh1[:, None, :] + jnp.einsum('eum,uv->evm', x1, w10)) * INV_TP
            return (out0, out1)

        def _forward(atom_feature, edge_vector, weights, edge_index):
            ls0, ls1, ld0, ld1, t1_00, t1_11, t1_01, t1_10, t2_00, t2_11, t2_01, t2_10, lh0, lh1, lsc = weights
            src, dst = (edge_index[0], edge_index[1])
            r = edge_vector / (jnp.linalg.norm(edge_vector, axis=-1, keepdims=True) + 1e-12)
            sh1 = SQ3 * r
            x0, x1 = _split(atom_feature)
            s0, s1 = _lin(x0[src], x1[src], ls0, ls1)
            d0, d1 = _lin(x0[dst], x1[dst], ld0, ld1)
            h0, h1 = _fctp(s0, s1, sh1, t1_00, t1_11, t1_01, t1_10)
            h0, h1 = _lin(h0, h1, lh0, lh1)
            sc = jax.nn.leaky_relu(h0) @ lsc * INV_MUL
            full = jnp.concatenate([sc, jnp.zeros((sc.shape[0], 3 * MUL), sc.dtype)], axis=-1)
            act = jax.nn.softmax(full, axis=-1)
            o0, o1 = _fctp(h0, h1, sh1, t2_00, t2_11, t2_01, t2_10)
            tp2_flat = jnp.concatenate([o0, o1.reshape(o1.shape[0], 3 * MUL)], axis=-1)
            msgs = act * tp2_flat
            agg = jax.ops.segment_sum(msgs, dst, num_segments=atom_feature.shape[0])
            return atom_feature + agg
        _WNAMES = ['lin_src_w0', 'lin_src_w1', 'lin_dst_w0', 'lin_dst_w1', 'tp1_w00', 'tp1_w11', 'tp1_w01', 'tp1_w10', 'tp2_w00', 'tp2_w11', 'tp2_w01', 'tp2_w10', 'lin_hidden_w0', 'lin_hidden_w1', 'lin_scalar_w']
        weights = (lin_src_w0, lin_src_w1, lin_dst_w0, lin_dst_w1, tp1_w00, tp1_w11, tp1_w01, tp1_w10, tp2_w00, tp2_w11, tp2_w01, tp2_w10, lin_hidden_w0, lin_hidden_w1, lin_scalar_w)
        return _forward(atom_feature, edge_vector, weights, edge_index)

    def _L0_mix_ref(x, kln_weight, kln_bias, vln_weight, vln_bias):
        import jax, jax.numpy as jnp
        import numpy as np
        EPS = 1e-05

        def _layernorm(x, weight, bias):
            mean = jnp.mean(x, axis=-1, keepdims=True)
            std = jnp.std(x, axis=-1, keepdims=True, ddof=1)
            out = (x - mean) / (std + EPS)
            return weight * out + bias
        B, N, C = x.shape
        H = kln_weight.shape[0]
        hc = C // H
        qkv = x.reshape(B, N, H, hc).transpose(0, 2, 1, 3)
        q = qkv
        k = _layernorm(qkv, kln_weight, kln_bias)
        v = _layernorm(qkv, vln_weight, vln_bias)
        kv = jnp.einsum('bhnd,bhne->bhde', k, v) / N
        out = jnp.einsum('bhnd,bhde->bhne', q, kv)
        out = out.transpose(0, 2, 1, 3).reshape(B, N, C)
        return out + x

    def _L0_ffn_ref(x, Wg, bg, W1, b1, W2, b2):
        import jax, jax.numpy as jnp
        import numpy as np
        TOP_K = 2
        B, L, D = x.shape
        E = W1.shape[0]
        xf = x.reshape(-1, D)
        gate_logits = xf @ Wg + bg
        top_w, top_i = jax.lax.top_k(gate_logits, TOP_K)
        top_w = jax.nn.softmax(top_w, axis=-1)
        w_dense = jnp.sum(jax.nn.one_hot(top_i, E, dtype=xf.dtype) * top_w[..., None], axis=1)
        out = jnp.zeros_like(xf)
        for e in range(E):
            h = jax.nn.gelu(xf @ W1[e] + b1[e], approximate=False)
            out = out + w_dense[:, e:e + 1] * (h @ W2[e] + b2[e])
        return out.reshape(B, L, D)
    edge_index = jnp.stack([src, dst])
    xn = _layernorm(x, axis=-1)
    x = x + _L0_gnn_ref(xn, edge_attr_3, L0_gnn_lin_src_w0, L0_gnn_lin_src_w1, L0_gnn_lin_dst_w0, L0_gnn_lin_dst_w1, L0_gnn_tp1_w00, L0_gnn_tp1_w11, L0_gnn_tp1_w01, L0_gnn_tp1_w10, L0_gnn_tp2_w00, L0_gnn_tp2_w11, L0_gnn_tp2_w01, L0_gnn_tp2_w10, L0_gnn_lin_hidden_w0, L0_gnn_lin_hidden_w1, L0_gnn_lin_scalar_w, edge_index) + _L0_mix_ref(xn[None], L0_mix_kln_weight, L0_mix_kln_bias, L0_mix_vln_weight, L0_mix_vln_bias)[0]
    x = x + _L0_ffn_ref(_layernorm(x, axis=-1)[None], L0_ffn_Wg, L0_ffn_bg, L0_ffn_W1, L0_ffn_b1, L0_ffn_W2, L0_ffn_b2)[0]
    return x

_drawn_inputs = setup_inputs


def setup_inputs(seed=0):
    import zlib

    import numpy as np

    out = dict(_drawn_inputs(seed))
    spreads = {'L0_mix_kln_weight': (1.0, 0.6),
     'L0_mix_kln_bias': (0.0, 2.0),
     'L0_mix_vln_weight': (1.0, 0.6),
     'L0_mix_vln_bias': (0.0, 2.0),
     'L0_ffn_bg': (0.0, 2.0),
     'L0_ffn_b1': (0.0, 2.0),
     'L0_ffn_b2': (0.0, 2.0)}
    factors = {'edge_attr_3': 8.0,
     'L0_gnn_lin_src_w0': 8.0,
     'L0_gnn_lin_src_w1': 8.0,
     'L0_gnn_tp1_w00': 8.0,
     'L0_gnn_tp1_w11': 8.0,
     'L0_gnn_tp1_w01': 8.0,
     'L0_gnn_tp1_w10': 8.0,
     'L0_gnn_tp2_w00': 8.0,
     'L0_gnn_tp2_w11': 8.0,
     'L0_gnn_tp2_w01': 8.0,
     'L0_gnn_tp2_w10': 8.0,
     'L0_gnn_lin_hidden_w0': 8.0,
     'L0_gnn_lin_hidden_w1': 8.0,
     'L0_gnn_lin_scalar_w': 8.0,
     'L0_ffn_W1': 23.352,
     'L0_ffn_W2': 21.76,
     'L0_ffn_Wg': 8.0}
    for name, (base, spread) in spreads.items():
        noise = np.random.default_rng([zlib.crc32(name.encode()), seed]).standard_normal(out[name].shape)
        drawn = base * np.exp(spread * noise) if base else spread * noise
        out[name] = jnp.asarray(drawn.astype(out[name].dtype))
    for name, factor in factors.items():
        out[name] = (out[name] * factor).astype(out[name].dtype)
    return out
```

```python
from contextlib import ExitStack

import concourse.bass as bass
from concourse import mybir

ALU = mybir.AluOpType
ACT = mybir.ActivationFunctionType
AX = mybir.AxisListType
F32 = mybir.dt.float32
I32 = mybir.dt.int32
U32 = mybir.dt.uint32

SQ3 = 3.0 ** 0.5
EPS = 1e-5


class Chain:

    def __init__(self, eng, sem):
        self.eng, self.sem, self.base, self.n = eng, sem, 0, 0

    def __call__(self, ins):
        self.n += 1
        ins.then_inc(self.sem, 1)
        self.eng.wait_ge(self.sem, self.base + self.n)

    def open(self, per):
        self.first, self.per = self.base + self.n, per

    def enter(self, i):
        self.base, self.n = self.first + i * self.per, 0

    def leave(self, turns):
        assert self.n == self.per, (self.n, self.per)
        self.base, self.n = self.first + turns * self.per, 0


def gps_layer_kernel(nc, t, out, dbg=None):
    x, src, dst, attr = t["x"], t["src"], t["dst"], t["edge_attr_3"]
    N, D = x.shape
    E = src.shape[0]
    M = t["L0_gnn_lin_src_w0"].shape[0]
    V = D - M
    H, _, HC = t["L0_mix_kln_weight"].shape
    NE, _, HID = t["L0_ffn_W1"].shape
    assert D == 256 and M == 64 and NE == 8 and HID == 1024

    P, J, JB = 125, N // 125, 5
    NB = J // JB
    assert P * J == N and NB * JB == J
    TG, WIN = 3, 32
    GE = TG * 128
    G = -(-E // GE)
    PAIRS = -(-G // 2)
    LAST = E - (PAIRS - 1) * 2 * GE
    NC6 = 2 * TG
    NT = PAIRS * NC6
    NW = N + WIN + 3
    NWIN = -(-N // WIN)
    FAR = 4000.0
    assert FAR > N + WIN and 64 < PAIRS <= 128
    RING = 6
    FIRST = 2
    TURNS = (G - 1 - FIRST - 2) // RING
    K2 = 2
    TILES = K2 * N // 128 + NE
    SLOTS = TILES * 128
    FC = HID // 128

    xn_dram = nc.dram_tensor("xn_rows", (N, D), F32, kind="Internal").ap()
    xs_dram = nc.dram_tensor("expert_in_rows", (SLOTS, D), F32, kind="Internal").ap()
    ys_dram = nc.dram_tensor("expert_out_rows", (SLOTS, D), F32, kind="Internal").ap()

    c_tp = (2.0 * M) ** -0.5
    c_lin = float(M) ** -0.5

    names = ["lin_src_w0", "lin_src_w1", "tp1_w00", "tp1_w11", "tp1_w01", "tp1_w10", "tp2_w00", "tp2_w11",
             "tp2_w01", "tp2_w10", "lin_hidden_w0", "lin_hidden_w1", "lin_scalar_w"]

    with ExitStack() as ctx:
        def sb(scope, name, shape, dt=F32):
            return scope.enter_context(nc.sbuf_tensor(name, shape, dt))

        def sem(name):
            return ctx.enter_context(nc.semaphore(name))

        ps1 = ctx.enter_context(nc.psum_tensor("ps1", [128, 2, 512], F32))
        ps2 = ctx.enter_context(nc.psum_tensor("ps2", [128, 2, 1024], F32))
        ps3 = ctx.enter_context(nc.psum_tensor("ps3", [128, 2, 512], F32))

        x_sb = sb(ctx, "x_sb", [P, J, D])
        ident = sb(ctx, "ident", [128, 128])
        ones = sb(ctx, "ones", [128, 128])
        below = sb(ctx, "below", [P, P])
        iota_e = sb(ctx, "iota_e", [P, NE])
        iota_tile = sb(ctx, "iota_tile", [1, TILES])
        wg_sb = sb(ctx, "wg_sb", [128, 2, NE])
        bg_bc = sb(ctx, "bg_bc", [P, NE])
        spread_i = sb(ctx, "spread_i", [1, 1], I32)
        mean2 = sb(ctx, "mean2", [P, J])
        rstd2 = sb(ctx, "rstd2", [P, J])
        top_w = sb(ctx, "top_w", [P, J, K2])
        top_i = sb(ctx, "top_i", [P, J, K2])
        ln_stats = sb(ctx, "ln_stats", [P, JB, 6])
        ln_mv = sb(ctx, "ln_mv", [P, JB, 2])
        ln_var = sb(ctx, "ln_var", [P, JB])
        ln_std = sb(ctx, "ln_std", [P, JB])
        ln_rstd = sb(ctx, "ln_rstd", [P, JB])

        graph = ExitStack()
        xn_sb = sb(graph, "xn_sb", [P, J, D])
        agg = sb(graph, "agg", [128, 6, NW])
        edge_dst = sb(graph, "edge_dst", [128, NT])
        edge_loc = sb(graph, "edge_loc", [128, NT])
        edge_src = sb(graph, "edge_src", [128, NT], I32)
        edge_r = sb(graph, "edge_r", [128, NT, 3])
        edge_rr = sb(graph, "edge_rr", [128, NT])
        base_i = sb(graph, "base_i", [1, PAIRS, 2], I32)
        iota_w = sb(graph, "iota_w", [128, WIN])
        w_hid = sb(graph, "w_hid", [128, 128])
        w_z = sb(graph, "w_z", [128, 192])
        w_sc = sb(graph, "w_sc", [128, 96])
        place = sb(graph, "place", [128, 3, M, 3])
        place_o0 = sb(graph, "place_o0", [128, 128])
        w_vec = sb(graph, "w_vec", [128, 2, M, 3])
        kv = sb(graph, "kv", [128, 2, 128])

        pre = ExitStack()
        dst_raw = sb(pre, "dst_raw", [PAIRS, 2 * GE], I32)
        src_raw = sb(pre, "src_raw", [PAIRS, 2 * GE], I32)
        attr_raw = sb(pre, "attr_raw", [PAIRS, 2 * GE, 3])
        dst_f = sb(pre, "dst_f", [PAIRS, 2, GE])
        src_f = sb(pre, "src_f", [PAIRS, 2 * GE])
        loc_f = sb(pre, "loc_f", [PAIRS, 2, GE])
        edge_tmp = sb(pre, "edge_tmp", [128, NT, 3])
        edge_len = sb(pre, "edge_len", [128, 2, NT])
        dlow = sb(pre, "dlow", [PAIRS, 2])
        dhigh = sb(pre, "dhigh", [PAIRS, 2])
        dspread = sb(pre, "dspread", [PAIRS, 2])
        spread_row = sb(pre, "spread_row", [1, 1])
        wsm = sb(pre, "wsm", [M, len(names), M])
        lin_t = sb(pre, "lin_t", [M, 128])
        tp_t = sb(pre, "tp_t", [M, 2, 128])
        ba_t = sb(pre, "ba_t", [M, 128])
        d_t = sb(pre, "d_t", [M, 128])
        c_t = sb(pre, "c_t", [M, 128])
        w_v = sb(pre, "w_v", [M, M])
        rep = sb(pre, "rep", [M, 2, 128])
        pick = sb(pre, "pick", [128, 2, M, 3])
        pick_m = sb(pre, "pick_m", [128, 2, 3])
        kw_col = sb(pre, "kw_col", [128, 2])
        kb_col = sb(pre, "kb_col", [128, 2])
        vw_bc = sb(pre, "vw_bc", [128, D])
        vb_bc = sb(pre, "vb_bc", [128, D])
        kv_tmp = sb(pre, "kv_tmp", [128, 3, 128])
        kv_col = sb(pre, "kv_col", [128, 2])
        head_block = sb(pre, "head_block", [128, 128])
        hx = sb(pre, "hx", [P, JB * H, HC])
        hsq = sb(pre, "hsq", [P, JB * H, HC])
        hstat = sb(pre, "hstat", [P, 3, JB * H])
        pre.close()

        loop = ExitStack()
        xg = sb(loop, "xg", [128, RING, TG, M + D])
        idx_st = sb(loop, "idx_st", [128, RING, TG], I32)
        prod = sb(loop, "prod", [128, TG, M, 3])
        zt = sb(loop, "zt", [128, 2, GE])
        hid_sb = sb(loop, "hid_sb", [128, 2, GE])
        qeo = sb(loop, "qeo", [128, 2, TG, 2, M])
        e0 = sb(loop, "e0", [128, 2, TG, M])
        o0 = sb(loop, "o0", [128, TG, M])
        top = sb(loop, "top", [128, TG])
        neg_top = sb(loop, "neg_top", [128, 2, TG])
        exp_sum = sb(loop, "exp_sum", [128, 2, TG])
        exp_neg = sb(loop, "exp_neg", [128, 2, TG])
        norm = sb(loop, "norm", [128, TG])
        coef = sb(loop, "coef", [128, TG, 5])
        hot = sb(loop, "hot", [128, TG, WIN])
        sel = sb(loop, "sel", [128, 2, (TG * 5 + 2) * WIN])
        loc_w = sb(loop, "loc_w", [128, TG])
        loop.close()

        epi = ExitStack()
        agg_st = sb(epi, "agg_st", [128, 6, JB, P])
        xn_st = sb(epi, "xn_st", [P, JB, D])
        xt_sb = sb(epi, "xt_sb", [128, JB, 2, P])
        xf_sb = sb(epi, "xf_sb", [P, JB, D])
        res = sb(epi, "res", [P, JB, D])
        logit = sb(epi, "logit", [P, JB, NE])
        top8 = sb(epi, "top8", [P, JB, 8])
        top8_i = sb(epi, "top8_i", [P, JB, 8], U32)
        epi.close()
        graph.close()

        w1_sb = sb(ctx, "w1_sb", [128, NE, 2, HID])
        w2_sb = sb(ctx, "w2_sb", [128, NE, FC, D])
        b1_sb = sb(ctx, "b1_sb", [128, NE, FC])
        b2_bc = sb(ctx, "b2_bc", [128, NE, D])
        picked = sb(ctx, "picked", [P, 2, J, NE])
        ranks = sb(ctx, "ranks", [P, J, NE])
        both = sb(ctx, "both", [P, J, NE])
        tot = sb(ctx, "tot", [P, NE])
        n_tiles = sb(ctx, "n_tiles", [128, 4, NE])
        n_tiles_i = sb(ctx, "n_tiles_i", [128, 2, NE], I32)
        row0 = sb(ctx, "row0", [P, NE])
        slot_f = sb(ctx, "slot_f", [P, 2, J])
        slot_i = sb(ctx, "slot_i", [P, J, 2], I32)
        gap = sb(ctx, "gap", [P, 2, J])
        ended = sb(ctx, "ended", [1, TILES, NE])
        etile_f = sb(ctx, "etile_f", [1, TILES])
        etile = sb(ctx, "etile", [1, TILES], I32)
        ffn = ExitStack()
        xs_sb = sb(ffn, "xs_sb", [128, 2, D])
        xst = sb(ffn, "xst", [128, 2, 2, 128])
        h_sb = sb(ffn, "h_sb", [128, HID])
        ht_sb = sb(ffn, "ht_sb", [128, FC, 128])
        b1_cur = sb(ffn, "b1_cur", [128, 2, FC])
        y_sb = sb(ffn, "y_sb", [128, 2, D])
        ffn.close()
        send = ExitStack()
        slot_st = sb(send, "slot_st", [P, JB, 2], I32)
        row_st = sb(send, "row_st", [P, JB, D])
        send.close()
        take = ExitStack()
        slot_st2 = sb(take, "slot_st2", [P, JB, 2], I32)
        y_st = sb(take, "y_st", [P, JB, 2, D])
        take.close()

        x_loaded, raw_padded, raw_loaded, w_loaded = map(sem, ("x_loaded", "raw_padded", "raw_loaded", "w_loaded"))
        mixw_loaded, gate_loaded = sem("mixw_loaded"), sem("gate_loaded")
        consts_ready, pool_own = sem("consts_ready"), sem("pool_own")
        agg_zeroed, zeros_written = sem("agg_zeroed"), sem("zeros_written")
        dve_own, act_own = sem("dve_own"), sem("act_own")
        ln_var_ready, ln_std_ready = sem("ln_var_ready"), sem("ln_std_ready")
        xn_ready, xn_written = sem("xn_ready"), sem("xn_written")
        edge_rows_ready, edge_cols_ready, edge_cols_taken = map(sem, ("edge_rows_ready", "edge_cols_ready", "edge_cols_taken"))
        spread_col = sem("spread_col")
        edge_sq_ready, edge_len_ready = sem("edge_sq_ready"), sem("edge_len_ready")
        base_ready, flag_ready = sem("base_ready"), sem("flag_ready")
        w_mm, w_copied = sem("w_mm"), sem("w_copied")
        banks_cleared = sem("banks_cleared")
        head_dev, head_sq, head_var, head_std, head_ready, head_used = map(
            sem, ("head_dev", "head_sq", "head_var", "head_std", "head_ready", "head_used"))
        kv_ready, sel_padded = sem("kv_ready"), sem("sel_padded")

        class GroupSems:

            def __init__(s, tag, ring):
                s.ring = ring
                s.gathered = [sem(f"{tag}gathered{i}") for i in range(ring)]
                (s.idx, s.prod, s.dot, s.zt_ps, s.zt_sb, s.hid_ps, s.hid_sb, s.pq, s.scores, s.top, s.neg_top, s.exp,
                 s.q_sb, s.o0, s.hot, s.norm, s.coef, s.eo, s.sel, s.scattered, s.added) = (
                    sem(tag + n) for n in ("idx", "prod", "dot", "zt_ps", "zt_sb", "hid_ps", "hid_sb", "pq", "scores",
                                           "top", "neg_top", "exp", "q_sb", "o0", "hot", "norm", "coef", "eo", "sel",
                                           "scattered", "added"))

        main, wide = GroupSems("", RING), GroupSems("wide_", 1)
        loc_ready, agg_final = sem("loc_ready"), sem("agg_final")

        epi_staged, epi_staged_x, epi_xt_ps, epi_xt_sb, epi_out, epi_res, epi_xf, epi_var, epi_std = map(
            sem, ("epi_staged", "epi_staged_x", "epi_xt_ps", "epi_xt_sb", "epi_out", "epi_res", "epi_xf", "epi_var",
                  "epi_std"))
        epi_ft_ps, epi_ft_sb, epi_logit, epi_done = map(sem, ("epi_ft_ps", "epi_ft_sb", "epi_logit", "epi_done"))
        gap_ready, gap_exp = sem("gap_ready"), sem("gap_exp")
        tot_ready, rank0_ps = sem("tot_ready"), sem("rank0_ps")
        slots_ready, etile_ready = sem("slots_ready"), sem("etile_ready")
        row_staged, slot_staged, rows_sent = sem("row_staged"), sem("slot_staged"), sem("rows_sent")
        ew_loaded, b_loaded = sem("ew_loaded"), sem("b_loaded")
        xs_loaded = [sem("xs_loaded0"), sem("xs_loaded1")]
        xst_ps, xst_sb, h_ps, h_half0, h_half1, ht_ps, ht_ready, y_ps, y_ready, b1_ready = map(
            sem, ("xst_ps", "xst_sb", "h_ps", "h_half0", "h_half1", "ht_ps", "ht_ready", "y_ps", "y_ready", "b1_ready"))
        ys_written = [sem("ys_written0"), sem("ys_written1")]
        slot_staged2, y_taken, y_first, summed, out_written = map(
            sem, ("slot_staged2", "y_taken", "y_first", "summed", "out_written"))

        block = ctx.enter_context(nc.Block())

        def count(eng, value):
            return value if isinstance(value, int) else eng.to_reg(value)

        def past(i):
            return not isinstance(i, int) or i > 0

        def batches(eng, turn):
            turn(0)
            with eng.Fori(1, NB) as b:
                turn(b)

        def group(i, o):
            return not isinstance(i, int) or 0 <= RING * i + o < G

        def steps(eng, step, first, start, turns, last):
            for k in range(first, start):
                step(0, k)
            with eng.Fori(0, turns) as i:
                for r in range(RING):
                    step(i, start + r)
            for k in range(start + RING * turns, last):
                step(0, k)

        @block.sync
        def _(sp):
            x_rows = x.rearrange("(p j) d -> p j d", j=J)
            for a, b in ((0, 112), (112, P)):
                sp.dma_start(x_sb[a:b, :, :], x_rows[a:b]).then_inc(x_loaded, 16)
            for k, w in enumerate(names):
                sp.dma_start(wsm[:, k, :], t["L0_gnn_" + w]).then_inc(w_loaded, 16)
            sp.wait_ge(raw_padded, 3)
            full = PAIRS - 1
            for raw, dram, c in ((dst_raw[:, :], dst, 1), (src_raw[:, :], src, 1),
                                 (attr_raw[:, :, :].rearrange("p e m -> p (e m)"), attr.rearrange("e m -> (e m)"), 3)):
                w = 2 * GE * c
                rows = dram[0:full * w].rearrange("(p e) -> p e", e=w)
                sp.dma_start(raw[0:64, :], rows[0:64]).then_inc(raw_loaded, 16)
                sp.dma_start(raw[64:full, :], rows[64:full]).then_inc(raw_loaded, 16)
                sp.dma_start(raw[full:PAIRS, 0:LAST * c], dram[full * w:full * w + LAST * c].rearrange("(p e) -> p e", p=1)) \
                    .then_inc(raw_loaded, 16)
            xn_rows = xn_dram.rearrange("(p j) d -> p j d", j=J)
            for b in range(NB):
                sp.wait_ge(xn_ready, b + 1)
                for p0, p1 in ((0, 112), (112, P)):
                    sp.dma_start(xn_rows[p0:p1, b * JB:(b + 1) * JB, :], xn_sb[p0:p1, b * JB:(b + 1) * JB, :]) \
                        .then_inc(xn_written, 16)
            with nc.allow_non_contiguous_dma(reason="256 elements"):
                for col, w in ((kw_col, "kln_weight"), (kb_col, "kln_bias")):
                    sp.dma_start(col[:, :], t["L0_mix_" + w].rearrange("h a c -> (h a c)").rearrange("(c p) -> p c", p=128)) \
                        .then_inc(mixw_loaded, 16)
            for bc, w in ((vw_bc, "vln_weight"), (vb_bc, "vln_bias")):
                sp.dma_start(bc[:, :], t["L0_mix_" + w].rearrange("h a c -> (a h c)").partition_broadcast(128)) \
                    .then_inc(mixw_loaded, 16)
            sp.dma_start(wg_sb[:, :, :], t["L0_ffn_Wg"].rearrange("(c p) e -> p c e", p=128)).then_inc(gate_loaded, 16)
            sp.dma_start(bg_bc[:, :], t["L0_ffn_bg"].partition_broadcast(P)).then_inc(gate_loaded, 16)
            sp.wait_ge(agg_zeroed, 1)
            zcols = SLOTS * D // 128
            sp.dma_start(xs_dram.rearrange("(p s) d -> p (s d)", p=128),
                         agg[:, :, :].rearrange("p s n -> p (s n)")[:, 0:zcols]).then_inc(zeros_written, 16)
            sp.wait_ge(epi_done, NB)
            sp.dma_start(b1_sb[:, :, :], t["L0_ffn_b1"].rearrange("e (p c) -> p e c", p=128)).then_inc(b_loaded, 16)
            sp.dma_start(b2_bc[:, :, :], t["L0_ffn_b2"].partition_broadcast(128)).then_inc(b_loaded, 16)
            for e in range(NE):
                if e:
                    sp.wait_ge(ew_loaded, 32 * e)
                sp.dma_start(w1_sb[:, e, :, :], t["L0_ffn_W1"][e].rearrange("(p c) h -> p c h", p=128)).then_inc(ew_loaded, 16)
                sp.dma_start(w2_sb[:, e, :, :], t["L0_ffn_W2"][e].rearrange("(p c) d -> p c d", p=128)).then_inc(ew_loaded, 16)
            sp.wait_ge(rows_sent, 16 * 2 * J)
            xs_t = xs_dram.rearrange("(k p) d -> p k d", p=128)
            ys_t = ys_dram.rearrange("(k p) d -> p k d", p=128)

            def load(i, o):
                s = o % 2
                if not isinstance(i, int) or o >= 2:
                    sp.wait_ge(xst_ps, 2 * i + o - 1)
                sp.dma_start(xs_sb[:, s, :], xs_t[:, bass.ds(2 * i + o, 1), :].rearrange("p k d -> p (k d)")) \
                    .then_inc(xs_loaded[s], 16)

            def store(i, o):
                s = o % 2
                sp.wait_ge(y_ready, 2 * i + o + 1)
                sp.dma_start(ys_t[:, bass.ds(2 * i + o, 1), :].rearrange("p k d -> p (k d)"), y_sb[:, s, :]) \
                    .then_inc(ys_written[s], 16)

            load(0, 0)
            load(0, 1)
            with sp.Fori(0, TILES // 2 - 1) as i:
                for o in (0, 1):
                    load(i, o + 2)
                    store(i, o)
            for o in (0, 1):
                store(TILES // 2 - 1, o)
            out_rows = out.rearrange("(p j) d -> p j d", j=J)
            for b in range(NB):
                sp.wait_ge(summed, JB * (b + 1))
                for p0, p1 in ((0, 112), (112, P)):
                    sp.dma_start(out_rows[p0:p1, b * JB:(b + 1) * JB, :], x_sb[p0:p1, b * JB:(b + 1) * JB, :]) \
                        .then_inc(out_written, 16)
            sp.wait_ge(out_written, 16 * 2 * NB)

        @block.gpsimd
        def _(pool):
            own = Chain(pool, pool_own)
            for buf, value in ((ident[:, :], 0.0), (ones[:, :], 1.0), (below[:, :], 1.0), (head_block[:, :], 1.0 / N),
                               (pick[:, :, :, :], 0.0), (place[:, :, :, :], 0.0), (place_o0[:, :], 0.0),
                               (d_t[:, M:128], 0.0), (c_t[:, 0:M], 0.0), (w_sc[:, M:96], 0.0)):
                pool.memset(buf, value)
            own(pool.memset(rep[:, :, :], 1.0))

            def pick_where(view, pattern, base, mult, op=ALU.not_equal, fill=1.0):
                return pool.affine_select(out=view, in_=view, compare_op=op, fill=fill, base=base, pattern=pattern,
                                          channel_multiplier=mult)

            pick_where(ident[:, :], [[-1, 128]], 0, 1).then_inc(consts_ready, 1)
            pick_where(below[:, :], [[1, P]], 0, -1, ALU.is_gt, 0.0).then_inc(consts_ready, 1)
            pick_where(place_o0[0:M, :], [[-1, 128]], 0, 1).then_inc(consts_ready, 1)
            for m in range(3):
                pick_where(place[:, m, :, m], [[-1, M]], -M, 1).then_inc(consts_ready, 1)
            for c, shift in ((0, -M), (1, 128 - M)):
                pick_where(pick[:, c, :, :], [[-3, M], [-1, 3]], shift, 1).then_inc(consts_ready, 1)
            hb = head_block[:, :].rearrange("p (h c) -> p h c", c=HC)
            own(pick_where(hb, [[-HC, 128 // HC], [0, HC]], 0, 1, ALU.is_ge, 0.0))
            pick_where(hb, [[HC, 128 // HC], [0, HC]], HC - 1, -1, ALU.is_ge, 0.0).then_inc(consts_ready, 1)
            for c, shift in ((0, -M), (1, 128 - M)):
                own(pick_where(rep[:, c, :], [[1, 128]], shift, -3, ALU.is_ge, 0.0))
                pick_where(rep[:, c, :], [[-1, 128]], 2 - shift, 3, ALU.is_ge, 0.0).then_inc(consts_ready, 1)
            for buf, n in ((iota_w, WIN), (iota_e, NE), (iota_tile, TILES)):
                pool.iota(buf[:, :], [[1, n]], base=0, channel_multiplier=0,
                          allow_small_or_imprecise_dtypes=True).then_inc(consts_ready, 1)
            pool.memset(agg[:, :, :], 0.0).then_inc(agg_zeroed, 1)

            pool.wait_ge(kv_ready, 2)
            pool.memset(sel[:, :, TG * 5 * WIN:], 0.0).then_inc(sel_padded, 1)

            def gather(i, o):
                if not group(i, o):
                    return
                s = o % RING
                staged, free = count(pool, RING * i + o + 1), count(pool, RING * i + o - RING + 1)
                pool.wait_ge(xn_written, 16 * 2 * NB)
                pool.wait_ge(main.idx, staged)
                if not isinstance(i, int) or o >= RING:
                    pool.wait_ge(main.scattered, free)
                for tt in range(TG):
                    pool.indirect_dma_start(xg[:, s, tt, M:], None, xn_dram,
                                            bass.IndirectOffsetOnAxis(ap=idx_st[:, s, tt:tt + 1], axis=0),
                                            bounds_check=N - 1, oob_is_err=False).then_inc(main.gathered[s], 16)

            steps(pool, gather, 0, RING, (G - RING) // RING, G)

            pool.wait_ge(flag_ready, 1)
            far = pool.value_load(spread_i[0:1, 0:1], min_val=0, max_val=1)
            with pool.If(far > 0):
                with pool.Fori(0, G) as g:
                    staged = count(pool, g + 1)
                    pool.wait_ge(xn_written, 16 * 2 * NB)
                    pool.wait_ge(wide.idx, staged)
                    for tt in range(TG):
                        pool.indirect_dma_start(xg[:, 0, tt, M:], None, xn_dram,
                                                bass.IndirectOffsetOnAxis(ap=idx_st[:, 0, tt:tt + 1], axis=0),
                                                bounds_check=N - 1, oob_is_err=False).then_inc(wide.gathered[0], 16)

            pool.wait_ge(slots_ready, 1)
            pool.wait_ge(zeros_written, 16)

            def send_rows(b):
                rows, staged = count(pool, (b + 1) * JB), count(pool, b + 1)
                pool.wait_ge(zeros_written, 16)
                pool.wait_ge(row_staged, rows)
                pool.wait_ge(slot_staged, staged)
                for jj in range(JB):
                    for k in range(K2):
                        pool.indirect_dma_start(xs_dram, bass.IndirectOffsetOnAxis(ap=slot_st[:, jj, k:k + 1], axis=0),
                                                row_st[:, jj, :], None, bounds_check=SLOTS - 1,
                                                oob_is_err=False).then_inc(rows_sent, 16)

            batches(pool, send_rows)

            for s in (0, 1):
                pool.wait_ge(ys_written[s], 16 * (TILES // 2))

            def take_rows(b):
                taken, staged = count(pool, b * JB), count(pool, b + 1)
                pool.wait_ge(ys_written[0], 16 * (TILES // 2))
                if past(b):
                    pool.wait_ge(summed, taken)
                pool.wait_ge(slot_staged2, staged)
                for jj in range(JB):
                    for k in range(K2):
                        pool.indirect_dma_start(y_st[:, jj, k, :], None, ys_dram,
                                                bass.IndirectOffsetOnAxis(ap=slot_st2[:, jj, k:k + 1], axis=0),
                                                bounds_check=SLOTS - 1, oob_is_err=False).then_inc(y_taken, 16)

            batches(pool, take_rows)

        @block.tensor
        def _(pe):
            W = {n: wsm[:, k, :] for k, n in enumerate(names)}

            pe.wait_ge(w_loaded, 16 * len(names))
            pe.wait_ge(consts_ready, 14)
            pw = ps1[:, 0, :]
            pe.transpose(pw[0:M, 0:M], W["lin_src_w1"], ident[0:M, 0:M])
            pe.transpose(pw[0:M, M:128], W["lin_src_w0"], ident[0:M, 0:M]).then_inc(w_mm, 1)
            pe.wait_ge(w_copied, 1)
            for k, (a, b) in enumerate((("tp1_w11", "tp1_w00"), ("tp1_w10", "tp1_w01"))):
                o = 128 + 128 * k
                pe.matmul(pw[0:M, o:o + M], W[a], lin_t[:, 0:M], start=True, stop=True)
                mm = pe.matmul(pw[0:M, o + M:o + 128], W[b], lin_t[:, M:128], start=True, stop=True)
            mm.then_inc(w_mm, 1)
            pe.wait_ge(w_copied, 2)
            pe.matmul(pw[:, 0:M], tp_t[:, 0, :], W["lin_hidden_w0"], start=True, stop=True)
            pe.matmul(pw[0:M, 128:256], W["lin_hidden_w0"], tp_t[:, 0, :], start=True, stop=True)
            pe.matmul(pw[0:M, 256:384], W["lin_hidden_w1"], tp_t[:, 1, :], start=True, stop=True).then_inc(w_mm, 1)
            pe.wait_ge(w_copied, 3)
            pe.matmul(pw[:, 0:M], ba_t[:, :], W["tp2_w00"], start=True, stop=False)
            pe.matmul(pw[:, 0:M], d_t[:, :], W["tp2_w11"], start=False, stop=True)
            pe.matmul(pw[:, M:128], c_t[:, :], W["tp2_w11"], start=True, stop=True)
            pe.matmul(pw[:, 128:192], ba_t[:, :], W["tp2_w01"], start=True, stop=False)
            pe.matmul(pw[:, 128:192], c_t[:, :], W["tp2_w10"], start=False, stop=True)
            pe.matmul(pw[0:M, 192:256], d_t[:, 0:M], W["tp2_w10"], start=True, stop=True).then_inc(w_mm, 1)
            pe.wait_ge(w_copied, 4)
            pe.matmul(pw[:, 256:320], rep[:, 0, :], w_v[:, :], start=True, stop=True)
            pe.matmul(pw[:, 320:384], rep[:, 1, :], w_v[:, :], start=True, stop=True).then_inc(w_mm, 1)

            pe.wait_ge(edge_rows_ready, 1)
            tables = [(dst_f[:, :, :].rearrange("p h e -> p (h e)"), 1, 0), (loc_f[:, :, :].rearrange("p h e -> p (h e)"), 1, 0),
                      (src_f[:, :], 1, 0)] + [(attr_raw[:, :, :].rearrange("p e m -> p (e m)"), 3, m) for m in range(3)]
            banks = [ps2[:, 0, 0:512], ps2[:, 0, 512:1024], ps2[:, 1, 0:512], ps2[:, 1, 512:1024], ps3[:, 0, :], ps3[:, 1, :]]
            for (tab, stride, m), bank in zip(tables, banks):
                for c in range(NC6):
                    lo = c * 128 * stride + m
                    mm = pe.transpose(bank[:, c * PAIRS:(c + 1) * PAIRS], tab[:, lo:lo + 127 * stride + 1:stride],
                                      ident[0:PAIRS, 0:PAIRS])
                mm.then_inc(edge_cols_ready, 1)
            for h in range(2):
                pe.transpose(ps1[0:1, 1, h * PAIRS:(h + 1) * PAIRS], dlow[:, h:h + 1], ident[0:PAIRS, 0:PAIRS])
            pe.transpose(ps1[0:1, 1, 2 * PAIRS:3 * PAIRS], dspread[:, 0:1], ident[0:PAIRS, 0:PAIRS]).then_inc(spread_col, 1)

            pe.wait_ge(edge_cols_taken, len(tables))
            pe.wait_ge(banks_cleared, 1)
            pe.wait_ge(flag_ready, 1)
            with pe.Fori(0, NB) as b:
                pe.wait_ge(head_ready, b + 1)
                u = hx[:, :, :].rearrange("p h c -> p (h c)").rearrange("p (j d) -> p j d", d=D)
                for jj in range(JB):
                    for c in range(2):
                        uc = u[:, jj, c * 128:(c + 1) * 128]
                        pe.matmul(ps2[:, c, 0:128], uc, uc, start=False, stop=False, skip_group_check=True)
                        pe.matmul(ps2[:, c, 512:513], uc, ones[0:P, 0:1], start=False, stop=False, skip_group_check=True)
                    mm = pe.matmul(ps3[:, 0, 0:D], ones[0:P, :], u[:, jj, :], start=False, stop=False, skip_group_check=True)
                mm.then_inc(head_used, 1)

            def turn_z(i, o):
                if not group(i, o):
                    return
                s = o % RING
                pe.wait_ge(main.dot, RING * i + o + 1)
                if not isinstance(i, int) or o >= 1:
                    pe.wait_ge(main.zt_sb, RING * i + o)
                for tt in range(TG):
                    mm = pe.transpose(ps1[:, 0, tt * 128:(tt + 1) * 128], xg[:, s, tt, 0:128], ident[:, :])
                mm.then_inc(main.zt_ps, 1)

            def hidden(i, o):
                if not group(i, o):
                    return
                s = o % 2
                pe.wait_ge(main.zt_sb, RING * i + o + 1)
                if not isinstance(i, int) or o >= 1:
                    pe.wait_ge(main.hid_sb, RING * i + o)
                pe.matmul(ps1[:, 1, 0:GE], w_hid[:, :], zt[:, s, :], start=True, stop=True).then_inc(main.hid_ps, 1)
                if not isinstance(i, int) or o >= 2:
                    pe.wait_ge(main.o0, RING * i + o - 1)
                    pe.wait_ge(main.q_sb, RING * i + o - 1)
                for tt in range(TG):
                    mm = pe.matmul(ps2[:, s, tt * 256:tt * 256 + 192], zt[:, s, tt * 128:(tt + 1) * 128], w_z[:, :],
                                   start=True, stop=True)
                mm.then_inc(main.pq, 1)

            def scores(i, o):
                if not group(i, o):
                    return
                s = o % 2
                pe.wait_ge(main.hid_sb, RING * i + o + 1)
                if not isinstance(i, int) or o >= 1:
                    pe.wait_ge(main.exp, RING * i + o)
                for tt in range(TG):
                    mm = pe.matmul(ps3[:, 1, tt * 96:(tt + 1) * 96], hid_sb[:, s, tt * 128:(tt + 1) * 128],
                                   w_sc[:, :], start=True, stop=True)
                mm.then_inc(main.scores, 1)

            def scatter(i, o):
                if not group(i, o):
                    return
                s, r = o % 2, o % RING
                pe.wait_ge(main.eo, RING * i + o + 1)
                pe.wait_ge(main.q_sb, RING * i + o + 1)
                pe.wait_ge(main.sel, RING * i + o + 1)
                if not isinstance(i, int) or o >= 1:
                    pe.wait_ge(main.added, RING * i + o)
                scatter_mm(s, r).then_inc(main.scattered, 1)

            def scatter_mm(s, r):
                for col, of, block0, n in ((0, "vec", 2, 3), (96, "qeo", 0, 4), (224, "x0", 4, 3)):
                    for tt in range(TG):
                        lhs = {"vec": xg[:, r, tt, 192:320], "x0": xg[:, r, tt, 64:192],
                               "qeo": qeo[:, s, tt, :, :].rearrange("p a f -> p (a f)")}[of]
                        lo = (tt * 5 + block0) * WIN
                        mm = pe.matmul(ps3[:, 0, col:col + n * WIN], lhs, sel[:, s, lo:lo + n * WIN],
                                       start=(tt == 0), stop=(tt == TG - 1))
                return mm

            pe.wait_ge(kv_ready, 2)
            pe.wait_ge(sel_padded, 1)

            def step(i, k):
                hidden(i, k)
                turn_z(i, k + 1)
                scores(i, k)
                scatter(i, k - 1)

            steps(pe, step, -1, FIRST, TURNS, G + 1)

            far = pe.value_load(spread_i[0:1, 0:1], min_val=0, max_val=1)
            with pe.If(far > 0):
                with pe.Fori(0, G) as g:
                    pe.wait_ge(wide.dot, g + 1)
                    for tt in range(TG):
                        mm = pe.transpose(ps1[:, 0, tt * 128:(tt + 1) * 128], xg[:, 0, tt, 0:128], ident[:, :])
                    mm.then_inc(wide.zt_ps, 1)
                    pe.wait_ge(wide.zt_sb, g + 1)
                    pe.matmul(ps1[:, 1, 0:GE], w_hid[:, :], zt[:, 0, :], start=True, stop=True).then_inc(wide.hid_ps, 1)
                    for tt in range(TG):
                        mm = pe.matmul(ps2[:, 0, tt * 256:tt * 256 + 192], zt[:, 0, tt * 128:(tt + 1) * 128], w_z[:, :],
                                       start=True, stop=True)
                    mm.then_inc(wide.pq, 1)
                    pe.wait_ge(wide.hid_sb, g + 1)
                    for tt in range(TG):
                        mm = pe.matmul(ps3[:, 1, tt * 96:(tt + 1) * 96], hid_sb[:, 0, tt * 128:(tt + 1) * 128],
                                       w_sc[:, :], start=True, stop=True)
                    mm.then_inc(wide.scores, 1)
                    with pe.Fori(0, NWIN) as w:
                        pe.wait_ge(wide.sel, g * NWIN + w + 1)
                        pe.wait_ge(wide.added, g * NWIN + w + 1)
                        scatter_mm(0, 0).then_inc(wide.scattered, 1)

            def mix_and_gate(b):
                pe.wait_ge(epi_staged_x, b + 1)
                for jj in range(JB):
                    if past(b) or jj:
                        pe.wait_ge(epi_xt_sb, b * JB + jj)
                    for c in range(2):
                        mm = pe.transpose(ps1[:, 0, c * 128:c * 128 + P], xn_st[:, jj, c * 128:(c + 1) * 128], ident[0:P, 0:P])
                    mm.then_inc(epi_xt_ps, 1)
                    if jj == 0:
                        pe.wait_ge(epi_staged, b + 1)
                    pe.wait_ge(epi_xt_sb, b * JB + jj + 1)
                    if past(b) or jj:
                        pe.wait_ge(epi_res, b * JB + jj)
                    o = ps1[0:P, 1, 0:D]
                    pe.matmul(o[:, 0:128], agg_st[:, 4, jj, :], place_o0[:, :], start=True, stop=False, skip_group_check=True)
                    pe.matmul(o[:, 128:256], xt_sb[:, jj, 1, :], kv[:, 1, :], start=False, stop=False, skip_group_check=True)
                    pe.matmul(o[:, 0:128], xt_sb[:, jj, 0, :], kv[:, 0, :], start=False, stop=False, skip_group_check=True)
                    for k, w in ((1, place[:, 0]), (2, place[:, 1]), (3, place[:, 2]), (5, w_vec[:, 0]), (0, w_vec[:, 1])):
                        mm = pe.matmul(o[:, M:D], agg_st[:, k, jj, :], w.rearrange("p v m -> p (v m)"),
                                       start=False, stop=(k == 0), skip_group_check=True)
                    mm.then_inc(epi_out, 1)
                pe.wait_ge(gate_loaded, 32)
                for jj in range(JB):
                    pe.wait_ge(epi_xf, b * JB + jj + 1)
                    if past(b) or jj:
                        pe.wait_ge(epi_ft_sb, b * JB + jj)
                    for c in range(2):
                        mm = pe.transpose(ps2[:, 0, c * 128:c * 128 + P], xf_sb[:, jj, c * 128:(c + 1) * 128], ident[0:P, 0:P])
                    mm.then_inc(epi_ft_ps, 1)
                    pe.wait_ge(epi_ft_sb, b * JB + jj + 1)
                    for c in range(2):
                        mm = pe.matmul(ps3[0:P, 0, jj * NE:(jj + 1) * NE], xt_sb[:, jj, c, :], wg_sb[:, c, :],
                                       start=(c == 0), stop=(c == 1))
                mm.then_inc(epi_logit, 1)

            batches(pe, mix_and_gate)

            pe.wait_ge(tot_ready, 1)
            pe.matmul(ps1[0:P, 0, 0:NE], below[:, :], tot[:, :], start=True, stop=True)
            pe.matmul(ps1[:, 0, 128:128 + NE], ones[0:P, :], tot[:, :], start=True, stop=True).then_inc(rank0_ps, 1)

            pe.wait_ge(etile_ready, 1)

            def tile(i, o):
                return not isinstance(i, int) or 0 <= 2 * i + o < TILES

            def turn_rows(i, o):
                if not tile(i, o):
                    return
                s = o % 2
                pe.wait_ge(xs_loaded[s], 16 * (i + o // 2 + 1))
                if not isinstance(i, int) or o >= 1:
                    pe.wait_ge(xst_sb, 2 * i + o)
                for c in range(2):
                    mm = pe.transpose(ps1[:, 0, c * 128:(c + 1) * 128], xs_sb[:, s, c::2], ident[:, :])
                mm.then_inc(xst_ps, 1)

            def up(i, o):
                if not tile(i, o):
                    return
                s = o % 2
                e = pe.value_load(etile[0:1, bass.ds(2 * i + o, 1)], min_val=0, max_val=NE - 1)
                pe.wait_ge(ew_loaded, 32 * e + 32)
                pe.wait_ge(xst_sb, 2 * i + o + 1)
                for half in range(2):
                    if not isinstance(i, int) or o >= 1:
                        pe.wait_ge((h_half0, h_half1)[half], 2 * i + o)
                    for c in range(2):
                        mm = pe.matmul(ps3[:, half, :], xst[:, s, c, :],
                                       w1_sb[:, bass.ds(e, 1), c, half * 512:(half + 1) * 512].rearrange("p e h -> p (e h)"),
                                       start=(c == 0), stop=(c == 1))
                    mm.then_inc(h_ps, 1)

            def turn_hidden(i, o):
                if not tile(i, o):
                    return
                pe.wait_ge(h_half0, 2 * i + o + 1)
                pe.wait_ge(h_half1, 2 * i + o + 1)
                if not isinstance(i, int) or o >= 1:
                    pe.wait_ge(ht_ready, 2 * i + o)
                for c in range(FC):
                    mm = pe.transpose(ps2[:, 0, c * 128:(c + 1) * 128], h_sb[:, c::FC], ident[:, :])
                mm.then_inc(ht_ps, 1)

            def down(i, o):
                if not tile(i, o):
                    return
                e = pe.value_load(etile[0:1, bass.ds(2 * i + o, 1)], min_val=0, max_val=NE - 1)
                pe.wait_ge(ht_ready, 2 * i + o + 1)
                if not isinstance(i, int) or o >= 1:
                    pe.wait_ge(y_ready, 2 * i + o)
                for c in range(FC):
                    mm = pe.matmul(ps1[:, 1, 0:D], ht_sb[:, c, :], w2_sb[:, bass.ds(e, 1), c, :].rearrange("p e d -> p (e d)"),
                                   start=(c == 0), stop=(c == FC - 1))
                mm.then_inc(y_ps, 1)

            def expert_step(i, o):
                up(i, o)
                turn_rows(i, o + 1)
                down(i, o - 1)
                turn_hidden(i, o)

            expert_step(0, -1)
            expert_step(0, 0)
            with pe.Fori(0, (TILES - 2) // 2) as i:
                expert_step(i, 1)
                expert_step(i, 2)
            for k in (TILES - 1, TILES):
                expert_step(0, k)

        @block.scalar
        def _(act):
            own = Chain(act, act_own)

            with act.Fori(0, NB) as b:
                act.wait_ge(ln_var_ready, b + 1)
                act.activation(ln_std[:, :], ln_var[:, :], ACT.Sqrt).then_inc(ln_std_ready, 1)

            pw = ps1[:, 0, :]
            act.wait_ge(w_mm, 1)
            act.activation(lin_t[:, :], pw[0:M, 0:128], ACT.Copy).then_inc(w_copied, 1)
            act.wait_ge(w_mm, 2)
            act.activation(tp_t[:, :, :].rearrange("p a b -> p (a b)"), pw[0:M, 128:384], ACT.Copy,
                           scale=c_tp * c_lin * c_lin).then_inc(w_copied, 1)
            act.wait_ge(w_mm, 3)
            act.activation(w_hid[:, 0:M], pw[:, 0:M], ACT.Copy)
            act.activation(w_hid[:, M:128], pw[:, 0:M], ACT.Copy, scale=-1.0)
            act.activation(ba_t[:, :], pw[0:M, 128:256], ACT.Copy)
            act.activation(d_t[:, 0:M], pw[0:M, 256:320], ACT.Copy)
            act.activation(c_t[:, M:128], pw[0:M, 320:384], ACT.Copy).then_inc(w_copied, 1)
            act.wait_ge(w_mm, 4)
            act.activation(w_z[:, 0:M], pw[:, 0:M], ACT.Copy, scale=c_tp)
            act.activation(w_z[:, M:192], pw[:, M:192], ACT.Copy, scale=c_tp * SQ3)
            act.activation(w_v[:, :], pw[0:M, 192:256], ACT.Copy, scale=c_tp)
            act.activation(w_sc[0:M, 0:M], wsm[:, len(names) - 1, :], ACT.Copy, scale=c_lin)
            act.activation(w_sc[M:128, 0:M], wsm[:, len(names) - 1, :], ACT.Copy, scale=-0.01 * c_lin).then_inc(w_copied, 1)

            act.wait_ge(edge_sq_ready, 1)
            act.activation(edge_len[:, 1, :], edge_len[:, 0, :], ACT.Sqrt).then_inc(edge_len_ready, 1)

            with act.Fori(0, NB) as b:
                act.wait_ge(head_dev, b + 1)
                act.activation(hsq[:, :, :], hx[:, :, :], ACT.Square).then_inc(head_sq, 1)
                act.wait_ge(head_var, b + 1)
                act.activation(hstat[:, 2, :], hstat[:, 1, :], ACT.Sqrt, scale=1.0 / (HC - 1)).then_inc(head_std, 1)

            def stage_idx(i, o):
                if not group(i, o):
                    return
                s = o % RING
                if not isinstance(i, int) or o >= RING:
                    act.wait_ge(main.gathered[s], 16 * TG * (i + o // RING))
                act.activation(idx_st[:, s, :], edge_src[:, bass.ds(TG * (RING * i + o), TG)], ACT.Copy).then_inc(main.idx, 1)

            def copy_z(i, o):
                if not group(i, o):
                    return
                s = o % 2
                act.wait_ge(main.zt_ps, RING * i + o + 1)
                if not isinstance(i, int) or o >= 2:
                    act.wait_ge(main.pq, RING * i + o - 1)
                act.activation(zt[:, s, :], ps1[:, 0, 0:GE], ACT.Copy).then_inc(main.zt_sb, 1)

            def relu(i, o):
                if not group(i, o):
                    return
                s = o % 2
                act.wait_ge(main.hid_ps, RING * i + o + 1)
                if not isinstance(i, int) or o >= 2:
                    act.wait_ge(main.scores, RING * i + o - 1)
                act.activation(hid_sb[:, s, :], ps1[:, 1, 0:GE], ACT.Relu).then_inc(main.hid_sb, 1)

            def exps(i, o):
                if not group(i, o):
                    return
                s = o % 2
                act.wait_ge(main.neg_top, RING * i + o + 1)
                if not isinstance(i, int) or o >= 2:
                    act.wait_ge(main.eo, RING * i + o - 1)
                    act.wait_ge(main.coef, RING * i + o - 1)
                for tt in range(TG):
                    act.activation(e0[:, s, tt, :], ps3[:, 1, tt * 96:tt * 96 + M], ACT.Exp,
                                   bias=neg_top[:, s, tt:tt + 1], accum_out=exp_sum[:, s, tt:tt + 1])
                act.activation(exp_neg[:, s, :], neg_top[:, s, :], ACT.Exp).then_inc(main.exp, 1)

            def copy_q(i, o):
                if not group(i, o):
                    return
                s = o % 2
                act.wait_ge(main.pq, RING * i + o + 1)
                if not isinstance(i, int) or o >= 2:
                    act.wait_ge(main.scattered, RING * i + o - 1)
                act.activation(qeo[:, s, :, :, :].rearrange("p t a f -> p t (a f)"),
                               ps2[:, s, 0:768].rearrange("p (t f) -> p t f", f=256)[:, :, M:192], ACT.Copy).then_inc(main.q_sb, 1)

            act.wait_ge(kv_ready, 2)
            for k in range(-1 + 4):
                stage_idx(0, k)

            def step(i, k):
                relu(i, k)
                exps(i, k - 1)
                copy_z(i, k + 1)
                copy_q(i, k)
                stage_idx(i, k + 4)

            steps(act, step, -1, FIRST, TURNS, G + 1)

            act.wait_ge(flag_ready, 1)
            far = act.value_load(spread_i[0:1, 0:1], min_val=0, max_val=1)
            with act.If(far > 0):
                with act.Fori(0, G) as g:
                    act.wait_ge(wide.added, g * NWIN + 1)
                    act.activation(idx_st[:, 0, :], edge_src[:, bass.ds(TG * g, TG)], ACT.Copy).then_inc(wide.idx, 1)
                    act.wait_ge(wide.zt_ps, g + 1)
                    act.activation(zt[:, 0, :], ps1[:, 0, 0:GE], ACT.Copy).then_inc(wide.zt_sb, 1)
                    act.wait_ge(wide.hid_ps, g + 1)
                    act.activation(hid_sb[:, 0, :], ps1[:, 1, 0:GE], ACT.Relu).then_inc(wide.hid_sb, 1)
                    act.wait_ge(wide.pq, g + 1)
                    act.activation(qeo[:, 0, :, :, :].rearrange("p t a f -> p t (a f)"),
                                   ps2[:, 0, 0:768].rearrange("p (t f) -> p t f", f=256)[:, :, M:192],
                                   ACT.Copy).then_inc(wide.q_sb, 1)
                    act.wait_ge(wide.neg_top, g + 1)
                    for tt in range(TG):
                        act.activation(e0[:, 0, tt, :], ps3[:, 1, tt * 96:tt * 96 + M], ACT.Exp,
                                       bias=neg_top[:, 0, tt:tt + 1], accum_out=exp_sum[:, 0, tt:tt + 1])
                    act.activation(exp_neg[:, 0, :], neg_top[:, 0, :], ACT.Exp).then_inc(wide.exp, 1)

            act.wait_ge(agg_final, 1)

            def node_tiles(b):
                if past(b):
                    act.wait_ge(epi_xt_ps, b * JB)
                act.activation(xn_st[:, :, :], xn_sb[:, bass.ds(b * JB, JB), :], ACT.Copy).then_inc(epi_staged_x, 1)
                if past(b):
                    act.wait_ge(epi_out, b * JB)
                act.activation(agg_st[:, :, :, :], agg[:, :, 0:N].rearrange("q s (p j) -> q s j p", j=J)[:, :, bass.ds(b * JB, JB), :],
                               ACT.Copy).then_inc(epi_staged, 1)
                for jj in range(JB):
                    act.wait_ge(epi_xt_ps, b * JB + jj + 1)
                    act.activation(xt_sb[:, jj, :, :], ps1[:, 0, 0:256].rearrange("q (c p) -> q c p", p=128)[:, :, 0:P],
                                   ACT.Copy).then_inc(epi_xt_sb, 1)
                act.wait_ge(epi_var, b + 1)
                act.activation(ln_std[:, :], ln_var[:, :], ACT.Sqrt).then_inc(epi_std, 1)
                for jj in range(JB):
                    act.wait_ge(epi_ft_ps, b * JB + jj + 1)
                    act.activation(xt_sb[:, jj, :, :], ps2[:, 0, 0:256].rearrange("q (c p) -> q c p", p=128)[:, :, 0:P],
                                   ACT.Copy).then_inc(epi_ft_sb, 1)

            batches(act, node_tiles)

            act.wait_ge(gap_ready, 1)
            act.activation(gap[:, 1, :], gap[:, 0, :], ACT.Exp).then_inc(gap_exp, 1)

            act.wait_ge(slots_ready, 1)

            def slots_to_send(b):
                if past(b):
                    act.wait_ge(rows_sent, b * 2 * JB * 16)
                act.activation(slot_st[:, :, :], slot_i[:, bass.ds(b * JB, JB), :], ACT.Copy).then_inc(slot_staged, 1)

            batches(act, slots_to_send)

            act.wait_ge(etile_ready, 1)
            act.wait_ge(b_loaded, 32)

            def gelu_pair(i):
                for s in range(2):
                    act.wait_ge(h_ps, 2 * (2 * i + s) + 2)
                    if past(i) or s:
                        act.wait_ge(ht_ps, 2 * i + s)
                    act.activation(h_sb[:, 512:1024], ps3[:, 1, :], ACT.Copy).then_inc(h_half1, 1)
                    act.wait_ge(ht_ps, 2 * i + s + 1)
                    if past(i) or s:
                        act.wait_ge(y_ps, 2 * i + s)
                    act.wait_ge(b1_ready, 2 * i + s + 1)
                    for c in range(FC):
                        ins = act.activation(ht_sb[:, c, :], ps2[:, 0, c * 128:(c + 1) * 128], ACT.Gelu, bias=b1_cur[:, s, c:c + 1])
                    ins.then_inc(ht_ready, 1)

            gelu_pair(0)
            with act.Fori(1, TILES // 2) as i:
                gelu_pair(i)

            act.wait_ge(y_ready, TILES)

            def slots_to_take(b):
                if past(b):
                    act.wait_ge(y_taken, b * 2 * JB * 16)
                act.activation(slot_st2[:, :, :], slot_i[:, bass.ds(b * JB, JB), :], ACT.Copy).then_inc(slot_staged2, 1)

            batches(act, slots_to_take)

        @block.vector
        def _(dve):
            own = Chain(dve, dve_own)

            dve.memset(dst_raw[64:PAIRS, :], int(FAR)).then_inc(raw_padded, 1)
            dve.memset(src_raw[64:PAIRS, :], 0).then_inc(raw_padded, 1)
            dve.memset(attr_raw[64:PAIRS, :, :], 1.0).then_inc(raw_padded, 1)

            dve.wait_ge(x_loaded, 32)
            own.open(3)
            with dve.Fori(0, NB) as b:
                own.enter(b)
                for jj in range(JB):
                    ins = dve.bn_stats(ln_stats[:, jj, :], x_sb[:, bass.ds(b * JB + jj, 1), :].rearrange("p j d -> p (j d)"))
                own(ins)
                dve.memset(ln_var[:, :], 0.0)
                for jj in range(JB):
                    ins = dve.bn_aggr(ln_mv[:, jj, :], ln_stats[:, jj, :])
                own(ins)
                dve.tensor_scalar(ln_var[:, :], ln_mv[:, :, 1], EPS, None, ALU.add).then_inc(ln_var_ready, 1)
                dve.wait_ge(ln_std_ready, b + 1)
                own(dve.reciprocal(ln_rstd[:, :], ln_std[:, :]))
                for jj in range(JB):
                    ins = dve.tensor_scalar(xn_sb[:, bass.ds(b * JB + jj, 1), :].rearrange("p j d -> p (j d)"),
                                            x_sb[:, bass.ds(b * JB + jj, 1), :].rearrange("p j d -> p (j d)"),
                                            ln_mv[:, jj, 0:1], ln_rstd[:, jj:jj + 1], ALU.subtract, ALU.mult)
                ins.then_inc(xn_ready, 1)
                dve.wait_ge(xn_ready, b + 1)
            own.leave(NB)

            dve.wait_ge(raw_loaded, 16 * 9)
            dve.tensor_copy(src_f[:, :], src_raw[:, :])
            own(dve.tensor_copy(dst_f[:, :, :].rearrange("p h e -> p (h e)"), dst_raw[:, :]))
            own(dve.tensor_reduce(dlow[:, :], dst_f[:, :, :], AX.X, ALU.min))
            own(dve.scalar_tensor_tensor(out=loc_f[:, :, :], in0=dst_f[:, :, :], scalar=FAR - 1.0, in1=dst_f[:, :, :],
                                         op0=ALU.is_lt, op1=ALU.mult))
            own(dve.tensor_reduce(dhigh[:, :], loc_f[:, :, :], AX.X, ALU.max))
            own(dve.tensor_tensor(dspread[:, :], dhigh[:, :], dlow[:, :], ALU.subtract))
            own(dve.tensor_tensor(dspread[:, 0:1], dspread[:, 0:1], dspread[:, 1:2], ALU.max))
            for h in range(2):
                ins = dve.tensor_scalar(loc_f[:, h, :], dst_f[:, h, :], dlow[:, h:h + 1], None, ALU.subtract)
            ins.then_inc(edge_rows_ready, 1)
            dve.wait_ge(edge_rows_ready, 1)

            def cols(bank):
                return bank[:, 0:NT].rearrange("p (c j) -> p j c", j=PAIRS)

            def rows(tab):
                return tab.rearrange("p (j c) -> p j c", c=NC6)

            banks = [ps2[:, 0, 0:512], ps2[:, 0, 512:1024], ps2[:, 1, 0:512], ps2[:, 1, 512:1024], ps3[:, 0, :], ps3[:, 1, :]]
            dests = [edge_dst[:, :], edge_loc[:, :], edge_src[:, :]] + [edge_tmp[:, :, m] for m in range(3)]
            for k, (bank, tab) in enumerate(zip(banks, dests)):
                dve.wait_ge(edge_cols_ready, k + 1)
                dve.tensor_copy(rows(tab), cols(bank)).then_inc(edge_cols_taken, 1)
            dve.wait_ge(spread_col, 1)
            for h in range(2):
                ins = dve.tensor_copy(base_i[:, :, h], ps1[0:1, 1, h * PAIRS:(h + 1) * PAIRS])
            ins.then_inc(base_ready, 1)
            own(dve.tensor_reduce(spread_row[:, :], ps1[0:1, 1, 2 * PAIRS:3 * PAIRS], AX.X, ALU.max))
            dve.tensor_scalar(spread_i[:, :], spread_row[:, :], float(WIN), None, ALU.is_ge).then_inc(flag_ready, 1)
            dve.wait_ge(edge_cols_taken, 6)
            own(dve.tensor_tensor(edge_r[:, :, :], edge_tmp[:, :, :], edge_tmp[:, :, :], ALU.mult))
            dve.tensor_reduce(edge_len[:, 0, :], edge_r[:, :, :], AX.X, ALU.add).then_inc(edge_sq_ready, 1)
            dve.wait_ge(edge_len_ready, 1)
            own(dve.tensor_scalar(edge_len[:, 0, :], edge_len[:, 1, :], 1e-12, None, ALU.add))
            own(dve.reciprocal(edge_len[:, 1, :], edge_len[:, 0, :]))
            own(dve.tensor_tensor(edge_r[:, :, :], edge_tmp[:, :, :], edge_len[:, 1, :].unsqueeze(2).to_broadcast([128, NT, 3]),
                                  ALU.mult))
            own(dve.tensor_tensor(edge_tmp[:, :, :], edge_r[:, :, :], edge_r[:, :, :], ALU.mult))
            own(dve.tensor_reduce(edge_rr[:, :], edge_tmp[:, :, :], AX.X, ALU.add))

            dve.wait_ge(consts_ready, 14)
            for c in range(2):
                ins = dve.tensor_reduce(pick_m[:, c, :], pick[:, c, :, :].rearrange("p u m -> p m u"), AX.X, ALU.add)
            own(ins)
            dve.wait_ge(w_mm, 5)
            for c in range(2):
                ins = dve.tensor_tensor(w_vec[:, c, :, :], ps1[:, 0, 256 + c * M:256 + (c + 1) * M].unsqueeze(2).to_broadcast([128, M, 3]),
                                        pick_m[:, c, :].unsqueeze(1).to_broadcast([128, M, 3]), ALU.mult)
            own(ins)
            dve.memset(ps2[:, :, :], 0.0)
            dve.memset(ps3[:, :, :], 0.0).then_inc(banks_cleared, 1)

            own.open(4)

            def head_features(b):
                own.enter(b)
                xh = xn_sb[:, bass.ds(b * JB, JB), :].rearrange("p j (h c) -> p (j h) c", c=HC)
                own(dve.tensor_reduce(hstat[:, 0, :], xh, AX.X, ALU.add))
                own(dve.tensor_scalar(hstat[:, 0, :], hstat[:, 0, :], 1.0 / HC, None, ALU.mult))
                if past(b):
                    dve.wait_ge(head_used, b)
                dve.tensor_tensor(hx[:, :, :], xh, hstat[:, 0, :].unsqueeze(2).to_broadcast([P, JB * H, HC]),
                                  ALU.subtract).then_inc(head_dev, 1)
                dve.wait_ge(head_sq, b + 1)
                dve.tensor_reduce(hstat[:, 1, :], hsq[:, :, :], AX.X, ALU.add).then_inc(head_var, 1)
                dve.wait_ge(head_std, b + 1)
                own(dve.tensor_scalar(hstat[:, 1, :], hstat[:, 2, :], EPS, None, ALU.add))
                own(dve.reciprocal(hstat[:, 0, :], hstat[:, 1, :]))
                dve.tensor_tensor(hx[:, :, :], hx[:, :, :], hstat[:, 0, :].unsqueeze(2).to_broadcast([P, JB * H, HC]),
                                  ALU.mult).then_inc(head_ready, 1)
                dve.wait_ge(head_ready, b + 1)

            batches(dve, head_features)
            own.leave(NB)

            dve.wait_ge(head_used, NB)
            dve.wait_ge(mixw_loaded, 64)
            for c in range(2):
                cs = slice(c * 128, (c + 1) * 128)
                own(dve.tensor_scalar(kv_col[:, 0:1], kb_col[:, c:c + 1], float(N), None, ALU.mult))
                own(dve.scalar_tensor_tensor(out=kv_col[:, 1:2], in0=ps2[:, c, 512:513], scalar=kw_col[:, c:c + 1],
                                             in1=kv_col[:, 0:1], op0=ALU.mult, op1=ALU.add))
                own(dve.scalar_tensor_tensor(out=kv_tmp[:, 0, :], in0=ps2[:, c, 0:128], scalar=kw_col[:, c:c + 1],
                                             in1=vw_bc[:, cs], op0=ALU.mult, op1=ALU.mult))
                own(dve.scalar_tensor_tensor(out=kv_tmp[:, 1, :], in0=vb_bc[:, cs], scalar=kv_col[:, 1:2],
                                             in1=kv_tmp[:, 0, :], op0=ALU.mult, op1=ALU.add))
                own(dve.scalar_tensor_tensor(out=kv_tmp[:, 2, :], in0=ps3[:, 0, cs], scalar=kb_col[:, c:c + 1],
                                             in1=vw_bc[:, cs], op0=ALU.mult, op1=ALU.mult))
                own(dve.tensor_tensor(kv_tmp[:, 0, :], kv_tmp[:, 1, :], kv_tmp[:, 2, :], ALU.add))
                dve.tensor_tensor(kv[:, c, :], kv_tmp[:, 0, :], head_block[:, :], ALU.mult).then_inc(kv_ready, 1)
                dve.wait_ge(kv_ready, c + 1)

            def dots(i, o):
                if not group(i, o):
                    return
                s = o % RING
                dve.wait_ge(main.gathered[s], 16 * TG * (i + o // RING + 1))
                if not isinstance(i, int) or o >= 1:
                    dve.wait_ge(main.dot, RING * i + o)
                r = edge_r[:, bass.ds(TG * (RING * i + o), TG), :].unsqueeze(2).to_broadcast([128, TG, M, 3])
                dve.tensor_tensor(prod[:, :, :, :], xg[:, s, :, 128:320].rearrange("p t (u m) -> p t u m", m=3), r,
                                  ALU.mult).then_inc(main.prod, 1)
                dve.wait_ge(main.prod, RING * i + o + 1)
                dve.tensor_reduce(xg[:, s, :, 0:M], prod[:, :, :, :], AX.X, ALU.add).then_inc(main.dot, 1)

            def maxima(i, o):
                if not group(i, o):
                    return
                s = o % 2
                dve.wait_ge(main.scores, RING * i + o + 1)
                if not isinstance(i, int) or o >= 1:
                    dve.wait_ge(main.neg_top, RING * i + o)
                dve.tensor_reduce(top[:, :], ps3[:, 1, 0:TG * 96].rearrange("p (t f) -> p t f", f=96)[:, :, 0:M], AX.X,
                                  ALU.max).then_inc(main.top, 1)
                dve.wait_ge(main.top, RING * i + o + 1)
                dve.tensor_scalar(neg_top[:, s, :], top[:, :], -1.0, 0.0, ALU.mult, ALU.min).then_inc(main.neg_top, 1)

            def hots(i, o):
                if not group(i, o):
                    return
                if not isinstance(i, int) or o >= 1:
                    dve.wait_ge(main.sel, RING * i + o)
                loc = edge_loc[:, bass.ds(TG * (RING * i + o), TG)].unsqueeze(2).to_broadcast([128, TG, WIN])
                dve.tensor_tensor(hot[:, :, :], iota_w[:, :].unsqueeze(1).to_broadcast([128, TG, WIN]), loc,
                                  ALU.is_equal).then_inc(main.hot, 1)

            def out0(i, o):
                if not group(i, o):
                    return
                s = o % 2
                dve.wait_ge(main.q_sb, RING * i + o + 1)
                if not isinstance(i, int) or o >= 1:
                    dve.wait_ge(main.eo, RING * i + o)
                for tt in range(TG):
                    ins = dve.scalar_tensor_tensor(out=o0[:, tt, :], in0=qeo[:, s, tt, 0, :],
                                                   scalar=edge_rr[:, bass.ds(TG * (RING * i + o) + tt, 1)],
                                                   in1=ps2[:, s, tt * 256:tt * 256 + M], op0=ALU.mult, op1=ALU.add)
                ins.then_inc(main.o0, 1)

            def coefs(i, o):
                if not group(i, o):
                    return
                s = o % 2
                g = RING * i + o
                dve.wait_ge(main.exp, g + 1)
                if not isinstance(i, int) or o >= 1:
                    dve.wait_ge(main.sel, g)
                dve.scalar_tensor_tensor(out=norm[:, :], in0=exp_neg[:, s, :], scalar=float(V), in1=exp_sum[:, s, :],
                                         op0=ALU.mult, op1=ALU.add).then_inc(main.norm, 1)
                dve.wait_ge(main.norm, 3 * g + 1)
                dve.reciprocal(coef[:, :, 3], norm[:, :]).then_inc(main.norm, 1)
                dve.wait_ge(main.norm, 3 * g + 2)
                dve.tensor_tensor(coef[:, :, 4], exp_neg[:, s, :], coef[:, :, 3], ALU.mult).then_inc(main.norm, 1)
                dve.wait_ge(main.norm, 3 * g + 3)
                dve.tensor_tensor(coef[:, :, 0:3], edge_r[:, bass.ds(TG * g, TG), :],
                                  coef[:, :, 4].unsqueeze(2).to_broadcast([128, TG, 3]), ALU.mult).then_inc(main.coef, 1)

            def weigh(i, o):
                if not group(i, o):
                    return
                s = o % 2
                g = RING * i + o
                if not isinstance(i, int) or o >= 2:
                    dve.wait_ge(main.scattered, g - 1)
                dve.wait_ge(main.o0, g + 1)
                dve.tensor_tensor(qeo[:, s, :, 0, :], e0[:, s, :, :], o0[:, :, :], ALU.mult).then_inc(main.eo, 1)
                dve.wait_ge(main.hot, g + 1)
                dve.wait_ge(main.coef, g + 1)
                dve.tensor_tensor(sel[:, s, 0:TG * 5 * WIN].rearrange("p (t k w) -> p t k w", t=TG, k=5),
                                  hot[:, :, :].unsqueeze(2).to_broadcast([128, TG, 5, WIN]),
                                  coef[:, :, :].unsqueeze(3).to_broadcast([128, TG, 5, WIN]), ALU.mult).then_inc(main.sel, 1)

            def add(i, o):
                if not group(i, o):
                    return
                s = o % 2
                g = RING * i + o
                base = dve.value_load(base_i[0:1, :, :].rearrange("p a b -> p (a b)")[:, bass.ds(g, 1)], min_val=0, max_val=N)
                win = agg[:, :, bass.ds(base, WIN)]
                dve.wait_ge(main.scattered, g + 1)
                if not isinstance(i, int) or o >= 1:
                    dve.wait_ge(main.added, g)
                dve.tensor_tensor(win, win, ps3[:, 0, 64:64 + 6 * WIN].rearrange("p (k w) -> p k w", w=WIN),
                                  ALU.add).then_inc(main.added, 1)

            dve.wait_ge(kv_ready, 2)
            dve.wait_ge(base_ready, 1)
            dve.wait_ge(zeros_written, 16)

            def step(i, k):
                maxima(i, k - 1)
                dots(i, k + 1)
                add(i, k - 2)
                hots(i, k - 1)
                out0(i, k - 1)
                coefs(i, k - 1)
                weigh(i, k - 1)

            steps(dve, step, -1, FIRST, TURNS, G + 2)
            dve.wait_ge(main.added, G)

            far = dve.value_load(spread_i[0:1, 0:1], min_val=0, max_val=1)
            with dve.If(far > 0):
                dve.memset(agg[:, :, :], 0.0).then_inc(wide.added, 1)
                dve.wait_ge(wide.added, 1)
                with dve.Fori(0, G) as g:
                    dve.wait_ge(wide.gathered[0], 16 * TG * (g + 1))
                    r = edge_r[:, bass.ds(TG * g, TG), :].unsqueeze(2).to_broadcast([128, TG, M, 3])
                    dve.tensor_tensor(prod[:, :, :, :], xg[:, 0, :, 128:320].rearrange("p t (u m) -> p t u m", m=3), r,
                                      ALU.mult).then_inc(wide.prod, 1)
                    dve.wait_ge(wide.prod, g + 1)
                    dve.tensor_reduce(xg[:, 0, :, 0:M], prod[:, :, :, :], AX.X, ALU.add).then_inc(wide.dot, 1)
                    dve.wait_ge(wide.q_sb, g + 1)
                    for tt in range(TG):
                        ins = dve.scalar_tensor_tensor(out=o0[:, tt, :], in0=qeo[:, 0, tt, 0, :],
                                                       scalar=edge_rr[:, bass.ds(TG * g + tt, 1)],
                                                       in1=ps2[:, 0, tt * 256:tt * 256 + M], op0=ALU.mult, op1=ALU.add)
                    ins.then_inc(wide.o0, 1)
                    dve.wait_ge(wide.scores, g + 1)
                    dve.tensor_reduce(top[:, :], ps3[:, 1, 0:TG * 96].rearrange("p (t f) -> p t f", f=96)[:, :, 0:M], AX.X,
                                      ALU.max).then_inc(wide.top, 1)
                    dve.wait_ge(wide.top, g + 1)
                    dve.tensor_scalar(neg_top[:, 0, :], top[:, :], -1.0, 0.0, ALU.mult, ALU.min).then_inc(wide.neg_top, 1)
                    dve.wait_ge(wide.exp, g + 1)
                    dve.scalar_tensor_tensor(out=norm[:, :], in0=exp_neg[:, 0, :], scalar=float(V), in1=exp_sum[:, 0, :],
                                             op0=ALU.mult, op1=ALU.add).then_inc(wide.norm, 1)
                    dve.wait_ge(wide.norm, 3 * g + 1)
                    dve.reciprocal(coef[:, :, 3], norm[:, :]).then_inc(wide.norm, 1)
                    dve.wait_ge(wide.norm, 3 * g + 2)
                    dve.tensor_tensor(coef[:, :, 4], exp_neg[:, 0, :], coef[:, :, 3], ALU.mult).then_inc(wide.norm, 1)
                    dve.wait_ge(wide.norm, 3 * g + 3)
                    dve.tensor_tensor(coef[:, :, 0:3], edge_r[:, bass.ds(TG * g, TG), :],
                                      coef[:, :, 4].unsqueeze(2).to_broadcast([128, TG, 3]), ALU.mult).then_inc(wide.coef, 1)
                    dve.wait_ge(wide.o0, g + 1)
                    dve.tensor_tensor(qeo[:, 0, :, 0, :], e0[:, 0, :, :], o0[:, :, :], ALU.mult).then_inc(wide.eo, 1)
                    dve.wait_ge(wide.eo, g + 1)
                    dve.wait_ge(wide.coef, g + 1)
                    dve.tensor_scalar(loc_w[:, :], edge_dst[:, bass.ds(TG * g, TG)], 1.0, None, ALU.mult).then_inc(loc_ready, 1)
                    with dve.Fori(0, NWIN) as w:
                        n = g * NWIN + w
                        dve.wait_ge(loc_ready, n + g + 1)
                        dve.tensor_tensor(hot[:, :, :], iota_w[:, :].unsqueeze(1).to_broadcast([128, TG, WIN]),
                                          loc_w[:, :].unsqueeze(2).to_broadcast([128, TG, WIN]), ALU.is_equal).then_inc(wide.hot, 1)
                        dve.wait_ge(wide.hot, n + 1)
                        dve.tensor_tensor(sel[:, 0, 0:TG * 5 * WIN].rearrange("p (t k w) -> p t k w", t=TG, k=5),
                                          hot[:, :, :].unsqueeze(2).to_broadcast([128, TG, 5, WIN]),
                                          coef[:, :, :].unsqueeze(3).to_broadcast([128, TG, 5, WIN]), ALU.mult).then_inc(wide.sel, 1)
                        dve.tensor_scalar(loc_w[:, :], loc_w[:, :], float(WIN), None, ALU.subtract).then_inc(loc_ready, 1)
                        dve.wait_ge(wide.scattered, n + 1)
                        win = agg[:, :, bass.ds(w * WIN, WIN)]
                        dve.tensor_tensor(win, win, ps3[:, 0, 64:64 + 6 * WIN].rearrange("p (k w) -> p k w", w=WIN),
                                          ALU.add).then_inc(wide.added, 1)
                dve.wait_ge(wide.added, G * NWIN + 1)
            dve.tensor_scalar(agg[:, :, N:NW], agg[:, :, N:NW], 0.0, None, ALU.mult).then_inc(agg_final, 1)

            own.open(7)

            def sums_and_gate(b):
                own.enter(b)
                xb = x_sb[:, bass.ds(b * JB, JB), :]
                own(dve.scalar_tensor_tensor(out=res[:, :, :], in0=xn_sb[:, bass.ds(b * JB, JB), :], scalar=2.0, in1=xb,
                                             op0=ALU.mult, op1=ALU.add))
                for jj in range(JB):
                    dve.wait_ge(epi_out, b * JB + jj + 1)
                    dve.tensor_tensor(res[:, jj, :], res[:, jj, :], ps1[0:P, 1, 0:D], ALU.add).then_inc(epi_res, 1)
                dve.wait_ge(epi_res, (b + 1) * JB)
                for jj in range(JB):
                    ins = dve.bn_stats(ln_stats[:, jj, :], res[:, jj, :])
                own(ins)
                dve.tensor_scalar(xb, res[:, :, :], 1.0, None, ALU.mult)
                for jj in range(JB):
                    ins = dve.bn_aggr(ln_mv[:, jj, :], ln_stats[:, jj, :])
                own(ins)
                dve.tensor_scalar(ln_var[:, :], ln_mv[:, :, 1], EPS, None, ALU.add).then_inc(epi_var, 1)
                dve.tensor_copy(mean2[:, bass.ds(b * JB, JB)], ln_mv[:, :, 0])
                dve.wait_ge(epi_std, b + 1)
                own(dve.reciprocal(ln_rstd[:, :], ln_std[:, :]))
                for jj in range(JB):
                    dve.tensor_scalar(xf_sb[:, jj, :], res[:, jj, :], ln_mv[:, jj, 0:1], ln_rstd[:, jj:jj + 1],
                                      ALU.subtract, ALU.mult).then_inc(epi_xf, 1)
                dve.wait_ge(epi_logit, b + 1)
                own(dve.tensor_tensor(logit[:, :, :], ps3[0:P, 0, 0:JB * NE].rearrange("p (j e) -> p j e", e=NE),
                                      bg_bc[:, :].unsqueeze(1).to_broadcast([P, JB, NE]), ALU.add))
                dve.tensor_scalar(rstd2[:, bass.ds(b * JB, JB)], ln_rstd[:, :], 1.0, None, ALU.mult)
                for jj in range(JB):
                    ins = dve.max(top8[:, jj, :], logit[:, jj, :])
                own(ins)
                dve.tensor_scalar(top_w[:, bass.ds(b * JB, JB), :], top8[:, :, 0:K2], 1.0, None, ALU.mult)
                for jj in range(JB):
                    ins = dve.max_index(top8_i[:, jj, :], top8[:, jj, :], logit[:, jj, :])
                own(ins)
                dve.tensor_scalar(top_i[:, bass.ds(b * JB, JB), :], top8_i[:, :, 0:K2], 1.0, None, ALU.mult).then_inc(epi_done, 1)
                dve.wait_ge(epi_done, b + 1)

            batches(dve, sums_and_gate)
            own.leave(NB)

            dve.tensor_tensor(gap[:, 0, :], top_w[:, :, 1], top_w[:, :, 0], ALU.subtract).then_inc(gap_ready, 1)
            for k in range(K2):
                ins = dve.tensor_tensor(picked[:, k, :, :], top_i[:, :, k].unsqueeze(2).to_broadcast([P, J, NE]),
                                        iota_e[:, :].unsqueeze(1).to_broadcast([P, J, NE]), ALU.is_equal)
            own(ins)
            own(dve.tensor_tensor(both[:, :, :], picked[:, 0, :, :], picked[:, 1, :, :], ALU.add))
            for e in range(NE):
                ins = dve.tensor_tensor_scan(ranks[:, :, e], ones[0:P, 0:J], both[:, :, e], 0.0, ALU.mult, ALU.add)
            own(ins)
            dve.tensor_copy(tot[:, :], ranks[:, J - 1, :]).then_inc(tot_ready, 1)
            dve.wait_ge(tot_ready, 1)
            own(dve.tensor_tensor(ranks[:, :, :], ranks[:, :, :], both[:, :, :], ALU.subtract))
            dve.wait_ge(rank0_ps, 1)
            own(dve.tensor_scalar(n_tiles_i[:, 0, :], ps1[:, 0, 128:128 + NE], 127.0, None, ALU.add))
            own(dve.tensor_scalar(n_tiles_i[:, 1, :], n_tiles_i[:, 0, :], 7, None, ALU.arith_shift_right))
            own(dve.tensor_copy(n_tiles[:, 0, :], n_tiles_i[:, 1, :]))
            own(dve.tensor_tensor_scan(n_tiles[:, 1, :], ones[:, 0:NE], n_tiles[:, 0, :], 0.0, ALU.mult, ALU.add))
            own(dve.tensor_tensor(n_tiles[:, 2, :], n_tiles[:, 1, :], n_tiles[:, 0, :], ALU.subtract))
            own(dve.scalar_tensor_tensor(out=row0[:, :], in0=n_tiles[0:P, 2, :], scalar=128.0, in1=ps1[0:P, 0, 0:NE],
                                         op0=ALU.mult, op1=ALU.add))
            own(dve.tensor_tensor(ranks[:, :, :], ranks[:, :, :], row0[:, :].unsqueeze(1).to_broadcast([P, J, NE]), ALU.add))
            for k in range(K2):
                own(dve.tensor_tensor(both[:, :, :], ranks[:, :, :], picked[:, k, :, :], ALU.mult))
                own(dve.tensor_reduce(slot_f[:, k, :], both[:, :, :], AX.X, ALU.add))
            dve.tensor_copy(slot_i[:, :, :].rearrange("p j k -> p k j"), slot_f[:, :, :]).then_inc(slots_ready, 1)
            own(dve.tensor_tensor(ended[:, :, :], iota_tile[:, :].unsqueeze(2).to_broadcast([1, TILES, NE]),
                                  n_tiles[0:1, 1, :].unsqueeze(1).to_broadcast([1, TILES, NE]), ALU.is_ge))
            own(dve.tensor_reduce(etile_f[:, :], ended[:, :, :], AX.X, ALU.add))
            dve.tensor_scalar(etile[:, :], etile_f[:, :], float(NE - 1), None, ALU.min).then_inc(etile_ready, 1)
            dve.wait_ge(gap_exp, 1)
            own(dve.tensor_scalar(gap[:, 0, :], gap[:, 1, :], 1.0, None, ALU.add))
            own(dve.reciprocal(top_w[:, :, 0], gap[:, 0, :]))
            own(dve.tensor_tensor(top_w[:, :, 1], gap[:, 1, :], top_w[:, :, 0], ALU.mult))

            def stage_rows(b):
                if past(b):
                    dve.wait_ge(rows_sent, b * 2 * JB * 16)
                for jj in range(JB):
                    j = b * JB + jj
                    dve.tensor_scalar(row_st[:, jj, :], x_sb[:, bass.ds(j, 1), :].rearrange("p j d -> p (j d)"),
                                      mean2[:, bass.ds(j, 1)], rstd2[:, bass.ds(j, 1)], ALU.subtract,
                                      ALU.mult).then_inc(row_staged, 1)

            batches(dve, stage_rows)

            dve.wait_ge(rows_sent, 16 * 2 * J)
            dve.wait_ge(etile_ready, 1)
            dve.wait_ge(b_loaded, 32)

            def rows_t(i, o):
                dve.wait_ge(xst_ps, 2 * i + o + 1)
                if not isinstance(i, int) or o >= 2:
                    dve.wait_ge(h_ps, 2 * (2 * i + o) - 2)
                dve.tensor_copy(xst[:, o % 2, :, :].rearrange("p c s -> p (c s)"), ps1[:, 0, 0:256]).then_inc(xst_sb, 1)

            rows_t(0, 0)

            def first_half(i, o):
                s = o % 2
                k = 2 * i + o
                e = dve.value_load(etile[0:1, bass.ds(k, 1)], min_val=0, max_val=NE - 1)
                if not isinstance(i, int) or o >= 2:
                    dve.wait_ge(ht_ready, k - 1)
                dve.tensor_scalar(b1_cur[:, s, :], b1_sb[:, bass.ds(e, 1), :].rearrange("p e c -> p (e c)"), 1.0, None,
                                  ALU.mult).then_inc(b1_ready, 1)
                dve.wait_ge(h_ps, 2 * k + 1)
                if past(i) or o:
                    dve.wait_ge(ht_ps, k)
                dve.tensor_copy(h_sb[:, 0:512], ps3[:, 0, :]).then_inc(h_half0, 1)

            def finish(i, o):
                s = o % 2
                k = 2 * i + o
                e = dve.value_load(etile[0:1, bass.ds(k, 1)], min_val=0, max_val=NE - 1)
                dve.wait_ge(y_ps, k + 1)
                if not isinstance(i, int) or o >= 2:
                    dve.wait_ge(ys_written[s], 16 * (i + o // 2))
                dve.tensor_tensor(y_sb[:, s, :], ps1[:, 1, 0:D], b2_bc[:, bass.ds(e, 1), :].rearrange("p e d -> p (e d)"),
                                  ALU.add).then_inc(y_ready, 1)

            first_half(0, 0)
            rows_t(0, 1)
            with dve.Fori(0, (TILES - 2) // 2) as i:
                for o in (1, 2):
                    first_half(i, o)
                    rows_t(i, o + 1)
                    finish(i, o - 1)
            first_half(0, TILES - 1)
            finish(0, TILES - 2)
            finish(0, TILES - 1)

            with dve.Fori(0, NB) as b:
                dve.wait_ge(y_taken, (b + 1) * 2 * JB * 16)
                for jj in range(JB):
                    j = b * JB + jj
                    xj = x_sb[:, bass.ds(j, 1), :].rearrange("p j d -> p (j d)")
                    w = top_w[:, :, :].rearrange("p j k -> p (j k)")
                    dve.scalar_tensor_tensor(out=xj, in0=y_st[:, jj, 0, :], scalar=w[:, bass.ds(2 * j, 1)], in1=xj,
                                             op0=ALU.mult, op1=ALU.add).then_inc(y_first, 1)
                for jj in range(JB):
                    j = b * JB + jj
                    xj = x_sb[:, bass.ds(j, 1), :].rearrange("p j d -> p (j d)")
                    w = top_w[:, :, :].rearrange("p j k -> p (j k)")
                    dve.wait_ge(y_first, j + 1)
                    dve.scalar_tensor_tensor(out=xj, in0=y_st[:, jj, 1, :], scalar=w[:, bass.ds(2 * j + 1, 1)], in1=xj,
                                             op0=ALU.mult, op1=ALU.add).then_inc(summed, 1)


_INS = ["x", "src", "dst", "edge_attr_3"] + ["L0_gnn_" + n for n in (
    "lin_src_w0", "lin_src_w1", "tp1_w00", "tp1_w11", "tp1_w01", "tp1_w10", "tp2_w00", "tp2_w11", "tp2_w01", "tp2_w10",
    "lin_hidden_w0", "lin_hidden_w1", "lin_scalar_w")] + ["L0_mix_" + n for n in (
    "kln_weight", "kln_bias", "vln_weight", "vln_bias")] + ["L0_ffn_" + n for n in ("Wg", "bg", "W1", "b1", "W2", "b2")]


def kernel(**inputs):
    import numpy as _np
    import concourse.bacc as _bacc
    from concourse import mybir as _mybir
    from concourse.bass_utils import run_bass_kernel_spmd as _run

    nc = _bacc.Bacc("TRN2", target_bir_lowering=False, num_devices=1)
    arrays, args = {}, {}
    for name in _INS:
        a = _np.ascontiguousarray(inputs[name])
        arrays[f"in_{name}"] = a
        args[name] = nc.dram_tensor(f"in_{name}", a.shape, _mybir.dt.from_np(a.dtype), kind="ExternalInput").ap()
    shape = inputs["x"].shape
    out = nc.dram_tensor("out_0", shape, _mybir.dt.float32, kind="ExternalOutput").ap()
    gps_layer_kernel(nc, args, out)
    r = _run(nc, [arrays], core_ids=[0])
    return r.results[0]["out_0"]
```

```python
from contextlib import ExitStack

import concourse.bass as bass
from concourse import mybir

ALU = mybir.AluOpType
ACT = mybir.ActivationFunctionType
AX = mybir.AxisListType
F32 = mybir.dt.float32
I32 = mybir.dt.int32
U32 = mybir.dt.uint32

SQ3 = 3.0 ** 0.5
EPS = 1e-5


class Chain:

    def __init__(self, eng, sem):
        self.eng, self.sem, self.base, self.n = eng, sem, 0, 0

    def __call__(self, ins):
        self.n += 1
        ins.then_inc(self.sem, 1)
        self.eng.wait_ge(self.sem, self.base + self.n)

    def open(self, per):
        self.first, self.per = self.base + self.n, per

    def enter(self, i):
        self.base, self.n = self.first + i * self.per, 0

    def leave(self, turns):
        assert self.n == self.per, (self.n, self.per)
        self.base, self.n = self.first + turns * self.per, 0


def gps_layer_kernel(nc, t, out, dbg=None):
    x, src, dst, attr = t["x"], t["src"], t["dst"], t["edge_attr_3"]
    N, D = x.shape
    E = src.shape[0]
    M = t["L0_gnn_lin_src_w0"].shape[0]
    V = D - M
    H, _, HC = t["L0_mix_kln_weight"].shape
    NE, _, HID = t["L0_ffn_W1"].shape
    assert D == 256 and M == 64 and NE == 8 and HID == 1024

    P, J, JB = 125, N // 125, 5
    NB = J // JB
    assert P * J == N and NB * JB == J
    TG, WIN = 3, 32
    GE = TG * 128
    G = -(-E // GE)
    PAIRS = -(-G // 2)
    LAST = E - (PAIRS - 1) * 2 * GE
    NC6 = 2 * TG
    NT = PAIRS * NC6
    NW = N + WIN + 3
    NWIN = -(-N // WIN)
    FAR = 4000.0
    assert FAR > N + WIN and 64 < PAIRS <= 128
    RING = 8
    AHEAD = 5
    FIRST = 6
    TURNS = (G - AHEAD - FIRST) // RING
    K2 = 2
    TILES = K2 * N // 128 + NE
    SLOTS = TILES * 128
    FC = HID // 128

    xn_dram = nc.dram_tensor("xn_rows", (N, D), F32, kind="Internal").ap()
    xs_dram = nc.dram_tensor("expert_in_rows", (SLOTS, D), F32, kind="Internal").ap()
    ys_dram = nc.dram_tensor("expert_out_rows", (SLOTS, D), F32, kind="Internal").ap()

    c_tp = (2.0 * M) ** -0.5
    c_lin = float(M) ** -0.5

    names = ["lin_src_w0", "lin_src_w1", "tp1_w00", "tp1_w11", "tp1_w01", "tp1_w10", "tp2_w00", "tp2_w11",
             "tp2_w01", "tp2_w10", "lin_hidden_w0", "lin_hidden_w1", "lin_scalar_w"]

    with ExitStack() as ctx:
        def sb(scope, name, shape, dt=F32):
            return scope.enter_context(nc.sbuf_tensor(name, shape, dt))

        def sem(name):
            return ctx.enter_context(nc.semaphore(name))

        ps1 = ctx.enter_context(nc.psum_tensor("ps1", [128, 2, 512], F32))
        ps2 = ctx.enter_context(nc.psum_tensor("ps2", [128, 2, 1024], F32))
        ps3 = ctx.enter_context(nc.psum_tensor("ps3", [128, 2, 512], F32))

        x_sb = sb(ctx, "x_sb", [P, J, D])
        ident = sb(ctx, "ident", [128, 128])
        ones = sb(ctx, "ones", [128, 128])
        below = sb(ctx, "below", [P, P])
        iota_e = sb(ctx, "iota_e", [P, NE])
        iota_tile = sb(ctx, "iota_tile", [1, TILES])
        wg_sb = sb(ctx, "wg_sb", [128, 2, NE])
        bg_bc = sb(ctx, "bg_bc", [P, NE])
        spread_i = sb(ctx, "spread_i", [1, 1], I32)
        mean2 = sb(ctx, "mean2", [P, J])
        rstd2 = sb(ctx, "rstd2", [P, J])
        top_w = sb(ctx, "top_w", [P, J, K2])
        top_i = sb(ctx, "top_i", [P, J, K2])
        ln_stats = sb(ctx, "ln_stats", [P, JB, 6])
        ln_mv = sb(ctx, "ln_mv", [P, JB, 2])
        ln_var = sb(ctx, "ln_var", [P, JB])
        ln_std = sb(ctx, "ln_std", [P, JB])
        ln_rstd = sb(ctx, "ln_rstd", [P, JB])

        graph = ExitStack()
        xn_sb = sb(graph, "xn_sb", [P, J, D])
        agg = sb(graph, "agg", [128, 6, NW])
        edge_dst = sb(graph, "edge_dst", [128, NT])
        edge_loc = sb(graph, "edge_loc", [128, NT])
        edge_src = sb(graph, "edge_src", [128, NT], I32)
        edge_r = sb(graph, "edge_r", [128, NT, 3])
        edge_rr = sb(graph, "edge_rr", [128, NT])
        base_i = sb(graph, "base_i", [1, PAIRS, 2], I32)
        iota_w = sb(graph, "iota_w", [128, WIN])
        w_hid = sb(graph, "w_hid", [128, 128])
        w_z = sb(graph, "w_z", [128, 128])
        w_sc = sb(graph, "w_sc", [128, 96])
        place = sb(graph, "place", [128, 3, M, 3])
        place_o0 = sb(graph, "place_o0", [128, 128])
        w_vec = sb(graph, "w_vec", [128, 2, M, 3])
        kv = sb(graph, "kv", [128, 2, 128])

        pre = ExitStack()
        dst_raw = sb(pre, "dst_raw", [PAIRS, 2 * GE], I32)
        src_raw = sb(pre, "src_raw", [PAIRS, 2 * GE], I32)
        attr_raw = sb(pre, "attr_raw", [PAIRS, 2 * GE, 3])
        dst_f = sb(pre, "dst_f", [PAIRS, 2, GE])
        src_f = sb(pre, "src_f", [PAIRS, 2 * GE])
        loc_f = sb(pre, "loc_f", [PAIRS, 2, GE])
        edge_tmp = sb(pre, "edge_tmp", [128, NT, 3])
        edge_len = sb(pre, "edge_len", [128, 2, NT])
        dlow = sb(pre, "dlow", [PAIRS, 2])
        dhigh = sb(pre, "dhigh", [PAIRS, 2])
        dspread = sb(pre, "dspread", [PAIRS, 2])
        spread_row = sb(pre, "spread_row", [1, 1])
        wsm = sb(pre, "wsm", [M, len(names), M])
        lin_t = sb(pre, "lin_t", [M, 128])
        tp_t = sb(pre, "tp_t", [M, 2, 128])
        ba_t = sb(pre, "ba_t", [M, 128])
        d_t = sb(pre, "d_t", [M, 128])
        c_t = sb(pre, "c_t", [M, 128])
        w_v = sb(pre, "w_v", [M, M])
        rep = sb(pre, "rep", [M, 2, 128])
        pick = sb(pre, "pick", [128, 2, M, 3])
        pick_m = sb(pre, "pick_m", [128, 2, 3])
        kw_col = sb(pre, "kw_col", [128, 2])
        kb_col = sb(pre, "kb_col", [128, 2])
        vw_bc = sb(pre, "vw_bc", [128, D])
        vb_bc = sb(pre, "vb_bc", [128, D])
        kv_tmp = sb(pre, "kv_tmp", [128, 3, 128])
        kv_col = sb(pre, "kv_col", [128, 2])
        head_block = sb(pre, "head_block", [128, 128])
        hx = sb(pre, "hx", [P, JB * H, HC])
        hsq = sb(pre, "hsq", [P, JB * H, HC])
        hstat = sb(pre, "hstat", [P, 3, JB * H])
        pre.close()

        loop = ExitStack()
        xg = sb(loop, "xg", [128, RING, TG, 2 * M + D])
        idx_st = sb(loop, "idx_st", [128, RING, TG], I32)
        prod = sb(loop, "prod", [128, TG, M, 3])
        zt = sb(loop, "zt", [128, 2, GE])
        hid_sb = sb(loop, "hid_sb", [128, 2, GE])
        e0 = sb(loop, "e0", [128, 2, TG, M])
        o0 = sb(loop, "o0", [128, 4, TG, M])
        neg_top = sb(loop, "neg_top", [128, 2, TG])
        exp_sum = sb(loop, "exp_sum", [128, 2, TG])
        exp_neg = sb(loop, "exp_neg", [128, 2, TG])
        norm = sb(loop, "norm", [128, TG])
        coef = sb(loop, "coef", [128, 2, TG, 5])
        hot = sb(loop, "hot", [128, 2, TG, WIN])
        sel = sb(loop, "sel", [128, 2, (TG * 5 + 1) * WIN])
        loc_w = sb(loop, "loc_w", [128, TG])
        loop.close()

        epi = ExitStack()
        agg_st = sb(epi, "agg_st", [128, 6, JB, P])
        xn_st = sb(epi, "xn_st", [P, JB, D])
        xt_sb = sb(epi, "xt_sb", [128, JB, 2, P])
        xf_sb = sb(epi, "xf_sb", [P, JB, D])
        res = sb(epi, "res", [P, JB, D])
        logit = sb(epi, "logit", [P, JB, NE])
        top8 = sb(epi, "top8", [P, JB, 8])
        top8_i = sb(epi, "top8_i", [P, JB, 8], U32)
        epi.close()
        graph.close()

        w1_sb = sb(ctx, "w1_sb", [128, NE, 2, HID])
        w2_sb = sb(ctx, "w2_sb", [128, NE, FC, D])
        b1_sb = sb(ctx, "b1_sb", [128, NE, FC])
        b2_bc = sb(ctx, "b2_bc", [128, NE, D])
        picked = sb(ctx, "picked", [P, 2, J, NE])
        ranks = sb(ctx, "ranks", [P, J, NE])
        both = sb(ctx, "both", [P, J, NE])
        tot = sb(ctx, "tot", [P, NE])
        n_tiles = sb(ctx, "n_tiles", [128, 4, NE])
        n_tiles_i = sb(ctx, "n_tiles_i", [128, 2, NE], I32)
        row0 = sb(ctx, "row0", [P, NE])
        slot_f = sb(ctx, "slot_f", [P, 2, J])
        slot_i = sb(ctx, "slot_i", [P, J, 2], I32)
        gap = sb(ctx, "gap", [P, 2, J])
        ended = sb(ctx, "ended", [1, TILES, NE])
        etile_f = sb(ctx, "etile_f", [1, TILES])
        etile = sb(ctx, "etile", [1, TILES], I32)
        ffn = ExitStack()
        xs_sb = sb(ffn, "xs_sb", [128, 2, D])
        xst = sb(ffn, "xst", [128, 2, 2, 128])
        h_sb = sb(ffn, "h_sb", [128, HID])
        ht_sb = sb(ffn, "ht_sb", [128, FC, 128])
        b1_cur = sb(ffn, "b1_cur", [128, 2, FC])
        y_sb = sb(ffn, "y_sb", [128, 2, D])
        ffn.close()
        send = ExitStack()
        slot_st = sb(send, "slot_st", [P, JB, 2], I32)
        row_st = sb(send, "row_st", [P, JB, D])
        send.close()
        take = ExitStack()
        slot_st2 = sb(take, "slot_st2", [P, JB, 2], I32)
        y_st = sb(take, "y_st", [P, JB, 2, D])
        take.close()

        x_loaded, raw_padded, raw_loaded, w_loaded = map(sem, ("x_loaded", "raw_padded", "raw_loaded", "w_loaded"))
        mixw_loaded, gate_loaded = sem("mixw_loaded"), sem("gate_loaded")
        consts_ready, pool_own = sem("consts_ready"), sem("pool_own")
        agg_zeroed, zeros_written = sem("agg_zeroed"), sem("zeros_written")
        dve_own, act_own = sem("dve_own"), sem("act_own")
        ln_var_ready, ln_std_ready = sem("ln_var_ready"), sem("ln_std_ready")
        xn_ready, xn_written = sem("xn_ready"), sem("xn_written")
        edge_rows_ready, edge_cols_ready, edge_cols_taken = map(sem, ("edge_rows_ready", "edge_cols_ready", "edge_cols_taken"))
        spread_col = sem("spread_col")
        edge_sq_ready, edge_len_ready = sem("edge_sq_ready"), sem("edge_len_ready")
        base_ready, flag_ready = sem("base_ready"), sem("flag_ready")
        w_mm, w_copied = sem("w_mm"), sem("w_copied")
        banks_cleared = sem("banks_cleared")
        head_dev, head_sq, head_var, head_std, head_ready, head_used = map(
            sem, ("head_dev", "head_sq", "head_var", "head_std", "head_ready", "head_used"))
        kv_ready, sel_padded = sem("kv_ready"), sem("sel_padded")

        class GroupSems:

            def __init__(s, tag, ring):
                s.ring = ring
                s.gathered = [sem(f"{tag}gathered{i}") for i in range(ring)]
                (s.idx, s.prod, s.dot, s.zt_ps, s.zt_sb, s.hid_ps, s.hid_sb, s.pq, s.scores, s.neg_top, s.exp,
                 s.q_sb, s.o0, s.hot, s.norm, s.coef, s.eo, s.sel, s.scattered, s.added) = (
                    sem(tag + n) for n in ("idx", "prod", "dot", "zt_ps", "zt_sb", "hid_ps", "hid_sb", "pq", "scores",
                                           "neg_top", "exp", "q_sb", "o0", "hot", "norm", "coef", "eo", "sel",
                                           "scattered", "added"))

        main, wide = GroupSems("", RING), GroupSems("wide_", 1)
        loc_ready, agg_final = sem("loc_ready"), sem("agg_final")

        epi_staged, epi_staged_x, epi_xt_ps, epi_xt_sb, epi_out, epi_res, epi_xf, epi_var, epi_std = map(
            sem, ("epi_staged", "epi_staged_x", "epi_xt_ps", "epi_xt_sb", "epi_out", "epi_res", "epi_xf", "epi_var",
                  "epi_std"))
        epi_ft_ps, epi_ft_sb, epi_logit, epi_done = map(sem, ("epi_ft_ps", "epi_ft_sb", "epi_logit", "epi_done"))
        gap_ready, gap_exp = sem("gap_ready"), sem("gap_exp")
        tot_ready, rank0_ps = sem("tot_ready"), sem("rank0_ps")
        slots_ready, etile_ready = sem("slots_ready"), sem("etile_ready")
        row_staged, slot_staged, rows_sent = sem("row_staged"), sem("slot_staged"), sem("rows_sent")
        ew_loaded, b_loaded = sem("ew_loaded"), sem("b_loaded")
        xs_loaded = [sem("xs_loaded0"), sem("xs_loaded1")]
        xst_ps, xst_sb, h_ps, h_half0, h_half1, ht_ps, ht_ready, y_ps, y_ready, b1_ready = map(
            sem, ("xst_ps", "xst_sb", "h_ps", "h_half0", "h_half1", "ht_ps", "ht_ready", "y_ps", "y_ready", "b1_ready"))
        ys_written = [sem("ys_written0"), sem("ys_written1")]
        slot_staged2, y_taken, y_first, summed, out_written = map(
            sem, ("slot_staged2", "y_taken", "y_first", "summed", "out_written"))

        block = ctx.enter_context(nc.Block())

        def count(eng, value):
            return value if isinstance(value, int) else eng.to_reg(value)

        def past(i):
            return not isinstance(i, int) or i > 0

        def batches(eng, turn):
            turn(0)
            with eng.Fori(1, NB) as b:
                turn(b)

        def group(i, o):
            return not isinstance(i, int) or 0 <= RING * i + o < G

        def steps(eng, step, first, start, turns, last):
            for k in range(first, start):
                step(0, k)
            with eng.Fori(0, turns) as i:
                for r in range(RING):
                    step(i, start + r)
            for k in range(start + RING * turns, last):
                step(0, k)

        def pq_ps(s):
            return ps2[:, 0, s * 512:s * 512 + TG * 128]

        def score_ps(s):
            return ps2[:, 1, s * 512:s * 512 + TG * 96]

        @block.sync
        def _(sp):
            x_rows = x.rearrange("(p j) d -> p j d", j=J)
            for a, b in ((0, 112), (112, P)):
                sp.dma_start(x_sb[a:b, :, :], x_rows[a:b]).then_inc(x_loaded, 16)
            for k, w in enumerate(names):
                sp.dma_start(wsm[:, k, :], t["L0_gnn_" + w]).then_inc(w_loaded, 16)
            sp.wait_ge(raw_padded, 3)
            full = PAIRS - 1
            for raw, dram, c in ((dst_raw[:, :], dst, 1), (src_raw[:, :], src, 1),
                                 (attr_raw[:, :, :].rearrange("p e m -> p (e m)"), attr.rearrange("e m -> (e m)"), 3)):
                w = 2 * GE * c
                rows = dram[0:full * w].rearrange("(p e) -> p e", e=w)
                sp.dma_start(raw[0:64, :], rows[0:64]).then_inc(raw_loaded, 16)
                sp.dma_start(raw[64:full, :], rows[64:full]).then_inc(raw_loaded, 16)
                sp.dma_start(raw[full:PAIRS, 0:LAST * c], dram[full * w:full * w + LAST * c].rearrange("(p e) -> p e", p=1)) \
                    .then_inc(raw_loaded, 16)
            xn_rows = xn_dram.rearrange("(p j) d -> p j d", j=J)
            for b in range(NB):
                sp.wait_ge(xn_ready, b + 1)
                for p0, p1 in ((0, 112), (112, P)):
                    sp.dma_start(xn_rows[p0:p1, b * JB:(b + 1) * JB, :], xn_sb[p0:p1, b * JB:(b + 1) * JB, :]) \
                        .then_inc(xn_written, 16)
            with nc.allow_non_contiguous_dma(reason="256 elements"):
                for col, w in ((kw_col, "kln_weight"), (kb_col, "kln_bias")):
                    sp.dma_start(col[:, :], t["L0_mix_" + w].rearrange("h a c -> (h a c)").rearrange("(c p) -> p c", p=128)) \
                        .then_inc(mixw_loaded, 16)
            for bc, w in ((vw_bc, "vln_weight"), (vb_bc, "vln_bias")):
                sp.dma_start(bc[:, :], t["L0_mix_" + w].rearrange("h a c -> (a h c)").partition_broadcast(128)) \
                    .then_inc(mixw_loaded, 16)
            sp.dma_start(wg_sb[:, :, :], t["L0_ffn_Wg"].rearrange("(c p) e -> p c e", p=128)).then_inc(gate_loaded, 16)
            sp.dma_start(bg_bc[:, :], t["L0_ffn_bg"].partition_broadcast(P)).then_inc(gate_loaded, 16)
            sp.wait_ge(agg_zeroed, 1)
            zcols = SLOTS * D // 128
            sp.dma_start(xs_dram.rearrange("(p s) d -> p (s d)", p=128),
                         agg[:, :, :].rearrange("p s n -> p (s n)")[:, 0:zcols]).then_inc(zeros_written, 16)
            sp.wait_ge(epi_done, NB)
            sp.dma_start(b1_sb[:, :, :], t["L0_ffn_b1"].rearrange("e (p c) -> p e c", p=128)).then_inc(b_loaded, 16)
            sp.dma_start(b2_bc[:, :, :], t["L0_ffn_b2"].partition_broadcast(128)).then_inc(b_loaded, 16)
            for e in range(NE):
                if e:
                    sp.wait_ge(ew_loaded, 32 * e)
                sp.dma_start(w1_sb[:, e, :, :], t["L0_ffn_W1"][e].rearrange("(p c) h -> p c h", p=128)).then_inc(ew_loaded, 16)
                sp.dma_start(w2_sb[:, e, :, :], t["L0_ffn_W2"][e].rearrange("(p c) d -> p c d", p=128)).then_inc(ew_loaded, 16)
            sp.wait_ge(rows_sent, 16 * 2 * J)
            xs_t = xs_dram.rearrange("(k p) d -> p k d", p=128)
            ys_t = ys_dram.rearrange("(k p) d -> p k d", p=128)

            def load(i, o):
                s = o % 2
                if not isinstance(i, int) or o >= 2:
                    sp.wait_ge(xst_ps, 2 * i + o - 1)
                sp.dma_start(xs_sb[:, s, :], xs_t[:, bass.ds(2 * i + o, 1), :].rearrange("p k d -> p (k d)")) \
                    .then_inc(xs_loaded[s], 16)

            def store(i, o):
                s = o % 2
                sp.wait_ge(y_ready, 2 * i + o + 1)
                sp.dma_start(ys_t[:, bass.ds(2 * i + o, 1), :].rearrange("p k d -> p (k d)"), y_sb[:, s, :]) \
                    .then_inc(ys_written[s], 16)

            load(0, 0)
            load(0, 1)
            with sp.Fori(0, TILES // 2 - 1) as i:
                for o in (0, 1):
                    load(i, o + 2)
                    store(i, o)
            for o in (0, 1):
                store(TILES // 2 - 1, o)
            out_rows = out.rearrange("(p j) d -> p j d", j=J)
            for b in range(NB):
                sp.wait_ge(summed, JB * (b + 1))
                for p0, p1 in ((0, 112), (112, P)):
                    sp.dma_start(out_rows[p0:p1, b * JB:(b + 1) * JB, :], x_sb[p0:p1, b * JB:(b + 1) * JB, :]) \
                        .then_inc(out_written, 16)
            sp.wait_ge(out_written, 16 * 2 * NB)

        @block.gpsimd
        def _(pool):
            own = Chain(pool, pool_own)
            for buf, value in ((ident[:, :], 0.0), (ones[:, :], 1.0), (below[:, :], 1.0), (head_block[:, :], 1.0 / N),
                               (pick[:, :, :, :], 0.0), (place[:, :, :, :], 0.0), (place_o0[:, :], 0.0),
                               (d_t[:, M:128], 0.0), (c_t[:, 0:M], 0.0), (w_sc[:, M:96], 0.0)):
                pool.memset(buf, value)
            own(pool.memset(rep[:, :, :], 1.0))

            def pick_where(view, pattern, base, mult, op=ALU.not_equal, fill=1.0):
                return pool.affine_select(out=view, in_=view, compare_op=op, fill=fill, base=base, pattern=pattern,
                                          channel_multiplier=mult)

            pick_where(ident[:, :], [[-1, 128]], 0, 1).then_inc(consts_ready, 1)
            pick_where(below[:, :], [[1, P]], 0, -1, ALU.is_gt, 0.0).then_inc(consts_ready, 1)
            pick_where(place_o0[:, :], [[-1, 128]], -M, 1).then_inc(consts_ready, 1)
            for c, shift in ((0, 128), (1, 0)):
                pick_where(pick[:, c, :, :], [[-3, M], [-1, 3]], shift, 1).then_inc(consts_ready, 1)
            hb = head_block[:, :].rearrange("p (h c) -> p h c", c=HC)
            own(pick_where(hb, [[-HC, 128 // HC], [0, HC]], 0, 1, ALU.is_ge, 0.0))
            pick_where(hb, [[HC, 128 // HC], [0, HC]], HC - 1, -1, ALU.is_ge, 0.0).then_inc(consts_ready, 1)
            for c, shift in ((0, 128), (1, 0)):
                own(pick_where(rep[:, c, :], [[1, 128]], shift, -3, ALU.is_ge, 0.0))
                pick_where(rep[:, c, :], [[-1, 128]], 2 - shift, 3, ALU.is_ge, 0.0).then_inc(consts_ready, 1)
            for buf, n in ((iota_w, WIN), (iota_e, NE), (iota_tile, TILES)):
                pool.iota(buf[:, :], [[1, n]], base=0, channel_multiplier=0,
                          allow_small_or_imprecise_dtypes=True).then_inc(consts_ready, 1)
            pool.memset(agg[:, :, :], 0.0).then_inc(agg_zeroed, 1)

            pool.wait_ge(kv_ready, 2)
            pool.memset(sel[:, :, TG * 5 * WIN:], 0.0).then_inc(sel_padded, 1)

            def gather(i, o):
                if not group(i, o):
                    return
                s = o % RING
                staged, free = count(pool, RING * i + o + 1), count(pool, RING * i + o - RING + 1)
                pool.wait_ge(xn_written, 16 * 2 * NB)
                pool.wait_ge(main.idx, staged)
                if not isinstance(i, int) or o >= RING:
                    pool.wait_ge(main.scattered, free)
                for tt in range(TG):
                    pool.indirect_dma_start(xg[:, s, tt, M:M + D], None, xn_dram,
                                            bass.IndirectOffsetOnAxis(ap=idx_st[:, s, tt:tt + 1], axis=0),
                                            bounds_check=N - 1, oob_is_err=False).then_inc(main.gathered[s], 16)

            steps(pool, gather, 0, RING, (G - RING) // RING, G)

            pool.wait_ge(flag_ready, 1)
            far = pool.value_load(spread_i[0:1, 0:1], min_val=0, max_val=1)
            with pool.If(far > 0):
                with pool.Fori(0, G) as g:
                    staged = count(pool, g + 1)
                    pool.wait_ge(xn_written, 16 * 2 * NB)
                    pool.wait_ge(wide.idx, staged)
                    for tt in range(TG):
                        pool.indirect_dma_start(xg[:, 0, tt, M:M + D], None, xn_dram,
                                                bass.IndirectOffsetOnAxis(ap=idx_st[:, 0, tt:tt + 1], axis=0),
                                                bounds_check=N - 1, oob_is_err=False).then_inc(wide.gathered[0], 16)

            pool.wait_ge(slots_ready, 1)
            pool.wait_ge(zeros_written, 16)

            def send_rows(b):
                rows, staged = count(pool, (b + 1) * JB), count(pool, b + 1)
                pool.wait_ge(zeros_written, 16)
                pool.wait_ge(row_staged, rows)
                pool.wait_ge(slot_staged, staged)
                for jj in range(JB):
                    for k in range(K2):
                        pool.indirect_dma_start(xs_dram, bass.IndirectOffsetOnAxis(ap=slot_st[:, jj, k:k + 1], axis=0),
                                                row_st[:, jj, :], None, bounds_check=SLOTS - 1,
                                                oob_is_err=False).then_inc(rows_sent, 16)

            batches(pool, send_rows)

            for s in (0, 1):
                pool.wait_ge(ys_written[s], 16 * (TILES // 2))

            def take_rows(b):
                taken, staged = count(pool, b * JB), count(pool, b + 1)
                pool.wait_ge(ys_written[0], 16 * (TILES // 2))
                if past(b):
                    pool.wait_ge(summed, taken)
                pool.wait_ge(slot_staged2, staged)
                for jj in range(JB):
                    for k in range(K2):
                        pool.indirect_dma_start(y_st[:, jj, k, :], None, ys_dram,
                                                bass.IndirectOffsetOnAxis(ap=slot_st2[:, jj, k:k + 1], axis=0),
                                                bounds_check=SLOTS - 1, oob_is_err=False).then_inc(y_taken, 16)

            batches(pool, take_rows)

        @block.tensor
        def _(pe):
            W = {n: wsm[:, k, :] for k, n in enumerate(names)}

            pe.wait_ge(w_loaded, 16 * len(names))
            pe.wait_ge(consts_ready, 11)
            pw = ps1[:, 0, :]
            pe.transpose(pw[0:M, 0:M], W["lin_src_w1"], ident[0:M, 0:M])
            pe.transpose(pw[0:M, M:128], W["lin_src_w0"], ident[0:M, 0:M]).then_inc(w_mm, 1)
            pe.wait_ge(w_copied, 1)
            for k, (a, b) in enumerate((("tp1_w11", "tp1_w00"), ("tp1_w10", "tp1_w01"))):
                o = 128 + 128 * k
                pe.matmul(pw[0:M, o:o + M], W[a], lin_t[:, 0:M], start=True, stop=True)
                mm = pe.matmul(pw[0:M, o + M:o + 128], W[b], lin_t[:, M:128], start=True, stop=True)
            mm.then_inc(w_mm, 1)
            pe.wait_ge(w_copied, 2)
            pe.matmul(pw[:, 0:M], tp_t[:, 0, :], W["lin_hidden_w0"], start=True, stop=True)
            pe.matmul(pw[0:M, 128:256], W["lin_hidden_w0"], tp_t[:, 0, :], start=True, stop=True)
            pe.matmul(pw[0:M, 256:384], W["lin_hidden_w1"], tp_t[:, 1, :], start=True, stop=True).then_inc(w_mm, 1)
            pe.wait_ge(w_copied, 3)
            pe.matmul(pw[:, 0:M], ba_t[:, :], W["tp2_w00"], start=True, stop=False)
            pe.matmul(pw[:, 0:M], d_t[:, :], W["tp2_w11"], start=False, stop=True)
            pe.matmul(pw[:, M:128], c_t[:, :], W["tp2_w11"], start=True, stop=True)
            pe.matmul(pw[:, 128:192], ba_t[:, :], W["tp2_w01"], start=True, stop=False)
            pe.matmul(pw[:, 128:192], c_t[:, :], W["tp2_w10"], start=False, stop=True)
            pe.matmul(pw[0:M, 192:256], d_t[:, 0:M], W["tp2_w10"], start=True, stop=True).then_inc(w_mm, 1)
            pe.wait_ge(w_copied, 4)
            pe.matmul(pw[:, 256:320], rep[:, 0, :], w_v[:, :], start=True, stop=True)
            pe.matmul(pw[:, 320:384], rep[:, 1, :], w_v[:, :], start=True, stop=True).then_inc(w_mm, 1)

            pe.wait_ge(edge_rows_ready, 1)
            tables = [(dst_f[:, :, :].rearrange("p h e -> p (h e)"), 1, 0), (loc_f[:, :, :].rearrange("p h e -> p (h e)"), 1, 0),
                      (src_f[:, :], 1, 0)] + [(attr_raw[:, :, :].rearrange("p e m -> p (e m)"), 3, m) for m in range(3)]
            banks = [ps2[:, 0, 0:512], ps2[:, 0, 512:1024], ps2[:, 1, 0:512], ps2[:, 1, 512:1024], ps3[:, 0, :], ps3[:, 1, :]]
            for (tab, stride, m), bank in zip(tables, banks):
                for c in range(NC6):
                    lo = c * 128 * stride + m
                    mm = pe.transpose(bank[:, c * PAIRS:(c + 1) * PAIRS], tab[:, lo:lo + 127 * stride + 1:stride],
                                      ident[0:PAIRS, 0:PAIRS])
                mm.then_inc(edge_cols_ready, 1)
            for h in range(2):
                pe.transpose(ps1[0:1, 1, h * PAIRS:(h + 1) * PAIRS], dlow[:, h:h + 1], ident[0:PAIRS, 0:PAIRS])
            pe.transpose(ps1[0:1, 1, 2 * PAIRS:3 * PAIRS], dspread[:, 0:1], ident[0:PAIRS, 0:PAIRS]).then_inc(spread_col, 1)

            pe.wait_ge(edge_cols_taken, len(tables))
            pe.wait_ge(banks_cleared, 1)
            pe.wait_ge(flag_ready, 1)
            with pe.Fori(0, NB) as b:
                pe.wait_ge(head_ready, b + 1)
                u = hx[:, :, :].rearrange("p h c -> p (h c)").rearrange("p (j d) -> p j d", d=D)
                for jj in range(JB):
                    for c in range(2):
                        uc = u[:, jj, c * 128:(c + 1) * 128]
                        pe.matmul(ps2[:, c, 0:128], uc, uc, start=False, stop=False, skip_group_check=True)
                        pe.matmul(ps2[:, c, 512:513], uc, ones[0:P, 0:1], start=False, stop=False, skip_group_check=True)
                    mm = pe.matmul(ps3[:, 0, 0:D], ones[0:P, :], u[:, jj, :], start=False, stop=False, skip_group_check=True)
                mm.then_inc(head_used, 1)

            def turn_z(i, o):
                if not group(i, o):
                    return
                s = o % RING
                pe.wait_ge(main.dot, RING * i + o + 1)
                if not isinstance(i, int) or o >= 1:
                    pe.wait_ge(main.zt_sb, RING * i + o)
                for tt in range(TG):
                    mm = pe.transpose(ps1[:, 0, tt * 128:(tt + 1) * 128], xg[:, s, tt, 0:128], ident[:, :])
                mm.then_inc(main.zt_ps, 1)

            def hidden(i, o):
                if not group(i, o):
                    return
                s = o % 2
                pe.wait_ge(main.zt_sb, RING * i + o + 1)
                if not isinstance(i, int) or o >= 1:
                    pe.wait_ge(main.hid_sb, RING * i + o)
                pe.matmul(ps1[:, 1, 0:GE], w_hid[:, :], zt[:, s, :], start=True, stop=True).then_inc(main.hid_ps, 1)
                if not isinstance(i, int) or o >= 2:
                    pe.wait_ge(main.o0, RING * i + o - 1)
                    pe.wait_ge(main.q_sb, RING * i + o - 1)
                for tt in range(TG):
                    mm = pe.matmul(pq_ps(s)[:, tt * 128:(tt + 1) * 128], zt[:, s, tt * 128:(tt + 1) * 128], w_z[:, :],
                                   start=True, stop=True)
                mm.then_inc(main.pq, 1)

            def scores(i, o):
                if not group(i, o):
                    return
                s = o % 2
                pe.wait_ge(main.hid_sb, RING * i + o + 1)
                if not isinstance(i, int) or o >= 2:
                    pe.wait_ge(main.exp, RING * i + o - 1)
                for tt in range(TG):
                    mm = pe.matmul(score_ps(s)[:, tt * 96:(tt + 1) * 96], hid_sb[:, s, tt * 128:(tt + 1) * 128],
                                   w_sc[:, :], start=True, stop=True)
                mm.then_inc(main.scores, 1)

            def scatter(i, o):
                if not group(i, o):
                    return
                s, r = o % 2, o % RING
                pe.wait_ge(main.eo, RING * i + o + 1)
                pe.wait_ge(main.sel, RING * i + o + 1)
                if not isinstance(i, int) or o >= 2:
                    pe.wait_ge(main.added, RING * i + o - 1)
                scatter_mm(s, r).then_inc(main.scattered, 1)

            def scatter_mm(s, r):
                for col, lhs0, coef0 in ((0, 256, 2), (96, 0, 0), (192, 128, 3)):
                    for tt in range(TG):
                        lo = (tt * 5 + coef0) * WIN
                        mm = pe.matmul(ps3[:, s, col:col + 96], xg[:, r, tt, lhs0:lhs0 + 128], sel[:, s, lo:lo + 96],
                                       start=(tt == 0), stop=(tt == TG - 1))
                return mm

            pe.wait_ge(kv_ready, 2)
            pe.wait_ge(sel_padded, 1)

            def step(i, k):
                hidden(i, k)
                scores(i, k - 1)
                turn_z(i, k + 1)
                scatter(i, k - 4)

            steps(pe, step, -1, FIRST, TURNS, G + 4)

            far = pe.value_load(spread_i[0:1, 0:1], min_val=0, max_val=1)
            with pe.If(far > 0):
                with pe.Fori(0, G) as g:
                    pe.wait_ge(wide.dot, g + 1)
                    for tt in range(TG):
                        mm = pe.transpose(ps1[:, 0, tt * 128:(tt + 1) * 128], xg[:, 0, tt, 0:128], ident[:, :])
                    mm.then_inc(wide.zt_ps, 1)
                    pe.wait_ge(wide.zt_sb, g + 1)
                    pe.matmul(ps1[:, 1, 0:GE], w_hid[:, :], zt[:, 0, :], start=True, stop=True).then_inc(wide.hid_ps, 1)
                    for tt in range(TG):
                        mm = pe.matmul(pq_ps(0)[:, tt * 128:(tt + 1) * 128], zt[:, 0, tt * 128:(tt + 1) * 128], w_z[:, :],
                                       start=True, stop=True)
                    mm.then_inc(wide.pq, 1)
                    pe.wait_ge(wide.hid_sb, g + 1)
                    for tt in range(TG):
                        mm = pe.matmul(score_ps(0)[:, tt * 96:(tt + 1) * 96], hid_sb[:, 0, tt * 128:(tt + 1) * 128],
                                       w_sc[:, :], start=True, stop=True)
                    mm.then_inc(wide.scores, 1)
                    with pe.Fori(0, NWIN) as w:
                        pe.wait_ge(wide.sel, g * NWIN + w + 1)
                        pe.wait_ge(wide.added, g * NWIN + w + 1)
                        scatter_mm(0, 0).then_inc(wide.scattered, 1)

            def mix_and_gate(b):
                pe.wait_ge(epi_staged_x, b + 1)
                for jj in range(JB):
                    if past(b) or jj:
                        pe.wait_ge(epi_xt_sb, b * JB + jj)
                    for c in range(2):
                        mm = pe.transpose(ps1[:, 0, c * 128:c * 128 + P], xn_st[:, jj, c * 128:(c + 1) * 128], ident[0:P, 0:P])
                    mm.then_inc(epi_xt_ps, 1)
                    if jj == 0:
                        pe.wait_ge(epi_staged, b + 1)
                    pe.wait_ge(epi_xt_sb, b * JB + jj + 1)
                    if past(b) or jj:
                        pe.wait_ge(epi_res, b * JB + jj)
                    o = ps1[0:P, 1, 0:D]
                    pe.matmul(o[:, 0:128], agg_st[:, 1, jj, :], place_o0[:, :], start=True, stop=False, skip_group_check=True)
                    pe.matmul(o[:, 128:256], xt_sb[:, jj, 1, :], kv[:, 1, :], start=False, stop=False, skip_group_check=True)
                    pe.matmul(o[:, 0:128], xt_sb[:, jj, 0, :], kv[:, 0, :], start=False, stop=False, skip_group_check=True)
                    for k, w in ((2, place[:, 0]), (3, place[:, 1]), (4, place[:, 2]), (5, w_vec[:, 1]), (0, w_vec[:, 0])):
                        mm = pe.matmul(o[:, M:D], agg_st[:, k, jj, :], w.rearrange("p v m -> p (v m)"),
                                       start=False, stop=(k == 0), skip_group_check=True)
                    mm.then_inc(epi_out, 1)
                pe.wait_ge(gate_loaded, 32)
                for jj in range(JB):
                    pe.wait_ge(epi_xf, b * JB + jj + 1)
                    if past(b) or jj:
                        pe.wait_ge(epi_ft_sb, b * JB + jj)
                    for c in range(2):
                        mm = pe.transpose(ps2[:, 0, c * 128:c * 128 + P], xf_sb[:, jj, c * 128:(c + 1) * 128], ident[0:P, 0:P])
                    mm.then_inc(epi_ft_ps, 1)
                    pe.wait_ge(epi_ft_sb, b * JB + jj + 1)
                    for c in range(2):
                        mm = pe.matmul(ps3[0:P, 0, jj * NE:(jj + 1) * NE], xt_sb[:, jj, c, :], wg_sb[:, c, :],
                                       start=(c == 0), stop=(c == 1))
                mm.then_inc(epi_logit, 1)

            batches(pe, mix_and_gate)

            pe.wait_ge(tot_ready, 1)
            pe.matmul(ps1[0:P, 0, 0:NE], below[:, :], tot[:, :], start=True, stop=True)
            pe.matmul(ps1[:, 0, 128:128 + NE], ones[0:P, :], tot[:, :], start=True, stop=True).then_inc(rank0_ps, 1)

            pe.wait_ge(etile_ready, 1)

            def tile(i, o):
                return not isinstance(i, int) or 0 <= 2 * i + o < TILES

            def turn_rows(i, o):
                if not tile(i, o):
                    return
                s = o % 2
                pe.wait_ge(xs_loaded[s], 16 * (i + o // 2 + 1))
                if not isinstance(i, int) or o >= 1:
                    pe.wait_ge(xst_sb, 2 * i + o)
                for c in range(2):
                    mm = pe.transpose(ps1[:, 0, c * 128:(c + 1) * 128], xs_sb[:, s, c::2], ident[:, :])
                mm.then_inc(xst_ps, 1)

            def up(i, o):
                if not tile(i, o):
                    return
                s = o % 2
                e = pe.value_load(etile[0:1, bass.ds(2 * i + o, 1)], min_val=0, max_val=NE - 1)
                pe.wait_ge(ew_loaded, 32 * e + 32)
                pe.wait_ge(xst_sb, 2 * i + o + 1)
                for half in range(2):
                    if not isinstance(i, int) or o >= 1:
                        pe.wait_ge((h_half0, h_half1)[half], 2 * i + o)
                    for c in range(2):
                        mm = pe.matmul(ps3[:, half, :], xst[:, s, c, :],
                                       w1_sb[:, bass.ds(e, 1), c, half * 512:(half + 1) * 512].rearrange("p e h -> p (e h)"),
                                       start=(c == 0), stop=(c == 1))
                    mm.then_inc(h_ps, 1)

            def turn_hidden(i, o):
                if not tile(i, o):
                    return
                pe.wait_ge(h_half0, 2 * i + o + 1)
                pe.wait_ge(h_half1, 2 * i + o + 1)
                if not isinstance(i, int) or o >= 1:
                    pe.wait_ge(ht_ready, 2 * i + o)
                for c in range(FC):
                    mm = pe.transpose(ps2[:, 0, c * 128:(c + 1) * 128], h_sb[:, c::FC], ident[:, :])
                mm.then_inc(ht_ps, 1)

            def down(i, o):
                if not tile(i, o):
                    return
                e = pe.value_load(etile[0:1, bass.ds(2 * i + o, 1)], min_val=0, max_val=NE - 1)
                pe.wait_ge(ht_ready, 2 * i + o + 1)
                if not isinstance(i, int) or o >= 1:
                    pe.wait_ge(y_ready, 2 * i + o)
                for c in range(FC):
                    mm = pe.matmul(ps1[:, 1, 0:D], ht_sb[:, c, :], w2_sb[:, bass.ds(e, 1), c, :].rearrange("p e d -> p (e d)"),
                                   start=(c == 0), stop=(c == FC - 1))
                mm.then_inc(y_ps, 1)

            def expert_step(i, o):
                up(i, o)
                turn_rows(i, o + 1)
                down(i, o - 1)
                turn_hidden(i, o)

            for k in (-1, 0, 1, 2):
                expert_step(0, k)
            with pe.Fori(0, (TILES - 4) // 2) as i:
                expert_step(i, 3)
                expert_step(i, 4)
            for k in (TILES - 1, TILES):
                expert_step(0, k)

        @block.scalar
        def _(act):
            own = Chain(act, act_own)

            with act.Fori(0, NB) as b:
                act.wait_ge(ln_var_ready, b + 1)
                act.activation(ln_std[:, :], ln_var[:, :], ACT.Sqrt).then_inc(ln_std_ready, 1)

            pw = ps1[:, 0, :]
            act.wait_ge(w_mm, 1)
            act.activation(lin_t[:, :], pw[0:M, 0:128], ACT.Copy).then_inc(w_copied, 1)
            act.wait_ge(w_mm, 2)
            act.activation(tp_t[:, :, :].rearrange("p a b -> p (a b)"), pw[0:M, 128:384], ACT.Copy,
                           scale=c_tp * c_lin * c_lin).then_inc(w_copied, 1)
            act.wait_ge(w_mm, 3)
            act.activation(w_hid[:, 0:M], pw[:, 0:M], ACT.Copy)
            act.activation(w_hid[:, M:128], pw[:, 0:M], ACT.Copy, scale=-1.0)
            act.activation(ba_t[:, :], pw[0:M, 128:256], ACT.Copy)
            act.activation(d_t[:, 0:M], pw[0:M, 256:320], ACT.Copy)
            act.activation(c_t[:, M:128], pw[0:M, 320:384], ACT.Copy).then_inc(w_copied, 1)
            act.wait_ge(w_mm, 4)
            act.activation(w_z[:, 0:M], pw[:, 0:M], ACT.Copy, scale=c_tp)
            act.activation(w_z[:, M:128], pw[:, M:128], ACT.Copy, scale=c_tp * SQ3)
            act.wait_ge(consts_ready, 11)
            for m in range(3):
                act.activation(place[:, m, :, m], pw[:, 128:192], ACT.Copy, scale=c_tp * SQ3)
            act.activation(w_v[:, :], pw[0:M, 192:256], ACT.Copy, scale=c_tp)
            act.activation(w_sc[0:M, 0:M], wsm[:, len(names) - 1, :], ACT.Copy, scale=c_lin)
            act.activation(w_sc[M:128, 0:M], wsm[:, len(names) - 1, :], ACT.Copy, scale=-0.01 * c_lin).then_inc(w_copied, 1)

            act.wait_ge(edge_sq_ready, 1)
            act.activation(edge_len[:, 1, :], edge_len[:, 0, :], ACT.Sqrt).then_inc(edge_len_ready, 1)

            with act.Fori(0, NB) as b:
                act.wait_ge(head_dev, b + 1)
                act.activation(hsq[:, :, :], hx[:, :, :], ACT.Square).then_inc(head_sq, 1)
                act.wait_ge(head_var, b + 1)
                act.activation(hstat[:, 2, :], hstat[:, 1, :], ACT.Sqrt, scale=1.0 / (HC - 1)).then_inc(head_std, 1)

            def stage_idx(i, o):
                if not group(i, o):
                    return
                s = o % RING
                if not isinstance(i, int) or o >= RING:
                    act.wait_ge(main.gathered[s], 16 * TG * (i + o // RING))
                act.activation(idx_st[:, s, :], edge_src[:, bass.ds(TG * (RING * i + o), TG)], ACT.Copy).then_inc(main.idx, 1)

            def copy_z(i, o):
                if not group(i, o):
                    return
                s = o % 2
                act.wait_ge(main.zt_ps, RING * i + o + 1)
                if not isinstance(i, int) or o >= 2:
                    act.wait_ge(main.pq, RING * i + o - 1)
                act.activation(zt[:, s, :], ps1[:, 0, 0:GE], ACT.Copy).then_inc(main.zt_sb, 1)

            def relu(i, o):
                if not group(i, o):
                    return
                s = o % 2
                act.wait_ge(main.hid_ps, RING * i + o + 1)
                if not isinstance(i, int) or o >= 2:
                    act.wait_ge(main.scores, RING * i + o - 1)
                act.activation(hid_sb[:, s, :], ps1[:, 1, 0:GE], ACT.Relu).then_inc(main.hid_sb, 1)

            def exps(i, o):
                if not group(i, o):
                    return
                s = o % 2
                act.wait_ge(main.neg_top, RING * i + o + 1)
                if not isinstance(i, int) or o >= 2:
                    act.wait_ge(main.eo, RING * i + o - 1)
                    act.wait_ge(main.coef, RING * i + o - 1)
                for tt in range(TG):
                    act.activation(e0[:, s, tt, :], score_ps(s)[:, tt * 96:tt * 96 + M], ACT.Exp,
                                   bias=neg_top[:, s, tt:tt + 1], accum_out=exp_sum[:, s, tt:tt + 1])
                act.activation(exp_neg[:, s, :], neg_top[:, s, :], ACT.Exp).then_inc(main.exp, 1)

            def scale_q(i, o):
                if not group(i, o):
                    return
                g = RING * i + o
                act.wait_ge(main.pq, g + 1)
                if not isinstance(i, int) or o >= 4:
                    act.wait_ge(main.eo, g - 3)
                for tt in range(TG):
                    ins = act.activation(o0[:, o % 4, tt, :], pq_ps(o % 2)[:, tt * 128 + M:(tt + 1) * 128], ACT.Copy,
                                         scale=edge_rr[:, bass.ds(TG * g + tt, 1)])
                ins.then_inc(main.q_sb, 1)

            act.wait_ge(kv_ready, 2)
            for k in range(-1 + AHEAD):
                stage_idx(0, k)

            def step(i, k):
                relu(i, k)
                exps(i, k - 2)
                scale_q(i, k)
                copy_z(i, k + 1)
                stage_idx(i, k + AHEAD)

            steps(act, step, -1, FIRST, TURNS, G + 2)

            act.wait_ge(flag_ready, 1)
            far = act.value_load(spread_i[0:1, 0:1], min_val=0, max_val=1)
            with act.If(far > 0):
                with act.Fori(0, G) as g:
                    act.wait_ge(wide.added, g * NWIN + 1)
                    act.activation(idx_st[:, 0, :], edge_src[:, bass.ds(TG * g, TG)], ACT.Copy).then_inc(wide.idx, 1)
                    act.wait_ge(wide.zt_ps, g + 1)
                    act.activation(zt[:, 0, :], ps1[:, 0, 0:GE], ACT.Copy).then_inc(wide.zt_sb, 1)
                    act.wait_ge(wide.hid_ps, g + 1)
                    act.activation(hid_sb[:, 0, :], ps1[:, 1, 0:GE], ACT.Relu).then_inc(wide.hid_sb, 1)
                    act.wait_ge(wide.pq, g + 1)
                    for tt in range(TG):
                        ins = act.activation(o0[:, 0, tt, :], pq_ps(0)[:, tt * 128 + M:(tt + 1) * 128], ACT.Copy,
                                             scale=edge_rr[:, bass.ds(TG * g + tt, 1)])
                    ins.then_inc(wide.q_sb, 1)
                    act.wait_ge(wide.neg_top, g + 1)
                    for tt in range(TG):
                        act.activation(e0[:, 0, tt, :], score_ps(0)[:, tt * 96:tt * 96 + M], ACT.Exp,
                                       bias=neg_top[:, 0, tt:tt + 1], accum_out=exp_sum[:, 0, tt:tt + 1])
                    act.activation(exp_neg[:, 0, :], neg_top[:, 0, :], ACT.Exp).then_inc(wide.exp, 1)

            act.wait_ge(agg_final, 1)

            def node_tiles(b):
                if past(b):
                    act.wait_ge(epi_xt_ps, b * JB)
                act.activation(xn_st[:, :, :], xn_sb[:, bass.ds(b * JB, JB), :], ACT.Copy).then_inc(epi_staged_x, 1)
                if past(b):
                    act.wait_ge(epi_out, b * JB)
                act.activation(agg_st[:, :, :, :], agg[:, :, 0:N].rearrange("q s (p j) -> q s j p", j=J)[:, :, bass.ds(b * JB, JB), :],
                               ACT.Copy).then_inc(epi_staged, 1)
                for jj in range(JB):
                    act.wait_ge(epi_xt_ps, b * JB + jj + 1)
                    act.activation(xt_sb[:, jj, :, :], ps1[:, 0, 0:256].rearrange("q (c p) -> q c p", p=128)[:, :, 0:P],
                                   ACT.Copy).then_inc(epi_xt_sb, 1)
                act.wait_ge(epi_var, b + 1)
                act.activation(ln_std[:, :], ln_var[:, :], ACT.Sqrt).then_inc(epi_std, 1)
                for jj in range(JB):
                    act.wait_ge(epi_ft_ps, b * JB + jj + 1)
                    act.activation(xt_sb[:, jj, :, :], ps2[:, 0, 0:256].rearrange("q (c p) -> q c p", p=128)[:, :, 0:P],
                                   ACT.Copy).then_inc(epi_ft_sb, 1)

            batches(act, node_tiles)

            act.wait_ge(gap_ready, 1)
            act.activation(gap[:, 1, :], gap[:, 0, :], ACT.Exp).then_inc(gap_exp, 1)

            act.wait_ge(slots_ready, 1)

            def slots_to_send(b):
                if past(b):
                    act.wait_ge(rows_sent, b * 2 * JB * 16)
                act.activation(slot_st[:, :, :], slot_i[:, bass.ds(b * JB, JB), :], ACT.Copy).then_inc(slot_staged, 1)

            batches(act, slots_to_send)

            act.wait_ge(etile_ready, 1)
            act.wait_ge(b_loaded, 32)

            def gelu_pair(i):
                for s in range(2):
                    act.wait_ge(h_ps, 2 * (2 * i + s) + 2)
                    if past(i) or s:
                        act.wait_ge(ht_ps, 2 * i + s)
                    act.activation(h_sb[:, 512:1024], ps3[:, 1, :], ACT.Copy).then_inc(h_half1, 1)
                    act.wait_ge(ht_ps, 2 * i + s + 1)
                    if past(i) or s:
                        act.wait_ge(y_ps, 2 * i + s)
                    act.wait_ge(b1_ready, 2 * i + s + 1)
                    for c in range(FC):
                        ins = act.activation(ht_sb[:, c, :], ps2[:, 0, c * 128:(c + 1) * 128], ACT.Gelu, bias=b1_cur[:, s, c:c + 1])
                    ins.then_inc(ht_ready, 1)

            gelu_pair(0)
            with act.Fori(1, TILES // 2) as i:
                gelu_pair(i)

            act.wait_ge(y_ready, TILES)

            def slots_to_take(b):
                if past(b):
                    act.wait_ge(y_taken, b * 2 * JB * 16)
                act.activation(slot_st2[:, :, :], slot_i[:, bass.ds(b * JB, JB), :], ACT.Copy).then_inc(slot_staged2, 1)

            batches(act, slots_to_take)

        @block.vector
        def _(dve):
            own = Chain(dve, dve_own)

            dve.memset(dst_raw[64:PAIRS, :], int(FAR)).then_inc(raw_padded, 1)
            dve.memset(src_raw[64:PAIRS, :], 0).then_inc(raw_padded, 1)
            dve.memset(attr_raw[64:PAIRS, :, :], 1.0).then_inc(raw_padded, 1)

            dve.wait_ge(x_loaded, 32)
            own.open(3)
            with dve.Fori(0, NB) as b:
                own.enter(b)
                for jj in range(JB):
                    ins = dve.bn_stats(ln_stats[:, jj, :], x_sb[:, bass.ds(b * JB + jj, 1), :].rearrange("p j d -> p (j d)"))
                own(ins)
                dve.memset(ln_var[:, :], 0.0)
                for jj in range(JB):
                    ins = dve.bn_aggr(ln_mv[:, jj, :], ln_stats[:, jj, :])
                own(ins)
                dve.tensor_scalar(ln_var[:, :], ln_mv[:, :, 1], EPS, None, ALU.add).then_inc(ln_var_ready, 1)
                dve.wait_ge(ln_std_ready, b + 1)
                own(dve.reciprocal(ln_rstd[:, :], ln_std[:, :]))
                for jj in range(JB):
                    ins = dve.tensor_scalar(xn_sb[:, bass.ds(b * JB + jj, 1), :].rearrange("p j d -> p (j d)"),
                                            x_sb[:, bass.ds(b * JB + jj, 1), :].rearrange("p j d -> p (j d)"),
                                            ln_mv[:, jj, 0:1], ln_rstd[:, jj:jj + 1], ALU.subtract, ALU.mult)
                ins.then_inc(xn_ready, 1)
                dve.wait_ge(xn_ready, b + 1)
            own.leave(NB)

            dve.wait_ge(raw_loaded, 16 * 9)
            dve.tensor_copy(src_f[:, :], src_raw[:, :])
            own(dve.tensor_copy(dst_f[:, :, :].rearrange("p h e -> p (h e)"), dst_raw[:, :]))
            own(dve.tensor_reduce(dlow[:, :], dst_f[:, :, :], AX.X, ALU.min))
            own(dve.scalar_tensor_tensor(out=loc_f[:, :, :], in0=dst_f[:, :, :], scalar=FAR - 1.0, in1=dst_f[:, :, :],
                                         op0=ALU.is_lt, op1=ALU.mult))
            own(dve.tensor_reduce(dhigh[:, :], loc_f[:, :, :], AX.X, ALU.max))
            own(dve.tensor_tensor(dspread[:, :], dhigh[:, :], dlow[:, :], ALU.subtract))
            own(dve.tensor_tensor(dspread[:, 0:1], dspread[:, 0:1], dspread[:, 1:2], ALU.max))
            for h in range(2):
                ins = dve.tensor_scalar(loc_f[:, h, :], dst_f[:, h, :], dlow[:, h:h + 1], None, ALU.subtract)
            ins.then_inc(edge_rows_ready, 1)
            dve.wait_ge(edge_rows_ready, 1)

            def cols(bank):
                return bank[:, 0:NT].rearrange("p (c j) -> p j c", j=PAIRS)

            def rows(tab):
                return tab.rearrange("p (j c) -> p j c", c=NC6)

            banks = [ps2[:, 0, 0:512], ps2[:, 0, 512:1024], ps2[:, 1, 0:512], ps2[:, 1, 512:1024], ps3[:, 0, :], ps3[:, 1, :]]
            dests = [edge_dst[:, :], edge_loc[:, :], edge_src[:, :]] + [edge_tmp[:, :, m] for m in range(3)]
            for k, (bank, tab) in enumerate(zip(banks, dests)):
                dve.wait_ge(edge_cols_ready, k + 1)
                dve.tensor_copy(rows(tab), cols(bank)).then_inc(edge_cols_taken, 1)
            dve.wait_ge(spread_col, 1)
            for h in range(2):
                ins = dve.tensor_copy(base_i[:, :, h], ps1[0:1, 1, h * PAIRS:(h + 1) * PAIRS])
            ins.then_inc(base_ready, 1)
            own(dve.tensor_reduce(spread_row[:, :], ps1[0:1, 1, 2 * PAIRS:3 * PAIRS], AX.X, ALU.max))
            dve.tensor_scalar(spread_i[:, :], spread_row[:, :], float(WIN), None, ALU.is_ge).then_inc(flag_ready, 1)
            dve.wait_ge(edge_cols_taken, 6)
            own(dve.tensor_tensor(edge_r[:, :, :], edge_tmp[:, :, :], edge_tmp[:, :, :], ALU.mult))
            dve.tensor_reduce(edge_len[:, 0, :], edge_r[:, :, :], AX.X, ALU.add).then_inc(edge_sq_ready, 1)
            dve.wait_ge(edge_len_ready, 1)
            own(dve.tensor_scalar(edge_len[:, 0, :], edge_len[:, 1, :], 1e-12, None, ALU.add))
            own(dve.reciprocal(edge_len[:, 1, :], edge_len[:, 0, :]))
            own(dve.tensor_tensor(edge_r[:, :, :], edge_tmp[:, :, :], edge_len[:, 1, :].unsqueeze(2).to_broadcast([128, NT, 3]),
                                  ALU.mult))
            own(dve.tensor_tensor(edge_tmp[:, :, :], edge_r[:, :, :], edge_r[:, :, :], ALU.mult))
            own(dve.tensor_reduce(edge_rr[:, :], edge_tmp[:, :, :], AX.X, ALU.add))

            dve.wait_ge(consts_ready, 11)
            for c in range(2):
                ins = dve.tensor_reduce(pick_m[:, c, :], pick[:, c, :, :].rearrange("p u m -> p m u"), AX.X, ALU.add)
            own(ins)
            dve.wait_ge(w_mm, 5)
            for c in range(2):
                ins = dve.tensor_tensor(w_vec[:, c, :, :], ps1[:, 0, 256 + c * M:256 + (c + 1) * M].unsqueeze(2).to_broadcast([128, M, 3]),
                                        pick_m[:, c, :].unsqueeze(1).to_broadcast([128, M, 3]), ALU.mult)
            own(ins)
            dve.memset(ps2[:, :, :], 0.0)
            dve.memset(ps3[:, :, :], 0.0).then_inc(banks_cleared, 1)

            own.open(4)

            def head_features(b):
                own.enter(b)
                xh = xn_sb[:, bass.ds(b * JB, JB), :].rearrange("p j (h c) -> p (j h) c", c=HC)
                own(dve.tensor_reduce(hstat[:, 0, :], xh, AX.X, ALU.add))
                own(dve.tensor_scalar(hstat[:, 0, :], hstat[:, 0, :], 1.0 / HC, None, ALU.mult))
                if past(b):
                    dve.wait_ge(head_used, b)
                dve.tensor_tensor(hx[:, :, :], xh, hstat[:, 0, :].unsqueeze(2).to_broadcast([P, JB * H, HC]),
                                  ALU.subtract).then_inc(head_dev, 1)
                dve.wait_ge(head_sq, b + 1)
                dve.tensor_reduce(hstat[:, 1, :], hsq[:, :, :], AX.X, ALU.add).then_inc(head_var, 1)
                dve.wait_ge(head_std, b + 1)
                own(dve.tensor_scalar(hstat[:, 1, :], hstat[:, 2, :], EPS, None, ALU.add))
                own(dve.reciprocal(hstat[:, 0, :], hstat[:, 1, :]))
                dve.tensor_tensor(hx[:, :, :], hx[:, :, :], hstat[:, 0, :].unsqueeze(2).to_broadcast([P, JB * H, HC]),
                                  ALU.mult).then_inc(head_ready, 1)
                dve.wait_ge(head_ready, b + 1)

            batches(dve, head_features)
            own.leave(NB)

            dve.wait_ge(head_used, NB)
            dve.wait_ge(mixw_loaded, 64)
            for c in range(2):
                cs = slice(c * 128, (c + 1) * 128)
                own(dve.tensor_scalar(kv_col[:, 0:1], kb_col[:, c:c + 1], float(N), None, ALU.mult))
                own(dve.scalar_tensor_tensor(out=kv_col[:, 1:2], in0=ps2[:, c, 512:513], scalar=kw_col[:, c:c + 1],
                                             in1=kv_col[:, 0:1], op0=ALU.mult, op1=ALU.add))
                own(dve.scalar_tensor_tensor(out=kv_tmp[:, 0, :], in0=ps2[:, c, 0:128], scalar=kw_col[:, c:c + 1],
                                             in1=vw_bc[:, cs], op0=ALU.mult, op1=ALU.mult))
                own(dve.scalar_tensor_tensor(out=kv_tmp[:, 1, :], in0=vb_bc[:, cs], scalar=kv_col[:, 1:2],
                                             in1=kv_tmp[:, 0, :], op0=ALU.mult, op1=ALU.add))
                own(dve.scalar_tensor_tensor(out=kv_tmp[:, 2, :], in0=ps3[:, 0, cs], scalar=kb_col[:, c:c + 1],
                                             in1=vw_bc[:, cs], op0=ALU.mult, op1=ALU.mult))
                own(dve.tensor_tensor(kv_tmp[:, 0, :], kv_tmp[:, 1, :], kv_tmp[:, 2, :], ALU.add))
                dve.tensor_tensor(kv[:, c, :], kv_tmp[:, 0, :], head_block[:, :], ALU.mult).then_inc(kv_ready, 1)
                dve.wait_ge(kv_ready, c + 1)

            def products(i, o):
                if not group(i, o):
                    return
                s = o % RING
                dve.wait_ge(main.gathered[s], 16 * TG * (i + o // RING + 1))
                if not isinstance(i, int) or o >= 1:
                    dve.wait_ge(main.dot, RING * i + o)
                products_of(s, RING * i + o).then_inc(main.prod, 1)

            def products_of(s, g):
                r = edge_r[:, bass.ds(TG * g, TG), :].unsqueeze(2).to_broadcast([128, TG, M, 3])
                return dve.tensor_tensor(prod[:, :, :, :], xg[:, s, :, 128:320].rearrange("p t (u m) -> p t u m", m=3), r,
                                         ALU.mult)

            def dots(i, o):
                if not group(i, o):
                    return
                dve.wait_ge(main.prod, RING * i + o + 1)
                dve.tensor_reduce(xg[:, o % RING, :, 0:M], prod[:, :, :, :], AX.X, ALU.add).then_inc(main.dot, 1)

            def maxima(i, o):
                if not group(i, o):
                    return
                s = o % 2
                dve.wait_ge(main.scores, RING * i + o + 1)
                if not isinstance(i, int) or o >= 2:
                    dve.wait_ge(main.exp, RING * i + o - 1)
                maxima_of(s).then_inc(main.neg_top, 1)

            def maxima_of(s):
                return dve.tensor_reduce(neg_top[:, s, :], score_ps(s).rearrange("p (t f) -> p t f", f=96)[:, :, 0:M + 1], AX.X,
                                         ALU.max, negate=True)

            def hots(i, o):
                if not group(i, o):
                    return
                if not isinstance(i, int) or o >= 2:
                    dve.wait_ge(main.sel, RING * i + o - 1)
                loc = edge_loc[:, bass.ds(TG * (RING * i + o), TG)].unsqueeze(2).to_broadcast([128, TG, WIN])
                dve.tensor_tensor(hot[:, o % 2, :, :], iota_w[:, :].unsqueeze(1).to_broadcast([128, TG, WIN]), loc,
                                  ALU.is_equal).then_inc(main.hot, 1)

            def out0(i, o):
                if not group(i, o):
                    return
                dve.wait_ge(main.q_sb, RING * i + o + 1)
                out0_of(o % 4, o % 2).then_inc(main.o0, 1)

            def out0_of(q, s):
                return dve.tensor_tensor(o0[:, q, :, :], o0[:, q, :, :],
                                         pq_ps(s).rearrange("p (t f) -> p t f", f=128)[:, :, 0:M], ALU.add)

            def norm_of(s):
                return dve.scalar_tensor_tensor(out=norm[:, :], in0=exp_neg[:, s, :], scalar=float(V), in1=exp_sum[:, s, :],
                                                op0=ALU.mult, op1=ALU.add)

            def norms(i, o):
                if not group(i, o):
                    return
                g = RING * i + o
                dve.wait_ge(main.exp, g + 1)
                if not isinstance(i, int) or o >= 1:
                    dve.wait_ge(main.norm, 3 * g)
                norm_of(o % 2).then_inc(main.norm, 1)

            def inverses(i, o):
                if not group(i, o):
                    return
                dve.wait_ge(main.norm, 3 * (RING * i + o) + 1)
                dve.reciprocal(coef[:, o % 2, :, 4], norm[:, :]).then_inc(main.norm, 1)

            def weights(i, o):
                if not group(i, o):
                    return
                dve.wait_ge(main.norm, 3 * (RING * i + o) + 2)
                dve.tensor_tensor(coef[:, o % 2, :, 3], exp_neg[:, o % 2, :], coef[:, o % 2, :, 4],
                                  ALU.mult).then_inc(main.norm, 1)

            def vector_weights(i, o):
                if not group(i, o):
                    return
                g = RING * i + o
                dve.wait_ge(main.norm, 3 * g + 3)
                vector_weights_of(o % 2, g).then_inc(main.coef, 1)

            def vector_weights_of(s, g):
                return dve.tensor_tensor(coef[:, s, :, 0:3], edge_r[:, bass.ds(TG * g, TG), :],
                                         coef[:, s, :, 3].unsqueeze(2).to_broadcast([128, TG, 3]), ALU.mult)

            def messages(i, o):
                if not group(i, o):
                    return
                dve.wait_ge(main.o0, RING * i + o + 1)
                messages_of(o % RING, o % 2, o % 4).then_inc(main.eo, 1)

            def messages_of(r, s, q):
                return dve.tensor_tensor(xg[:, r, :, M + D:2 * M + D], e0[:, s, :, :], o0[:, q, :, :], ALU.mult)

            def weigh(i, o):
                if not group(i, o):
                    return
                g = RING * i + o
                if not isinstance(i, int) or o >= 2:
                    dve.wait_ge(main.scattered, g - 1)
                dve.wait_ge(main.hot, g + 1)
                dve.wait_ge(main.coef, g + 1)
                weigh_of(o % 2).then_inc(main.sel, 1)

            def weigh_of(s):
                return dve.tensor_tensor(sel[:, s, 0:TG * 5 * WIN].rearrange("p (t k w) -> p t k w", t=TG, k=5),
                                         hot[:, s, :, :].unsqueeze(2).to_broadcast([128, TG, 5, WIN]),
                                         coef[:, s, :, :].unsqueeze(3).to_broadcast([128, TG, 5, WIN]), ALU.mult)

            def add(i, o):
                if not group(i, o):
                    return
                g = RING * i + o
                base = dve.value_load(base_i[0:1, :, :].rearrange("p a b -> p (a b)")[:, bass.ds(g, 1)], min_val=0, max_val=N)
                dve.wait_ge(main.scattered, g + 1)
                if not isinstance(i, int) or o >= 1:
                    dve.wait_ge(main.added, g)
                add_to(agg[:, :, bass.ds(base, WIN)], o % 2).then_inc(main.added, 1)

            def add_to(win, s):
                return dve.tensor_tensor(win, win, ps3[:, s, WIN:7 * WIN].rearrange("p (k w) -> p k w", w=WIN), ALU.add)

            dve.wait_ge(kv_ready, 2)
            dve.wait_ge(base_ready, 1)
            dve.wait_ge(zeros_written, 16)

            def step(i, k):
                products(i, k + 1)
                norms(i, k - 3)
                hots(i, k - 3)
                inverses(i, k - 3)
                dots(i, k + 1)
                weights(i, k - 3)
                out0(i, k - 1)
                vector_weights(i, k - 3)
                messages(i, k - 3)
                weigh(i, k - 3)
                maxima(i, k - 1)
                add(i, k - 5)

            steps(dve, step, -1, FIRST, TURNS, G + 5)
            dve.wait_ge(main.added, G)

            far = dve.value_load(spread_i[0:1, 0:1], min_val=0, max_val=1)
            with dve.If(far > 0):
                dve.memset(agg[:, :, :], 0.0).then_inc(wide.added, 1)
                dve.wait_ge(wide.added, 1)
                with dve.Fori(0, G) as g:
                    dve.wait_ge(wide.gathered[0], 16 * TG * (g + 1))
                    products_of(0, g).then_inc(wide.prod, 1)
                    dve.wait_ge(wide.prod, g + 1)
                    dve.tensor_reduce(xg[:, 0, :, 0:M], prod[:, :, :, :], AX.X, ALU.add).then_inc(wide.dot, 1)
                    dve.wait_ge(wide.q_sb, g + 1)
                    out0_of(0, 0).then_inc(wide.o0, 1)
                    dve.wait_ge(wide.scores, g + 1)
                    maxima_of(0).then_inc(wide.neg_top, 1)
                    dve.wait_ge(wide.exp, g + 1)
                    norm_of(0).then_inc(wide.norm, 1)
                    dve.wait_ge(wide.norm, 3 * g + 1)
                    dve.reciprocal(coef[:, 0, :, 4], norm[:, :]).then_inc(wide.norm, 1)
                    dve.wait_ge(wide.norm, 3 * g + 2)
                    dve.tensor_tensor(coef[:, 0, :, 3], exp_neg[:, 0, :], coef[:, 0, :, 4], ALU.mult).then_inc(wide.norm, 1)
                    dve.wait_ge(wide.norm, 3 * g + 3)
                    vector_weights_of(0, g).then_inc(wide.coef, 1)
                    dve.wait_ge(wide.o0, g + 1)
                    messages_of(0, 0, 0).then_inc(wide.eo, 1)
                    dve.wait_ge(wide.eo, g + 1)
                    dve.wait_ge(wide.coef, g + 1)
                    dve.tensor_scalar(loc_w[:, :], edge_dst[:, bass.ds(TG * g, TG)], 1.0, None, ALU.mult).then_inc(loc_ready, 1)
                    with dve.Fori(0, NWIN) as w:
                        n = g * NWIN + w
                        dve.wait_ge(loc_ready, n + g + 1)
                        dve.tensor_tensor(hot[:, 0, :, :], iota_w[:, :].unsqueeze(1).to_broadcast([128, TG, WIN]),
                                          loc_w[:, :].unsqueeze(2).to_broadcast([128, TG, WIN]), ALU.is_equal).then_inc(wide.hot, 1)
                        dve.wait_ge(wide.hot, n + 1)
                        weigh_of(0).then_inc(wide.sel, 1)
                        dve.tensor_scalar(loc_w[:, :], loc_w[:, :], float(WIN), None, ALU.subtract).then_inc(loc_ready, 1)
                        dve.wait_ge(wide.scattered, n + 1)
                        add_to(agg[:, :, bass.ds(w * WIN, WIN)], 0).then_inc(wide.added, 1)
                dve.wait_ge(wide.added, G * NWIN + 1)
            dve.tensor_scalar(agg[:, :, N:NW], agg[:, :, N:NW], 0.0, None, ALU.mult).then_inc(agg_final, 1)

            own.open(7)

            def sums_and_gate(b):
                own.enter(b)
                xb = x_sb[:, bass.ds(b * JB, JB), :]
                own(dve.scalar_tensor_tensor(out=res[:, :, :], in0=xn_sb[:, bass.ds(b * JB, JB), :], scalar=2.0, in1=xb,
                                             op0=ALU.mult, op1=ALU.add))
                for jj in range(JB):
                    dve.wait_ge(epi_out, b * JB + jj + 1)
                    dve.tensor_tensor(res[:, jj, :], res[:, jj, :], ps1[0:P, 1, 0:D], ALU.add).then_inc(epi_res, 1)
                dve.wait_ge(epi_res, (b + 1) * JB)
                for jj in range(JB):
                    ins = dve.bn_stats(ln_stats[:, jj, :], res[:, jj, :])
                own(ins)
                dve.tensor_scalar(xb, res[:, :, :], 1.0, None, ALU.mult)
                for jj in range(JB):
                    ins = dve.bn_aggr(ln_mv[:, jj, :], ln_stats[:, jj, :])
                own(ins)
                dve.tensor_scalar(ln_var[:, :], ln_mv[:, :, 1], EPS, None, ALU.add).then_inc(epi_var, 1)
                dve.tensor_copy(mean2[:, bass.ds(b * JB, JB)], ln_mv[:, :, 0])
                dve.wait_ge(epi_std, b + 1)
                own(dve.reciprocal(ln_rstd[:, :], ln_std[:, :]))
                for jj in range(JB):
                    dve.tensor_scalar(xf_sb[:, jj, :], res[:, jj, :], ln_mv[:, jj, 0:1], ln_rstd[:, jj:jj + 1],
                                      ALU.subtract, ALU.mult).then_inc(epi_xf, 1)
                dve.wait_ge(epi_logit, b + 1)
                own(dve.tensor_tensor(logit[:, :, :], ps3[0:P, 0, 0:JB * NE].rearrange("p (j e) -> p j e", e=NE),
                                      bg_bc[:, :].unsqueeze(1).to_broadcast([P, JB, NE]), ALU.add))
                dve.tensor_scalar(rstd2[:, bass.ds(b * JB, JB)], ln_rstd[:, :], 1.0, None, ALU.mult)
                for jj in range(JB):
                    ins = dve.max(top8[:, jj, :], logit[:, jj, :])
                own(ins)
                dve.tensor_scalar(top_w[:, bass.ds(b * JB, JB), :], top8[:, :, 0:K2], 1.0, None, ALU.mult)
                for jj in range(JB):
                    ins = dve.max_index(top8_i[:, jj, :], top8[:, jj, :], logit[:, jj, :])
                own(ins)
                dve.tensor_scalar(top_i[:, bass.ds(b * JB, JB), :], top8_i[:, :, 0:K2], 1.0, None, ALU.mult).then_inc(epi_done, 1)
                dve.wait_ge(epi_done, b + 1)

            batches(dve, sums_and_gate)
            own.leave(NB)

            dve.tensor_tensor(gap[:, 0, :], top_w[:, :, 1], top_w[:, :, 0], ALU.subtract).then_inc(gap_ready, 1)
            for k in range(K2):
                ins = dve.tensor_tensor(picked[:, k, :, :], top_i[:, :, k].unsqueeze(2).to_broadcast([P, J, NE]),
                                        iota_e[:, :].unsqueeze(1).to_broadcast([P, J, NE]), ALU.is_equal)
            own(ins)
            own(dve.tensor_tensor(both[:, :, :], picked[:, 0, :, :], picked[:, 1, :, :], ALU.add))
            for e in range(NE):
                ins = dve.tensor_tensor_scan(ranks[:, :, e], ones[0:P, 0:J], both[:, :, e], 0.0, ALU.mult, ALU.add)
            own(ins)
            dve.tensor_copy(tot[:, :], ranks[:, J - 1, :]).then_inc(tot_ready, 1)
            dve.wait_ge(tot_ready, 1)
            own(dve.tensor_tensor(ranks[:, :, :], ranks[:, :, :], both[:, :, :], ALU.subtract))
            dve.wait_ge(rank0_ps, 1)
            own(dve.tensor_scalar(n_tiles_i[:, 0, :], ps1[:, 0, 128:128 + NE], 127.0, None, ALU.add))
            own(dve.tensor_scalar(n_tiles_i[:, 1, :], n_tiles_i[:, 0, :], 7, None, ALU.arith_shift_right))
            own(dve.tensor_copy(n_tiles[:, 0, :], n_tiles_i[:, 1, :]))
            own(dve.tensor_tensor_scan(n_tiles[:, 1, :], ones[:, 0:NE], n_tiles[:, 0, :], 0.0, ALU.mult, ALU.add))
            own(dve.tensor_tensor(n_tiles[:, 2, :], n_tiles[:, 1, :], n_tiles[:, 0, :], ALU.subtract))
            own(dve.scalar_tensor_tensor(out=row0[:, :], in0=n_tiles[0:P, 2, :], scalar=128.0, in1=ps1[0:P, 0, 0:NE],
                                         op0=ALU.mult, op1=ALU.add))
            own(dve.tensor_tensor(ranks[:, :, :], ranks[:, :, :], row0[:, :].unsqueeze(1).to_broadcast([P, J, NE]), ALU.add))
            for k in range(K2):
                own(dve.tensor_tensor(both[:, :, :], ranks[:, :, :], picked[:, k, :, :], ALU.mult))
                own(dve.tensor_reduce(slot_f[:, k, :], both[:, :, :], AX.X, ALU.add))
            dve.tensor_copy(slot_i[:, :, :].rearrange("p j k -> p k j"), slot_f[:, :, :]).then_inc(slots_ready, 1)
            own(dve.tensor_tensor(ended[:, :, :], iota_tile[:, :].unsqueeze(2).to_broadcast([1, TILES, NE]),
                                  n_tiles[0:1, 1, :].unsqueeze(1).to_broadcast([1, TILES, NE]), ALU.is_ge))
            own(dve.tensor_reduce(etile_f[:, :], ended[:, :, :], AX.X, ALU.add))
            dve.tensor_scalar(etile[:, :], etile_f[:, :], float(NE - 1), None, ALU.min).then_inc(etile_ready, 1)
            dve.wait_ge(gap_exp, 1)
            own(dve.tensor_scalar(gap[:, 0, :], gap[:, 1, :], 1.0, None, ALU.add))
            own(dve.reciprocal(top_w[:, :, 0], gap[:, 0, :]))
            own(dve.tensor_tensor(top_w[:, :, 1], gap[:, 1, :], top_w[:, :, 0], ALU.mult))

            def stage_rows(b):
                if past(b):
                    dve.wait_ge(rows_sent, b * 2 * JB * 16)
                for jj in range(JB):
                    j = b * JB + jj
                    dve.tensor_scalar(row_st[:, jj, :], x_sb[:, bass.ds(j, 1), :].rearrange("p j d -> p (j d)"),
                                      mean2[:, bass.ds(j, 1)], rstd2[:, bass.ds(j, 1)], ALU.subtract,
                                      ALU.mult).then_inc(row_staged, 1)

            batches(dve, stage_rows)

            dve.wait_ge(rows_sent, 16 * 2 * J)
            dve.wait_ge(etile_ready, 1)
            dve.wait_ge(b_loaded, 32)

            def rows_t(i, o):
                dve.wait_ge(xst_ps, 2 * i + o + 1)
                if not isinstance(i, int) or o >= 2:
                    dve.wait_ge(h_ps, 2 * (2 * i + o) - 2)
                dve.tensor_copy(xst[:, o % 2, :, :].rearrange("p c s -> p (c s)"), ps1[:, 0, 0:256]).then_inc(xst_sb, 1)

            rows_t(0, 0)

            def first_half(i, o):
                s = o % 2
                k = 2 * i + o
                e = dve.value_load(etile[0:1, bass.ds(k, 1)], min_val=0, max_val=NE - 1)
                if not isinstance(i, int) or o >= 2:
                    dve.wait_ge(ht_ready, k - 1)
                dve.tensor_scalar(b1_cur[:, s, :], b1_sb[:, bass.ds(e, 1), :].rearrange("p e c -> p (e c)"), 1.0, None,
                                  ALU.mult).then_inc(b1_ready, 1)
                dve.wait_ge(h_ps, 2 * k + 1)
                if past(i) or o:
                    dve.wait_ge(ht_ps, k)
                dve.tensor_copy(h_sb[:, 0:512], ps3[:, 0, :]).then_inc(h_half0, 1)

            def finish(i, o):
                s = o % 2
                k = 2 * i + o
                e = dve.value_load(etile[0:1, bass.ds(k, 1)], min_val=0, max_val=NE - 1)
                dve.wait_ge(y_ps, k + 1)
                if not isinstance(i, int) or o >= 2:
                    dve.wait_ge(ys_written[s], 16 * (i + o // 2))
                dve.tensor_tensor(y_sb[:, s, :], ps1[:, 1, 0:D], b2_bc[:, bass.ds(e, 1), :].rearrange("p e d -> p (e d)"),
                                  ALU.add).then_inc(y_ready, 1)

            def expert_step(i, o):
                first_half(i, o)
                rows_t(i, o + 1)
                finish(i, o - 1)

            first_half(0, 0)
            rows_t(0, 1)
            for k in (1, 2):
                expert_step(0, k)
            with dve.Fori(0, (TILES - 4) // 2) as i:
                expert_step(i, 3)
                expert_step(i, 4)
            first_half(0, TILES - 1)
            finish(0, TILES - 2)
            finish(0, TILES - 1)

            with dve.Fori(0, NB) as b:
                dve.wait_ge(y_taken, (b + 1) * 2 * JB * 16)
                for jj in range(JB):
                    j = b * JB + jj
                    xj = x_sb[:, bass.ds(j, 1), :].rearrange("p j d -> p (j d)")
                    w = top_w[:, :, :].rearrange("p j k -> p (j k)")
                    dve.scalar_tensor_tensor(out=xj, in0=y_st[:, jj, 0, :], scalar=w[:, bass.ds(2 * j, 1)], in1=xj,
                                             op0=ALU.mult, op1=ALU.add).then_inc(y_first, 1)
                for jj in range(JB):
                    j = b * JB + jj
                    xj = x_sb[:, bass.ds(j, 1), :].rearrange("p j d -> p (j d)")
                    w = top_w[:, :, :].rearrange("p j k -> p (j k)")
                    dve.wait_ge(y_first, j + 1)
                    dve.scalar_tensor_tensor(out=xj, in0=y_st[:, jj, 1, :], scalar=w[:, bass.ds(2 * j + 1, 1)], in1=xj,
                                             op0=ALU.mult, op1=ALU.add).then_inc(summed, 1)


_INS = ["x", "src", "dst", "edge_attr_3"] + ["L0_gnn_" + n for n in (
    "lin_src_w0", "lin_src_w1", "tp1_w00", "tp1_w11", "tp1_w01", "tp1_w10", "tp2_w00", "tp2_w11", "tp2_w01", "tp2_w10",
    "lin_hidden_w0", "lin_hidden_w1", "lin_scalar_w")] + ["L0_mix_" + n for n in (
    "kln_weight", "kln_bias", "vln_weight", "vln_bias")] + ["L0_ffn_" + n for n in ("Wg", "bg", "W1", "b1", "W2", "b2")]


def kernel(**inputs):
    import numpy as _np
    import concourse.bacc as _bacc
    from concourse import mybir as _mybir
    from concourse.bass_utils import run_bass_kernel_spmd as _run

    nc = _bacc.Bacc("TRN2", target_bir_lowering=False, num_devices=1)
    arrays, args = {}, {}
    for name in _INS:
        a = _np.ascontiguousarray(inputs[name])
        arrays[f"in_{name}"] = a
        args[name] = nc.dram_tensor(f"in_{name}", a.shape, _mybir.dt.from_np(a.dtype), kind="ExternalInput").ap()
    shape = inputs["x"].shape
    out = nc.dram_tensor("out_0", shape, _mybir.dt.float32, kind="ExternalOutput").ap()
    gps_layer_kernel(nc, args, out)
    r = _run(nc, [arrays], core_ids=[0])
    return r.results[0]["out_0"]
```

```python
from contextlib import ExitStack

import concourse.bass as bass
from concourse import mybir

ALU = mybir.AluOpType
ACT = mybir.ActivationFunctionType
AX = mybir.AxisListType
F32 = mybir.dt.float32
I32 = mybir.dt.int32
U32 = mybir.dt.uint32

SQ3 = 3.0 ** 0.5
EPS = 1e-5


class Chain:

    def __init__(self, eng, sem):
        self.eng, self.sem, self.base, self.n = eng, sem, 0, 0

    def __call__(self, ins):
        self.n += 1
        ins.then_inc(self.sem, 1)
        self.eng.wait_ge(self.sem, self.base + self.n)

    def apart(self, ins, met):
        self.n += 1
        ins.then_inc(self.sem, 1)
        value = self.base + self.n
        if not isinstance(value, int):
            value = self.eng.to_reg(value)
        self.eng.wait_ge(*met)
        self.eng.wait_ge(self.sem, value)

    def open(self, per):
        self.first, self.per = self.base + self.n, per

    def enter(self, i):
        self.base, self.n = self.first + i * self.per, 0

    def leave(self, turns):
        assert self.n == self.per, (self.n, self.per)
        self.base, self.n = self.first + turns * self.per, 0


def gps_layer_kernel(nc, t, out, dbg=None):
    x, src, dst, attr = t["x"], t["src"], t["dst"], t["edge_attr_3"]
    N, D = x.shape
    E = src.shape[0]
    M = t["L0_gnn_lin_src_w0"].shape[0]
    V = D - M
    H, _, HC = t["L0_mix_kln_weight"].shape
    NE, _, HID = t["L0_ffn_W1"].shape
    assert D == 256 and M == 64 and NE == 8 and HID == 1024

    P, J, JB = 125, N // 125, 5
    NB = J // JB
    assert P * J == N and NB * JB == J
    TG, WIN = 3, 32
    GE = TG * 128
    G = -(-E // GE)
    PAIRS = -(-G // 2)
    LAST = E - (PAIRS - 1) * 2 * GE
    NC6 = 2 * TG
    NT = PAIRS * NC6
    NW = N + WIN + 3
    NWIN = -(-N // WIN)
    FAR = 4000.0
    assert FAR > N + WIN and 64 < PAIRS <= 128
    RING = 8
    AHEAD = 5
    FIRST = 6
    TURNS = (G - AHEAD - FIRST) // RING
    K2 = 2
    TILES = K2 * N // 128 + NE
    SLOTS = TILES * 128
    FC = HID // 128
    AT_ONCE = 4
    assert TILES % AT_ONCE == 0

    xn_dram = nc.dram_tensor("xn_rows", (N, D), F32, kind="Internal").ap()
    xs_dram = nc.dram_tensor("expert_in_rows", (SLOTS, D), F32, kind="Internal").ap()
    ys_dram = nc.dram_tensor("expert_out_rows", (SLOTS, D), F32, kind="Internal").ap()

    c_tp = (2.0 * M) ** -0.5
    c_lin = float(M) ** -0.5

    names = ["lin_src_w0", "lin_src_w1", "tp1_w00", "tp1_w11", "tp1_w01", "tp1_w10", "tp2_w00", "tp2_w11",
             "tp2_w01", "tp2_w10", "lin_hidden_w0", "lin_hidden_w1", "lin_scalar_w"]

    with ExitStack() as ctx:
        def sb(scope, name, shape, dt=F32):
            return scope.enter_context(nc.sbuf_tensor(name, shape, dt))

        def sem(name):
            return ctx.enter_context(nc.semaphore(name))

        ps1 = ctx.enter_context(nc.psum_tensor("ps1", [128, 2, 512], F32))
        ps2 = ctx.enter_context(nc.psum_tensor("ps2", [128, 2, 1024], F32))
        ps3 = ctx.enter_context(nc.psum_tensor("ps3", [128, 2, 512], F32))

        x_sb = sb(ctx, "x_sb", [P, J, D])
        ident = sb(ctx, "ident", [128, 128])
        ones = sb(ctx, "ones", [128, 128])
        below = sb(ctx, "below", [P, P])
        iota_e = sb(ctx, "iota_e", [P, NE])
        iota_tile = sb(ctx, "iota_tile", [1, TILES])
        wg_sb = sb(ctx, "wg_sb", [128, 2, NE])
        bg_bc = sb(ctx, "bg_bc", [P, NE])
        spread_i = sb(ctx, "spread_i", [1, 1], I32)
        mean2 = sb(ctx, "mean2", [P, J])
        rstd2 = sb(ctx, "rstd2", [P, J])
        top_w = sb(ctx, "top_w", [P, J, K2])
        top_i = sb(ctx, "top_i", [P, J, K2])
        ln_stats = sb(ctx, "ln_stats", [P, J, 6])
        ln_tmp = sb(ctx, "ln_tmp", [P, 5, J])
        ln_mv = sb(ctx, "ln_mv", [P, JB, 2])
        ln_var = sb(ctx, "ln_var", [P, JB])
        ln_std = sb(ctx, "ln_std", [P, JB])
        ln_rstd = sb(ctx, "ln_rstd", [P, JB])

        graph = ExitStack()
        xn_sb = sb(graph, "xn_sb", [P, J, D])
        early = ExitStack()
        dev = sb(early, "dev", [P, J, D])
        early.close()
        agg = sb(graph, "agg", [128, 6, NW])
        zero = sb(graph, "zero", [128, D])
        edge_dst = sb(graph, "edge_dst", [128, NT])
        edge_loc = sb(graph, "edge_loc", [128, NT])
        edge_src = sb(graph, "edge_src", [128, NT], I32)
        edge_r = sb(graph, "edge_r", [128, NT, 3])
        edge_rr = sb(graph, "edge_rr", [128, NT])
        base_i = sb(graph, "base_i", [1, PAIRS, 2], I32)
        iota_w = sb(graph, "iota_w", [128, WIN])
        w_hid = sb(graph, "w_hid", [128, 128])
        w_z = sb(graph, "w_z", [128, 128])
        w_sc = sb(graph, "w_sc", [128, 96])
        place = sb(graph, "place", [128, 3, M, 3])
        place_o0 = sb(graph, "place_o0", [128, 128])
        w_vec = sb(graph, "w_vec", [128, 2, M, 3])
        kv = sb(graph, "kv", [128, 2, 128])

        edges = ExitStack()
        dst_raw = sb(edges, "dst_raw", [PAIRS, 2 * GE], I32)
        src_raw = sb(edges, "src_raw", [PAIRS, 2 * GE], I32)
        attr_raw = sb(edges, "attr_raw", [PAIRS, 2 * GE, 3])
        dst_f = sb(edges, "dst_f", [PAIRS, 2, GE])
        src_f = sb(edges, "src_f", [PAIRS, 2 * GE])
        loc_f = sb(edges, "loc_f", [PAIRS, 2, GE])
        edge_tmp = sb(edges, "edge_tmp", [128, NT, 3])
        edge_len = sb(edges, "edge_len", [128, 3, NT])
        dlow = sb(edges, "dlow", [PAIRS, 2])
        dhigh = sb(edges, "dhigh", [PAIRS, 2])
        dspread = sb(edges, "dspread", [PAIRS, 2])
        spread_row = sb(edges, "spread_row", [1, 1])
        edges.close()
        ring = ExitStack()
        xg = sb(ring, "xg", [128, RING, TG, 2 * M + D])

        idx_st = sb(ring, "idx_st", [128, RING, TG], I32)

        pre = ExitStack()
        compose = ExitStack()
        wsm = sb(compose, "wsm", [M, len(names), M])
        lin_t = sb(compose, "lin_t", [M, 128])
        tp_t = sb(compose, "tp_t", [M, 2, 128])
        ba_t = sb(compose, "ba_t", [M, 128])
        d_t = sb(compose, "d_t", [M, 128])
        c_t = sb(compose, "c_t", [M, 128])
        w_v = sb(compose, "w_v", [M, M])
        rep = sb(compose, "rep", [M, 2, 128])
        compose.close()
        sq = sb(pre, "sq", [P, JB * H, HC])
        kv_tmp = sb(pre, "kv_tmp", [128, 3, 128])
        sum_diag = sb(pre, "sum_diag", [128, 2, 128])
        pick = sb(pre, "pick", [128, 2, M, 3])
        pick_m = sb(pre, "pick_m", [128, 2, 3])
        kw_col = sb(pre, "kw_col", [128, 2])
        kb_col = sb(pre, "kb_col", [128, 2])
        vw_bc = sb(pre, "vw_bc", [128, D])
        vb_bc = sb(pre, "vb_bc", [128, D])
        kv_col = sb(pre, "kv_col", [128, 2])
        head_block = sb(pre, "head_block", [128, 128])
        hstat = sb(pre, "hstat", [P, 3, J * H])
        hx = sb(pre, "hx", [P, JB, 2, 129])
        pre.close()

        loop = ExitStack()
        prod = sb(loop, "prod", [128, TG, M, 3])
        zt = sb(loop, "zt", [128, 2, GE])
        hid_sb = sb(loop, "hid_sb", [128, 2, GE])
        e0 = sb(loop, "e0", [128, 2, TG, M])
        o0 = sb(loop, "o0", [128, 4, TG, M])
        neg_top = sb(loop, "neg_top", [128, 2, TG])
        exp_sum = sb(loop, "exp_sum", [128, 2, TG])
        exp_neg = sb(loop, "exp_neg", [128, 2, TG])
        norm = sb(loop, "norm", [128, TG])
        coef = sb(loop, "coef", [128, 2, TG, 5])
        hot = sb(loop, "hot", [128, 2, TG, WIN])
        sel = sb(loop, "sel", [128, 2, (TG * 5 + 1) * WIN])
        loc_w = sb(loop, "loc_w", [128, TG])
        loop.close()

        ring.close()

        epi = ExitStack()
        agg_st = sb(epi, "agg_st", [128, JB, 6, P])
        xn_st = sb(epi, "xn_st", [P, JB, D])
        xt_sb = sb(epi, "xt_sb", [128, 2, 2, P])
        ft_sb = sb(epi, "ft_sb", [128, 2, 2, P])
        xf_sb = sb(epi, "xf_sb", [P, JB, D])
        wg_pad = sb(epi, "wg_pad", [128, 2, 96])
        logit = sb(epi, "logit", [P, JB, NE])
        top8 = sb(epi, "top8", [P, JB, 8])
        top8_i = sb(epi, "top8_i", [P, JB, 8], U32)
        epi.close()
        graph.close()

        w1_sb = sb(ctx, "w1_sb", [128, NE, 2, HID])
        w2_sb = sb(ctx, "w2_sb", [128, NE, FC, D])
        b1_sb = sb(ctx, "b1_sb", [128, NE, FC])
        b2_bc = sb(ctx, "b2_bc", [128, NE, D])
        picked = sb(ctx, "picked", [P, 2, J, NE])
        ranks = sb(ctx, "ranks", [P, J, NE])
        both = sb(ctx, "both", [P, J, NE])
        tot = sb(ctx, "tot", [P, NE])
        n_tiles = sb(ctx, "n_tiles", [128, 4, NE])
        n_tiles_i = sb(ctx, "n_tiles_i", [128, 2, NE], I32)
        row0 = sb(ctx, "row0", [P, NE])
        slot_f = sb(ctx, "slot_f", [P, 2, J])
        slot_i = sb(ctx, "slot_i", [P, J, 2], I32)
        gap = sb(ctx, "gap", [P, 2, J])
        ended = sb(ctx, "ended", [1, TILES, NE])
        etile_f = sb(ctx, "etile_f", [1, TILES])
        etile = sb(ctx, "etile", [1, TILES], I32)
        ffn = ExitStack()
        xs_sb = sb(ffn, "xs_sb", [128, AT_ONCE, D])
        xst = sb(ffn, "xst", [128, 2, 2, 128])
        w1_st = sb(ffn, "w1_st", [128, 2, 2, FC, 128])
        ht_sb = sb(ffn, "ht_sb", [128, 2, FC, 128])
        b1_cur = sb(ffn, "b1_cur", [128, 2, FC])
        y_sb = sb(ffn, "y_sb", [128, 2, D])
        ffn.close()
        send = ExitStack()
        slot_st = sb(send, "slot_st", [P, JB, 2], I32)
        row_st = sb(send, "row_st", [P, JB, D])
        send.close()
        take = ExitStack()
        slot_st2 = sb(take, "slot_st2", [P, JB, 2], I32)
        y_st = sb(take, "y_st", [P, JB, 2, D])
        take.close()

        x_loaded = [sem(f"x_loaded{b}") for b in range(NB)]
        raw_padded, raw_loaded, w_loaded = map(sem, ("raw_padded", "raw_loaded", "w_loaded"))
        attr_padded, edges_ready = sem("attr_padded"), sem("edges_ready")
        mixw_loaded, gate_loaded = sem("mixw_loaded"), sem("gate_loaded")
        consts_ready, pool_own = sem("consts_ready"), sem("pool_own")
        zero_ready, agg_zeroed, zeros_written = sem("zero_ready"), sem("agg_zeroed"), sem("zeros_written")
        dve_own, act_own = sem("dve_own"), sem("act_own")
        ln_stats_ready, ln_var_ready, ln_std_ready = sem("ln_stats_ready"), sem("ln_var_ready"), sem("ln_std_ready")
        xn_ready, xn_written = sem("xn_ready"), sem("xn_written")
        edge_rows_ready, edge_cols_ready, edge_cols_taken = map(sem, ("edge_rows_ready", "edge_cols_ready", "edge_cols_taken"))
        spread_col = sem("spread_col")
        edge_sq_ready, edge_len_ready = sem("edge_sq_ready"), sem("edge_len_ready")
        base_ready, flag_ready = sem("base_ready"), sem("flag_ready")
        w_mm, w_copied = sem("w_mm"), sem("w_copied")
        banks_cleared = sem("banks_cleared")
        head_dev, head_sq, head_var, head_std, sums_ready, rows_ready = map(
            sem, ("head_dev", "head_sq", "head_var", "head_std", "sums_ready", "rows_ready"))
        PARTS = ((0, 3), (3, JB))
        head_ready, head_used = ([sem(f"{n}{k}") for k in (0, 1)] for n in ("head_ready", "head_used"))
        kv_ready, sel_padded = sem("kv_ready"), sem("sel_padded")

        class GroupSems:

            def __init__(s, tag, ring):
                s.ring = ring
                s.gathered = [sem(f"{tag}gathered{i}") for i in range(ring)]
                (s.idx, s.prod, s.dot, s.zt_ps, s.zt_sb, s.hid_ps, s.hid_sb, s.pq, s.scores, s.neg_top, s.exp,
                 s.q_sb, s.o0, s.hot, s.norm, s.coef, s.eo, s.sel, s.scattered, s.added) = (
                    sem(tag + n) for n in ("idx", "prod", "dot", "zt_ps", "zt_sb", "hid_ps", "hid_sb", "pq", "scores",
                                           "neg_top", "exp", "q_sb", "o0", "hot", "norm", "coef", "eo", "sel",
                                           "scattered", "added"))

        main, wide = GroupSems("", RING), GroupSems("wide_", 1)
        loc_ready, agg_final = sem("loc_ready"), sem("agg_final")

        epi_staged, epi_xt_ps, epi_xt_sb, epi_out, epi_res, epi_xf, epi_var, epi_std = map(
            sem, ("epi_staged", "epi_xt_ps", "epi_xt_sb", "epi_out", "epi_res", "epi_xf", "epi_var", "epi_std"))
        wg_padded = sem("wg_padded")
        epi_ft_ps, epi_ft_sb, epi_logit, epi_done = map(sem, ("epi_ft_ps", "epi_ft_sb", "epi_logit", "epi_done"))
        gap_ready, gap_exp = sem("gap_ready"), sem("gap_exp")
        tot_ready, rank0_ps = sem("tot_ready"), sem("rank0_ps")
        slots_ready, etile_ready = sem("slots_ready"), sem("etile_ready")
        row_staged, slot_staged, rows_sent = ([sem(f"{n}{k}") for k in (0, 1)]
                                              for n in ("row_staged", "slot_staged", "rows_sent"))
        ew_loaded, b_loaded = sem("ew_loaded"), sem("b_loaded")
        xs_loaded = [sem(f"xs_loaded{k}") for k in range(AT_ONCE)]
        xst_ps, xst_sb, w1_half0, w1_half1, h_ps, ht_ready, y_ps, y_ready, b1_ready = map(
            sem, ("xst_ps", "xst_sb", "w1_half0", "w1_half1", "h_ps", "ht_ready", "y_ps", "y_ready", "b1_ready"))
        ys_written = [sem("ys_written0"), sem("ys_written1")]
        y_first, summed, out_written = map(sem, ("y_first", "summed", "out_written"))
        slot_staged2, y_taken = ([sem(f"{n}{k}") for k in (0, 1)] for n in ("slot_staged2", "y_taken"))

        block = ctx.enter_context(nc.Block())

        def count(eng, value):
            return value if isinstance(value, int) else eng.to_reg(value)

        def past(i):
            return not isinstance(i, int) or i > 0

        def batches(eng, turn):
            turn(0)
            with eng.Fori(1, NB) as b:
                turn(b)

        def group(i, o):
            return not isinstance(i, int) or 0 <= RING * i + o < G

        def steps(eng, step, first, start, turns, last):
            for k in range(first, start):
                step(0, k)
            with eng.Fori(0, turns) as i:
                for r in range(RING):
                    step(i, start + r)
            for k in range(start + RING * turns, last):
                step(0, k)

        def h_of(c):
            return ps3[:, c * 2 // FC, c % (FC // 2) * 128:(c % (FC // 2) + 1) * 128]

        def w1_columns(e, kc):
            return w1_sb[:, bass.ds(e, 1), kc, :].rearrange("p e (q c) -> p (e c) q", c=FC)

        out_ps = ps2[0:P, :, :].rearrange("p a b -> p (a b)")[:, 0:JB * D].rearrange("p (j d) -> p j d", d=D)

        def ft_ps(s):
            return (ps2[:, 1, 512:1024], ps3[:, 1, :])[s]

        agg_flat = agg[:, :, :].rearrange("p s n -> p (s n)")

        def pq_ps(s):
            return ps2[:, 0, s * 512:s * 512 + TG * 128]

        def score_ps(s):
            return ps2[:, 1, s * 512:s * 512 + TG * 96]

        @block.sync
        def _(sp):
            x_rows = x.rearrange("(p j) d -> p j d", j=J)
            for b in range(NB):
                for p0, p1 in ((0, 112), (112, P)):
                    sp.dma_start(x_sb[p0:p1, b * JB:(b + 1) * JB, :], x_rows[p0:p1, b * JB:(b + 1) * JB, :]).then_inc(x_loaded[b], 16)
            for k, w in enumerate(names):
                sp.dma_start(wsm[:, k, :], t["L0_gnn_" + w]).then_inc(w_loaded, 16)
            sp.wait_ge(raw_padded, 2)
            sp.wait_ge(attr_padded, 1)
            full = PAIRS - 1
            for raw, dram, c in ((dst_raw[:, :], dst, 1), (src_raw[:, :], src, 1),
                                 (attr_raw[:, :, :].rearrange("p e m -> p (e m)"), attr.rearrange("e m -> (e m)"), 3)):
                w = 2 * GE * c
                rows = dram[0:full * w].rearrange("(p e) -> p e", e=w)
                sp.dma_start(raw[0:64, :], rows[0:64]).then_inc(raw_loaded, 16)
                sp.dma_start(raw[64:full, :], rows[64:full]).then_inc(raw_loaded, 16)
                sp.dma_start(raw[full:PAIRS, 0:LAST * c], dram[full * w:full * w + LAST * c].rearrange("(p e) -> p e", p=1)) \
                    .then_inc(raw_loaded, 16)
            xn_rows = xn_dram.rearrange("(p j) d -> p j d", j=J)
            for b in range(NB):
                sp.wait_ge(xn_ready, b + 1)
                for p0, p1 in ((0, 112), (112, P)):
                    sp.dma_start(xn_rows[p0:p1, b * JB:(b + 1) * JB, :], xn_sb[p0:p1, b * JB:(b + 1) * JB, :]) \
                        .then_inc(xn_written, 16)
            with nc.allow_non_contiguous_dma(reason="256 elements"):
                for col, w in ((kw_col, "kln_weight"), (kb_col, "kln_bias")):
                    sp.dma_start(col[:, :], t["L0_mix_" + w].rearrange("h a c -> (h a c)").rearrange("(c p) -> p c", p=128)) \
                        .then_inc(mixw_loaded, 16)
            for bc, w in ((vw_bc, "vln_weight"), (vb_bc, "vln_bias")):
                sp.dma_start(bc[:, :], t["L0_mix_" + w].rearrange("h a c -> (a h c)").partition_broadcast(128)) \
                    .then_inc(mixw_loaded, 16)
            sp.dma_start(wg_sb[:, :, :], t["L0_ffn_Wg"].rearrange("(c p) e -> p c e", p=128)).then_inc(gate_loaded, 16)
            sp.dma_start(bg_bc[:, :], t["L0_ffn_bg"].partition_broadcast(P)).then_inc(gate_loaded, 16)
            sp.wait_ge(zero_ready, 1)
            sp.dma_start(xs_dram.rearrange("(p s) d -> p (s d)", p=128).rearrange("p (k z) -> p k z", z=D),
                         zero[:, :].unsqueeze(1).to_broadcast([128, SLOTS // 128, D])).then_inc(zeros_written, 16)
            sp.wait_ge(epi_done, NB)
            sp.dma_start(b1_sb[:, :, :], t["L0_ffn_b1"].rearrange("e (p c) -> p e c", p=128)).then_inc(b_loaded, 16)
            sp.dma_start(b2_bc[:, :, :], t["L0_ffn_b2"].partition_broadcast(128)).then_inc(b_loaded, 16)
            for e in range(NE):
                if e:
                    sp.wait_ge(ew_loaded, 32 * e)
                sp.dma_start(w1_sb[:, e, :, :], t["L0_ffn_W1"][e].rearrange("(p c) h -> p c h", p=128)).then_inc(ew_loaded, 16)
                sp.dma_start(w2_sb[:, e, :, :], t["L0_ffn_W2"][e].rearrange("(p c) d -> p c d", p=128)).then_inc(ew_loaded, 16)
            for k, (j0, j1) in enumerate(PARTS):
                sp.wait_ge(rows_sent[k], 16 * K2 * (j1 - j0) * NB)
            xs_t = xs_dram.rearrange("(k p) d -> p k d", p=128)
            ys_t = ys_dram.rearrange("(k p) d -> p k d", p=128)

            def load(i, o):
                s = o % AT_ONCE
                if past(i) or o >= AT_ONCE:
                    sp.wait_ge(xst_ps, AT_ONCE * i + o - AT_ONCE + 1)
                sp.dma_start(xs_sb[:, s, :], xs_t[:, bass.ds(AT_ONCE * i + o, 1), :].rearrange("p k d -> p (k d)")) \
                    .then_inc(xs_loaded[s], 16)

            def store(i, o):
                s = o % 2
                sp.wait_ge(y_ready, AT_ONCE * i + o + 1)
                sp.dma_start(ys_t[:, bass.ds(AT_ONCE * i + o, 1), :].rearrange("p k d -> p (k d)"), y_sb[:, s, :]) \
                    .then_inc(ys_written[s], 16)

            for o in range(AT_ONCE):
                load(0, o)
            with sp.Fori(0, TILES // AT_ONCE - 1) as i:
                for o in range(AT_ONCE):
                    load(i, o + AT_ONCE)
                    store(i, o)
            for o in range(AT_ONCE):
                store(TILES // AT_ONCE - 1, o)
            out_rows = out.rearrange("(p j) d -> p j d", j=J)
            for b in range(NB):
                sp.wait_ge(summed, JB * (b + 1))
                for p0, p1 in ((0, 112), (112, P)):
                    sp.dma_start(out_rows[p0:p1, b * JB:(b + 1) * JB, :], x_sb[p0:p1, b * JB:(b + 1) * JB, :]) \
                        .then_inc(out_written, 16)
            sp.wait_ge(out_written, 16 * 2 * NB)

        @block.gpsimd
        def _(pool):
            own = Chain(pool, pool_own)
            pool.memset(attr_raw[64:PAIRS, :, :], 1.0).then_inc(attr_padded, 1)
            pool.wait_ge(attr_padded, 1)
            for buf, value in ((ident[:, :], 0.0), (ones[:, :], 1.0), (below[:, :], 1.0), (head_block[:, :], 1.0 / N),
                               (pick[:, :, :, :], 0.0), (place[:, :, :, :], 0.0), (place_o0[:, :], 0.0),
                               (d_t[:, M:128], 0.0), (c_t[:, 0:M], 0.0), (w_sc[:, M:96], 0.0),
                               (hx[:, :, :, 128:129], 1.0)):
                pool.memset(buf, value)
            own(pool.memset(rep[:, :, :], 1.0))

            def pick_where(view, pattern, base, mult, op=ALU.not_equal, fill=1.0):
                return pool.affine_select(out=view, in_=view, compare_op=op, fill=fill, base=base, pattern=pattern,
                                          channel_multiplier=mult)

            pick_where(ident[:, :], [[-1, 128]], 0, 1).then_inc(consts_ready, 1)
            pick_where(below[:, :], [[1, P]], 0, -1, ALU.is_gt, 0.0).then_inc(consts_ready, 1)
            pick_where(place_o0[:, :], [[-1, 128]], -M, 1).then_inc(consts_ready, 1)
            for c, shift in ((0, 128), (1, 0)):
                pick_where(pick[:, c, :, :], [[-3, M], [-1, 3]], shift, 1).then_inc(consts_ready, 1)
            hb = head_block[:, :].rearrange("p (h c) -> p h c", c=HC)
            own(pick_where(hb, [[-HC, 128 // HC], [0, HC]], 0, 1, ALU.is_ge, 0.0))
            pick_where(hb, [[HC, 128 // HC], [0, HC]], HC - 1, -1, ALU.is_ge, 0.0).then_inc(consts_ready, 1)
            for c, shift in ((0, 128), (1, 0)):
                own(pick_where(rep[:, c, :], [[1, 128]], shift, -3, ALU.is_ge, 0.0))
                pick_where(rep[:, c, :], [[-1, 128]], 2 - shift, 3, ALU.is_ge, 0.0).then_inc(consts_ready, 1)
            for buf, n in ((iota_w, WIN), (iota_e, NE), (iota_tile, TILES)):
                pool.iota(buf[:, :], [[1, n]], base=0, channel_multiplier=0,
                          allow_small_or_imprecise_dtypes=True).then_inc(consts_ready, 1)
            pool.memset(zero[:, :], 0.0).then_inc(zero_ready, 1)
            pool.memset(agg_flat[:, J * D:], 0.0).then_inc(agg_zeroed, 1)

            def gather(i, o):
                if not group(i, o):
                    return
                s = o % RING
                staged, free = count(pool, RING * i + o + 1), count(pool, RING * i + o - RING + 1)
                pool.wait_ge(xn_written, 16 * 2 * NB)
                pool.wait_ge(main.idx, staged)
                if not isinstance(i, int) or o >= RING:
                    pool.wait_ge(main.scattered, free)
                for tt in range(TG):
                    pool.indirect_dma_start(xg[:, s, tt, M:M + D], None, xn_dram,
                                            bass.IndirectOffsetOnAxis(ap=idx_st[:, s, tt:tt + 1], axis=0),
                                            bounds_check=N - 1, oob_is_err=False).then_inc(main.gathered[s], 16)

            steps(pool, gather, 0, RING, (G - RING) // RING, G)

            pool.wait_ge(flag_ready, 1)
            far = pool.value_load(spread_i[0:1, 0:1], min_val=0, max_val=1)
            with pool.If(far > 0):
                with pool.Fori(0, G) as g:
                    staged = count(pool, g + 1)
                    pool.wait_ge(xn_written, 16 * 2 * NB)
                    pool.wait_ge(wide.idx, staged)
                    for tt in range(TG):
                        pool.indirect_dma_start(xg[:, 0, tt, M:M + D], None, xn_dram,
                                                bass.IndirectOffsetOnAxis(ap=idx_st[:, 0, tt:tt + 1], axis=0),
                                                bounds_check=N - 1, oob_is_err=False).then_inc(wide.gathered[0], 16)

            pool.wait_ge(slots_ready, 1)
            pool.wait_ge(zeros_written, 16)

            def send_rows(b):
                for k, (j0, j1) in enumerate(PARTS):
                    staged, rows = count(pool, b + 1), count(pool, (b + 1) * (j1 - j0))
                    pool.wait_ge(zeros_written, 16)
                    pool.wait_ge(slot_staged[k], staged)
                    pool.wait_ge(row_staged[k], rows)
                    for jj in range(j0, j1):
                        for c in range(K2):
                            pool.indirect_dma_start(xs_dram, bass.IndirectOffsetOnAxis(ap=slot_st[:, jj, c:c + 1], axis=0),
                                                    row_st[:, jj, :], None, bounds_check=SLOTS - 1,
                                                    oob_is_err=False).then_inc(rows_sent[k], 16)

            batches(pool, send_rows)

            for s in (0, 1):
                pool.wait_ge(ys_written[s], 16 * (TILES // 2))

            def take_rows(b):
                for k, (j0, j1) in enumerate(PARTS):
                    staged, free = count(pool, b + 1), count(pool, b * JB - (JB - j1)) if past(b) else 0
                    pool.wait_ge(ys_written[0], 16 * (TILES // 2))
                    pool.wait_ge(slot_staged2[k], staged)
                    if past(b):
                        pool.wait_ge(summed, free)
                    for jj in range(j0, j1):
                        for c in range(K2):
                            pool.indirect_dma_start(y_st[:, jj, c, :], None, ys_dram,
                                                    bass.IndirectOffsetOnAxis(ap=slot_st2[:, jj, c:c + 1], axis=0),
                                                    bounds_check=SLOTS - 1, oob_is_err=False).then_inc(y_taken[k], 16)

            batches(pool, take_rows)

        @block.tensor
        def _(pe):
            W = {n: wsm[:, k, :] for k, n in enumerate(names)}

            pe.wait_ge(w_loaded, 16 * len(names))
            pe.wait_ge(consts_ready, 11)
            pw = ps1[:, 0, :]
            pe.transpose(pw[0:M, 0:M], W["lin_src_w1"], ident[0:M, 0:M])
            pe.transpose(pw[0:M, M:128], W["lin_src_w0"], ident[0:M, 0:M]).then_inc(w_mm, 1)
            pe.wait_ge(w_copied, 1)
            for k, (a, b) in enumerate((("tp1_w11", "tp1_w00"), ("tp1_w10", "tp1_w01"))):
                o = 128 + 128 * k
                pe.matmul(pw[0:M, o:o + M], W[a], lin_t[:, 0:M], start=True, stop=True)
                mm = pe.matmul(pw[0:M, o + M:o + 128], W[b], lin_t[:, M:128], start=True, stop=True)
            mm.then_inc(w_mm, 1)
            pe.wait_ge(w_copied, 2)
            pe.matmul(pw[:, 0:M], tp_t[:, 0, :], W["lin_hidden_w0"], start=True, stop=True)
            pe.matmul(pw[0:M, 128:256], W["lin_hidden_w0"], tp_t[:, 0, :], start=True, stop=True)
            pe.matmul(pw[0:M, 256:384], W["lin_hidden_w1"], tp_t[:, 1, :], start=True, stop=True).then_inc(w_mm, 1)
            pe.wait_ge(w_copied, 3)
            pe.matmul(pw[:, 0:M], ba_t[:, :], W["tp2_w00"], start=True, stop=False)
            pe.matmul(pw[:, 0:M], d_t[:, :], W["tp2_w11"], start=False, stop=True)
            pe.matmul(pw[:, M:128], c_t[:, :], W["tp2_w11"], start=True, stop=True)
            pe.matmul(pw[:, 128:192], ba_t[:, :], W["tp2_w01"], start=True, stop=False)
            pe.matmul(pw[:, 128:192], c_t[:, :], W["tp2_w10"], start=False, stop=True)
            pe.matmul(pw[0:M, 192:256], d_t[:, 0:M], W["tp2_w10"], start=True, stop=True).then_inc(w_mm, 1)
            pe.wait_ge(w_copied, 4)
            pe.matmul(pw[:, 256:320], rep[:, 0, :], w_v[:, :], start=True, stop=True)
            pe.matmul(pw[:, 320:384], rep[:, 1, :], w_v[:, :], start=True, stop=True).then_inc(w_mm, 1)

            pe.wait_ge(edge_rows_ready, 1)
            tables = [(dst_f[:, :, :].rearrange("p h e -> p (h e)"), 1, 0), (loc_f[:, :, :].rearrange("p h e -> p (h e)"), 1, 0),
                      (src_f[:, :], 1, 0)] + [(attr_raw[:, :, :].rearrange("p e m -> p (e m)"), 3, m) for m in range(3)]
            banks = [ps2[:, 0, 0:512], ps2[:, 0, 512:1024], ps2[:, 1, 0:512], ps2[:, 1, 512:1024], ps3[:, 0, :], ps3[:, 1, :]]
            for (tab, stride, m), bank in zip(tables, banks):
                for c in range(NC6):
                    lo = c * 128 * stride + m
                    mm = pe.transpose(bank[:, c * PAIRS:(c + 1) * PAIRS], tab[:, lo:lo + 127 * stride + 1:stride],
                                      ident[0:PAIRS, 0:PAIRS])
                mm.then_inc(edge_cols_ready, 1)
            for h in range(2):
                pe.transpose(ps1[0:1, 1, h * PAIRS:(h + 1) * PAIRS], dlow[:, h:h + 1], ident[0:PAIRS, 0:PAIRS])
            pe.transpose(ps1[0:1, 1, 2 * PAIRS:3 * PAIRS], dspread[:, 0:1], ident[0:PAIRS, 0:PAIRS]).then_inc(spread_col, 1)

            pe.wait_ge(edge_cols_taken, len(tables))
            pe.wait_ge(banks_cleared, 1)
            with pe.Fori(0, NB) as b:
                for k, (j0, j1) in enumerate(PARTS):
                    pe.wait_ge(head_ready[k], b + 1)
                    for jj in range(j0, j1):
                        for c in range(2):
                            mm = pe.matmul(ps2[:, c, 0:129], hx[:, jj, c, 0:128], hx[:, jj, c, :], start=False, stop=False,
                                           skip_group_check=True)
                    mm.then_inc(head_used[k], 1)
            pe.wait_ge(sums_ready, 1)
            for c in range(2):
                mm = pe.matmul(ps3[:, 0, c * 128:(c + 1) * 128], ones[:, :], sum_diag[:, c, :], start=True, stop=True)
            mm.then_inc(rows_ready, 1)

            def turn_z(i, o):
                if not group(i, o):
                    return
                s = o % RING
                pe.wait_ge(main.dot, RING * i + o + 1)
                if not isinstance(i, int) or o >= 1:
                    pe.wait_ge(main.zt_sb, RING * i + o)
                for tt in range(TG):
                    mm = pe.transpose(ps1[:, 0, tt * 128:(tt + 1) * 128], xg[:, s, tt, 0:128], ident[:, :])
                mm.then_inc(main.zt_ps, 1)

            def hidden(i, o):
                if not group(i, o):
                    return
                s = o % 2
                pe.wait_ge(main.zt_sb, RING * i + o + 1)
                if not isinstance(i, int) or o >= 1:
                    pe.wait_ge(main.hid_sb, RING * i + o)
                pe.matmul(ps1[:, 1, 0:GE], w_hid[:, :], zt[:, s, :], start=True, stop=True).then_inc(main.hid_ps, 1)
                if not isinstance(i, int) or o >= 2:
                    pe.wait_ge(main.o0, RING * i + o - 1)
                    pe.wait_ge(main.q_sb, RING * i + o - 1)
                for tt in range(TG):
                    mm = pe.matmul(pq_ps(s)[:, tt * 128:(tt + 1) * 128], zt[:, s, tt * 128:(tt + 1) * 128], w_z[:, :],
                                   start=True, stop=True)
                mm.then_inc(main.pq, 1)

            def scores(i, o):
                if not group(i, o):
                    return
                s = o % 2
                pe.wait_ge(main.hid_sb, RING * i + o + 1)
                if not isinstance(i, int) or o >= 2:
                    pe.wait_ge(main.exp, RING * i + o - 1)
                for tt in range(TG):
                    mm = pe.matmul(score_ps(s)[:, tt * 96:(tt + 1) * 96], hid_sb[:, s, tt * 128:(tt + 1) * 128],
                                   w_sc[:, :], start=True, stop=True)
                mm.then_inc(main.scores, 1)

            def scatter(i, o):
                if not group(i, o):
                    return
                s, r = o % 2, o % RING
                pe.wait_ge(main.eo, RING * i + o + 1)
                pe.wait_ge(main.sel, RING * i + o + 1)
                if not isinstance(i, int) or o >= 2:
                    pe.wait_ge(main.added, RING * i + o - 1)
                scatter_mm(s, r).then_inc(main.scattered, 1)

            def scatter_mm(s, r):
                for col, lhs0, coef0 in ((0, 256, 2), (96, 0, 0), (192, 128, 3)):
                    for tt in range(TG):
                        lo = (tt * 5 + coef0) * WIN
                        mm = pe.matmul(ps3[:, s, col:col + 96], xg[:, r, tt, lhs0:lhs0 + 128], sel[:, s, lo:lo + 96],
                                       start=(tt == 0), stop=(tt == TG - 1))
                return mm

            pe.wait_ge(kv_ready, 2)
            pe.wait_ge(sel_padded, 1)

            def step(i, k):
                hidden(i, k)
                scores(i, k - 1)
                turn_z(i, k + 1)
                scatter(i, k - 4)

            steps(pe, step, -1, FIRST, TURNS, G + 4)

            far = pe.value_load(spread_i[0:1, 0:1], min_val=0, max_val=1)
            with pe.If(far > 0):
                with pe.Fori(0, G) as g:
                    pe.wait_ge(wide.dot, g + 1)
                    for tt in range(TG):
                        mm = pe.transpose(ps1[:, 0, tt * 128:(tt + 1) * 128], xg[:, 0, tt, 0:128], ident[:, :])
                    mm.then_inc(wide.zt_ps, 1)
                    pe.wait_ge(wide.zt_sb, g + 1)
                    pe.matmul(ps1[:, 1, 0:GE], w_hid[:, :], zt[:, 0, :], start=True, stop=True).then_inc(wide.hid_ps, 1)
                    for tt in range(TG):
                        mm = pe.matmul(pq_ps(0)[:, tt * 128:(tt + 1) * 128], zt[:, 0, tt * 128:(tt + 1) * 128], w_z[:, :],
                                       start=True, stop=True)
                    mm.then_inc(wide.pq, 1)
                    pe.wait_ge(wide.hid_sb, g + 1)
                    for tt in range(TG):
                        mm = pe.matmul(score_ps(0)[:, tt * 96:(tt + 1) * 96], hid_sb[:, 0, tt * 128:(tt + 1) * 128],
                                       w_sc[:, :], start=True, stop=True)
                    mm.then_inc(wide.scores, 1)
                    with pe.Fori(0, NWIN) as w:
                        pe.wait_ge(wide.sel, g * NWIN + w + 1)
                        pe.wait_ge(wide.added, g * NWIN + w + 1)
                        scatter_mm(0, 0).then_inc(wide.scattered, 1)

            def mix(b):
                def turn(jj):
                    pe.wait_ge(epi_staged, b * JB + jj + 1)
                    if past(b) or jj >= 2:
                        pe.wait_ge(epi_xt_sb, b * JB + jj - 1)
                    for c in range(2):
                        mm = pe.transpose(ps1[:, jj % 2, c * 128:c * 128 + P], xn_st[:, jj, c * 128:(c + 1) * 128], ident[0:P, 0:P])
                    mm.then_inc(epi_xt_ps, 1)

                turn(0)
                if past(b):
                    pe.wait_ge(epi_res, b)
                for jj in range(JB):
                    if jj + 1 < JB:
                        turn(jj + 1)
                    pe.wait_ge(epi_xt_sb, b * JB + jj + 1)
                    o = out_ps[:, jj, :]
                    pe.matmul(o[:, 0:128], agg_st[:, jj, 1, :], place_o0[:, :], start=True, stop=False, skip_group_check=True)
                    pe.matmul(o[:, 128:256], xt_sb[:, jj % 2, 1, :], kv[:, 1, :], start=False, stop=False, skip_group_check=True)
                    pe.matmul(o[:, 0:128], xt_sb[:, jj % 2, 0, :], kv[:, 0, :], start=False, stop=False, skip_group_check=True)
                    for k, w in ((2, place[:, 0]), (3, place[:, 1]), (4, place[:, 2]), (5, w_vec[:, 1]), (0, w_vec[:, 0])):
                        mm = pe.matmul(o[:, M:D], agg_st[:, jj, k, :], w.rearrange("p v m -> p (v m)"),
                                       start=False, stop=(k == 0), skip_group_check=True)
                    mm.then_inc(epi_out, 1)

            def gate(b):
                def turn(jj):
                    pe.wait_ge(epi_xf, b * JB + jj + 1)
                    if past(b) or jj >= 2:
                        pe.wait_ge(epi_ft_sb, b * JB + jj - 1)
                    for c in range(2):
                        mm = pe.transpose(ft_ps(jj % 2)[:, c * 128:c * 128 + P], xf_sb[:, jj, c * 128:(c + 1) * 128], ident[0:P, 0:P])
                    mm.then_inc(epi_ft_ps, 1)

                turn(0)
                if past(b):
                    pe.wait_ge(epi_done, b)
                for jj in range(JB):
                    if jj + 1 < JB:
                        turn(jj + 1)
                    pe.wait_ge(epi_ft_sb, b * JB + jj + 1)
                    for c in range(2):
                        mm = pe.matmul(ps3[0:P, 0, jj * 96:(jj + 1) * 96], ft_sb[:, jj % 2, c, :], wg_pad[:, c, :],
                                       start=(c == 0), stop=(c == 1))
                    mm.then_inc(epi_logit, 1)

            def step(b):
                mix(b)
                gate(b - 1)

            pe.wait_ge(wg_padded, 1)
            mix(0)
            step(1)
            with pe.Fori(2, NB) as b:
                step(b)
            gate(NB - 1)

            pe.wait_ge(tot_ready, 1)
            pe.matmul(ps1[0:P, 0, 0:NE], below[:, :], tot[:, :], start=True, stop=True)
            pe.matmul(ps1[:, 0, 128:128 + NE], ones[0:P, :], tot[:, :], start=True, stop=True).then_inc(rank0_ps, 1)

            pe.wait_ge(etile_ready, 1)

            def tile(i, o):
                return not isinstance(i, int) or 0 <= AT_ONCE * i + o < TILES

            def turn_rows(i, o):
                if not tile(i, o):
                    return
                s = o % AT_ONCE
                pe.wait_ge(xs_loaded[s], 16 * (i + o // AT_ONCE + 1))
                if not isinstance(i, int) or o >= 1:
                    pe.wait_ge(xst_sb, AT_ONCE * i + o)
                for c in range(2):
                    mm = pe.transpose(ps1[:, 0, c * 128:(c + 1) * 128], xs_sb[:, s, c::2], ident[:, :])
                mm.then_inc(xst_ps, 1)

            def up(i, o):
                if not tile(i, o):
                    return
                s = o % 2
                pe.wait_ge(w1_half0, AT_ONCE * i + o + 1)
                pe.wait_ge(w1_half1, AT_ONCE * i + o + 1)
                pe.wait_ge(xst_sb, AT_ONCE * i + o + 1)
                if not isinstance(i, int) or o >= 1:
                    pe.wait_ge(ht_ready, AT_ONCE * i + o)
                for half in range(2):
                    for c in range(half * FC // 2, (half + 1) * FC // 2):
                        for kc in range(2):
                            mm = pe.matmul(h_of(c), w1_st[:, s, kc, c, :], xst[:, s, kc, :], start=(kc == 0), stop=(kc == 1))
                    mm.then_inc(h_ps, 1)

            def expert(i, o):
                return pe.value_load(etile[0:1, bass.ds(AT_ONCE * i + o, 1)], min_val=0, max_val=NE - 1) if tile(i, o) else None

            def down(i, o, e):
                if not tile(i, o):
                    return
                pe.wait_ge(ht_ready, AT_ONCE * i + o + 1)
                if not isinstance(i, int) or o >= 1:
                    pe.wait_ge(y_ready, AT_ONCE * i + o)
                for c in range(FC):
                    mm = pe.matmul(ps1[:, 1, 0:D], ht_sb[:, o % 2, c, :], w2_sb[:, bass.ds(e, 1), c, :].rearrange("p e d -> p (e d)"),
                                   start=(c == 0), stop=(c == FC - 1))
                mm.then_inc(y_ps, 1)

            def expert_step(i, o):
                e = expert(i, o - 1)
                up(i, o)
                turn_rows(i, o + 1)
                down(i, o - 1, e)

            for k in (-1, 0, 1, 2):
                expert_step(0, k)
            with pe.Fori(0, TILES // AT_ONCE - 1) as i:
                for o in range(AT_ONCE):
                    expert_step(i, 3 + o)
            for k in (TILES - 1, TILES):
                expert_step(0, k)

        @block.scalar
        def _(act):
            own = Chain(act, act_own)

            act.wait_ge(ln_var_ready, 1)
            act.activation(ln_tmp[:, 3, :], ln_tmp[:, 2, :], ACT.Sqrt, scale=1.0 / D).then_inc(ln_std_ready, 1)

            pw = ps1[:, 0, :]
            act.wait_ge(w_mm, 1)
            act.activation(lin_t[:, :], pw[0:M, 0:128], ACT.Copy).then_inc(w_copied, 1)
            act.wait_ge(w_mm, 2)
            act.activation(tp_t[:, :, :].rearrange("p a b -> p (a b)"), pw[0:M, 128:384], ACT.Copy,
                           scale=c_tp * c_lin * c_lin).then_inc(w_copied, 1)
            act.wait_ge(w_mm, 3)
            act.activation(w_hid[:, 0:M], pw[:, 0:M], ACT.Copy)
            act.activation(w_hid[:, M:128], pw[:, 0:M], ACT.Copy, scale=-1.0)
            act.activation(ba_t[:, :], pw[0:M, 128:256], ACT.Copy)
            act.activation(d_t[:, 0:M], pw[0:M, 256:320], ACT.Copy)
            act.activation(c_t[:, M:128], pw[0:M, 320:384], ACT.Copy).then_inc(w_copied, 1)
            act.wait_ge(w_mm, 4)
            act.activation(w_z[:, 0:M], pw[:, 0:M], ACT.Copy, scale=c_tp)
            act.activation(w_z[:, M:128], pw[:, M:128], ACT.Copy, scale=c_tp * SQ3)
            act.wait_ge(consts_ready, 11)
            for m in range(3):
                act.activation(place[:, m, :, m], pw[:, 128:192], ACT.Copy, scale=c_tp * SQ3)
            act.activation(w_v[:, :], pw[0:M, 192:256], ACT.Copy, scale=c_tp)
            act.activation(w_sc[0:M, 0:M], wsm[:, len(names) - 1, :], ACT.Copy, scale=c_lin)
            act.activation(w_sc[M:128, 0:M], wsm[:, len(names) - 1, :], ACT.Copy, scale=-0.01 * c_lin).then_inc(w_copied, 1)

            act.wait_ge(edge_sq_ready, 1)
            act.activation(edge_len[:, 1, :], edge_len[:, 0, :], ACT.Sqrt).then_inc(edge_len_ready, 1)

            def stage_idx(i, o):
                if not group(i, o):
                    return
                s = o % RING
                if not isinstance(i, int) or o >= RING:
                    act.wait_ge(main.gathered[s], 16 * TG * (i + o // RING))
                act.activation(idx_st[:, s, :], edge_src[:, bass.ds(TG * (RING * i + o), TG)], ACT.Copy).then_inc(main.idx, 1)

            act.wait_ge(edges_ready, 1)
            for k in range(-1 + AHEAD):
                stage_idx(0, k)

            def squares(b):
                act.wait_ge(head_dev, b + 1)
                if past(b):
                    act.wait_ge(head_var, b)
                act.activation(sq[:, :, :], dev[:, bass.ds(b * JB, JB), :].rearrange("p j (h c) -> p (j h) c", c=HC),
                               ACT.Square).then_inc(head_sq, 1)

            batches(act, squares)
            act.wait_ge(head_var, NB)
            act.activation(hstat[:, 2, :], hstat[:, 1, :], ACT.Sqrt, scale=1.0 / (HC - 1)).then_inc(head_std, 1)
            act.wait_ge(zero_ready, 1)
            for k in (0, 1):
                act.wait_ge(head_ready[k], NB)
            act.activation(agg_flat[:, 0:J * D], zero[:, 0:1].to_broadcast([128, J * D]), ACT.Copy).then_inc(agg_zeroed, 1)

            def copy_z(i, o):
                if not group(i, o):
                    return
                s = o % 2
                act.wait_ge(main.zt_ps, RING * i + o + 1)
                if not isinstance(i, int) or o >= 2:
                    act.wait_ge(main.pq, RING * i + o - 1)
                act.activation(zt[:, s, :], ps1[:, 0, 0:GE], ACT.Copy).then_inc(main.zt_sb, 1)

            def relu(i, o):
                if not group(i, o):
                    return
                s = o % 2
                act.wait_ge(main.hid_ps, RING * i + o + 1)
                if not isinstance(i, int) or o >= 2:
                    act.wait_ge(main.scores, RING * i + o - 1)
                act.activation(hid_sb[:, s, :], ps1[:, 1, 0:GE], ACT.Relu).then_inc(main.hid_sb, 1)

            def exps(i, o):
                if not group(i, o):
                    return
                s = o % 2
                act.wait_ge(main.neg_top, RING * i + o + 1)
                if not isinstance(i, int) or o >= 2:
                    act.wait_ge(main.eo, RING * i + o - 1)
                    act.wait_ge(main.coef, RING * i + o - 1)
                for tt in range(TG):
                    act.activation(e0[:, s, tt, :], score_ps(s)[:, tt * 96:tt * 96 + M], ACT.Exp,
                                   bias=neg_top[:, s, tt:tt + 1], accum_out=exp_sum[:, s, tt:tt + 1])
                act.activation(exp_neg[:, s, :], neg_top[:, s, :], ACT.Exp).then_inc(main.exp, 1)

            def scale_q(i, o):
                if not group(i, o):
                    return
                g = RING * i + o
                act.wait_ge(main.pq, g + 1)
                if not isinstance(i, int) or o >= 4:
                    act.wait_ge(main.eo, g - 3)
                for tt in range(TG):
                    ins = act.activation(o0[:, o % 4, tt, :], pq_ps(o % 2)[:, tt * 128 + M:(tt + 1) * 128], ACT.Copy,
                                         scale=edge_rr[:, bass.ds(TG * g + tt, 1)])
                ins.then_inc(main.q_sb, 1)

            act.wait_ge(kv_ready, 2)

            def step(i, k):
                relu(i, k)
                exps(i, k - 2)
                scale_q(i, k)
                copy_z(i, k + 1)
                stage_idx(i, k + AHEAD)

            steps(act, step, -1, FIRST, TURNS, G + 2)

            act.wait_ge(flag_ready, 1)
            far = act.value_load(spread_i[0:1, 0:1], min_val=0, max_val=1)
            with act.If(far > 0):
                with act.Fori(0, G) as g:
                    act.wait_ge(wide.added, g * NWIN + 1)
                    act.activation(idx_st[:, 0, :], edge_src[:, bass.ds(TG * g, TG)], ACT.Copy).then_inc(wide.idx, 1)
                    act.wait_ge(wide.zt_ps, g + 1)
                    act.activation(zt[:, 0, :], ps1[:, 0, 0:GE], ACT.Copy).then_inc(wide.zt_sb, 1)
                    act.wait_ge(wide.hid_ps, g + 1)
                    act.activation(hid_sb[:, 0, :], ps1[:, 1, 0:GE], ACT.Relu).then_inc(wide.hid_sb, 1)
                    act.wait_ge(wide.pq, g + 1)
                    for tt in range(TG):
                        ins = act.activation(o0[:, 0, tt, :], pq_ps(0)[:, tt * 128 + M:(tt + 1) * 128], ACT.Copy,
                                             scale=edge_rr[:, bass.ds(TG * g + tt, 1)])
                    ins.then_inc(wide.q_sb, 1)
                    act.wait_ge(wide.neg_top, g + 1)
                    for tt in range(TG):
                        act.activation(e0[:, 0, tt, :], score_ps(0)[:, tt * 96:tt * 96 + M], ACT.Exp,
                                       bias=neg_top[:, 0, tt:tt + 1], accum_out=exp_sum[:, 0, tt:tt + 1])
                    act.activation(exp_neg[:, 0, :], neg_top[:, 0, :], ACT.Exp).then_inc(wide.exp, 1)

            act.wait_ge(agg_final, 1)
            act.wait_ge(gate_loaded, 32)
            act.activation(wg_pad[:, :, :], zero[:, 0:192].rearrange("p (c e) -> p c e", c=2), ACT.Copy).then_inc(act_own, 1)
            act.wait_ge(act_own, 1)
            act.activation(wg_pad[:, :, 0:NE], wg_sb[:, :, :], ACT.Copy).then_inc(wg_padded, 1)

            def stage(b, jj):
                if isinstance(b, int) and b >= NB:
                    return
                act.activation(agg_st[:, jj, :, :], agg[:, :, 0:N].rearrange("q s (p j) -> q s j p", j=J)[:, :, bass.ds(b * JB + jj, 1), :]
                               .rearrange("q s j p -> q s (j p)"), ACT.Copy)
                act.activation(xn_st[:, jj, :], xn_sb[:, bass.ds(b * JB + jj, 1), :].rearrange("p j d -> p (j d)"),
                               ACT.Copy).then_inc(epi_staged, 1)

            def turned(b):
                for jj in range(JB):
                    act.wait_ge(epi_xt_ps, b * JB + jj + 1)
                    if past(b) or jj >= 2:
                        act.wait_ge(epi_out, b * JB + jj - 1)
                    act.activation(xt_sb[:, jj % 2, :, :], ps1[:, jj % 2, 0:256].rearrange("q (c p) -> q c p", p=128)[:, :, 0:P],
                                   ACT.Copy).then_inc(epi_xt_sb, 1)
                    if jj:
                        act.wait_ge(epi_out, b * JB + jj)
                        stage(b + 1, jj - 1)
                act.wait_ge(epi_out, (b + 1) * JB)
                stage(b + 1, JB - 1)

            def gate_turned(b):
                for jj in range(JB):
                    act.wait_ge(epi_ft_ps, b * JB + jj + 1)
                    if past(b) or jj >= 2:
                        act.wait_ge(epi_logit, b * JB + jj - 1)
                    act.activation(ft_sb[:, jj % 2, :, :], ft_ps(jj % 2)[:, 0:256].rearrange("q (c p) -> q c p", p=128)[:, :, 0:P],
                                   ACT.Copy).then_inc(epi_ft_sb, 1)

            def deviations(b):
                act.wait_ge(epi_var, b + 1)
                act.activation(ln_std[:, :], ln_var[:, :], ACT.Sqrt).then_inc(epi_std, 1)

            def step(b):
                turned(b)
                gate_turned(b - 1)
                deviations(b)

            for jj in range(JB):
                stage(0, jj)
            turned(0)
            deviations(0)
            step(1)
            with act.Fori(2, NB - 1) as b:
                step(b)
            step(NB - 1)
            gate_turned(NB - 1)

            act.wait_ge(gap_ready, 1)
            act.activation(gap[:, 1, :], gap[:, 0, :], ACT.Exp).then_inc(gap_exp, 1)

            act.wait_ge(slots_ready, 1)

            def slots_to_send(b):
                for k, (j0, j1) in enumerate(PARTS):
                    if past(b):
                        act.wait_ge(rows_sent[k], b * K2 * (j1 - j0) * 16)
                    act.activation(slot_st[:, j0:j1, :], slot_i[:, bass.ds(b * JB + j0, j1 - j0), :], ACT.Copy).then_inc(slot_staged[k], 1)

            batches(act, slots_to_send)

            act.wait_ge(etile_ready, 1)
            act.wait_ge(b_loaded, 32)

            def stage_w1(i, o):
                if isinstance(i, int) and 2 * i + o >= TILES:
                    return
                e = act.value_load(etile[0:1, bass.ds(2 * i + o, 1)], min_val=0, max_val=NE - 1)
                act.wait_ge(ew_loaded, 32 * e + 32)
                if past(i) or o >= 2:
                    act.wait_ge(h_ps, 2 * (2 * i + o) - 2)
                act.activation(w1_st[:, o % 2, 1, :, :], w1_columns(e, 1), ACT.Copy).then_inc(w1_half1, 1)

            def gelu(i, o):
                k = 2 * i + o
                if past(i) or o >= 2:
                    act.wait_ge(y_ps, k - 1)
                act.wait_ge(b1_ready, k + 1)
                for half in range(2):
                    act.wait_ge(h_ps, 2 * k + half + 1)
                    for c in range(half * FC // 2, (half + 1) * FC // 2):
                        ins = act.activation(ht_sb[:, o % 2, c, :], h_of(c), ACT.Gelu, bias=b1_cur[:, o % 2, c:c + 1])
                ins.then_inc(ht_ready, 1)

            def expert_step(i, o):
                stage_w1(i, o + 1)
                gelu(i, o)

            stage_w1(0, 0)
            for k in (0, 1):
                expert_step(0, k)
            with act.Fori(0, (TILES - 4) // 2) as i:
                expert_step(i, 2)
                expert_step(i, 3)
            for k in (TILES - 2, TILES - 1):
                expert_step(0, k)

            act.wait_ge(y_ready, TILES)

            def slots_to_take(b):
                for k, (j0, j1) in enumerate(PARTS):
                    if past(b):
                        act.wait_ge(y_taken[k], b * K2 * (j1 - j0) * 16)
                    act.activation(slot_st2[:, j0:j1, :], slot_i[:, bass.ds(b * JB + j0, j1 - j0), :],
                                   ACT.Copy).then_inc(slot_staged2[k], 1)

            batches(act, slots_to_take)

        @block.vector
        def _(dve):
            own = Chain(dve, dve_own)

            dve.memset(dst_raw[64:PAIRS, :], int(FAR)).then_inc(raw_padded, 1)
            dve.memset(src_raw[64:PAIRS, :], 0).then_inc(raw_padded, 1)

            for b in range(NB):
                dve.wait_ge(x_loaded[b], 32)
                for j in range(b * JB, (b + 1) * JB):
                    ins = dve.bn_stats(ln_stats[:, j, :], x_sb[:, j, :])
                ins.then_inc(ln_stats_ready, 1)
            dve.wait_ge(ln_stats_ready, NB)
            own(dve.tensor_tensor(ln_tmp[:, 0, :], ln_stats[:, :, 1], ln_stats[:, :, 4], ALU.subtract))
            own(dve.scalar_tensor_tensor(out=ln_tmp[:, 1, :], in0=ln_tmp[:, 0, :], scalar=D / 4.0, in1=ln_tmp[:, 0, :],
                                         op0=ALU.mult, op1=ALU.mult))
            own(dve.scalar_tensor_tensor(out=ln_tmp[:, 0, :], in0=ln_stats[:, :, 2], scalar=D * EPS, in1=ln_stats[:, :, 5],
                                         op0=ALU.add, op1=ALU.add))
            dve.tensor_tensor(ln_tmp[:, 2, :], ln_tmp[:, 0, :], ln_tmp[:, 1, :], ALU.add).then_inc(ln_var_ready, 1)
            own(dve.tensor_tensor(ln_tmp[:, 4, :], ln_stats[:, :, 1], ln_stats[:, :, 4], ALU.add))
            own(dve.tensor_scalar(mean2[:, :], ln_tmp[:, 4, :], 0.5, None, ALU.mult))
            dve.wait_ge(ln_std_ready, 1)
            own(dve.reciprocal(rstd2[:, :], ln_tmp[:, 3, :]))
            with dve.Fori(0, NB) as b:
                for jj in range(JB):
                    j = b * JB + jj
                    ins = dve.tensor_scalar(xn_sb[:, bass.ds(j, 1), :].rearrange("p j d -> p (j d)"),
                                            x_sb[:, bass.ds(j, 1), :].rearrange("p j d -> p (j d)"),
                                            mean2[:, bass.ds(j, 1)], rstd2[:, bass.ds(j, 1)], ALU.subtract, ALU.mult)
                ins.then_inc(xn_ready, 1)

            dve.wait_ge(raw_loaded, 16 * 9)
            dve.tensor_copy(src_f[:, :], src_raw[:, :])
            own(dve.tensor_copy(dst_f[:, :, :].rearrange("p h e -> p (h e)"), dst_raw[:, :]))
            own(dve.tensor_reduce(dlow[:, :], dst_f[:, :, :], AX.X, ALU.min))
            own(dve.scalar_tensor_tensor(out=loc_f[:, :, :], in0=dst_f[:, :, :], scalar=FAR - 1.0, in1=dst_f[:, :, :],
                                         op0=ALU.is_lt, op1=ALU.mult))
            own(dve.tensor_reduce(dhigh[:, :], loc_f[:, :, :], AX.X, ALU.max))
            own(dve.tensor_tensor(dspread[:, :], dhigh[:, :], dlow[:, :], ALU.subtract))
            own(dve.tensor_tensor(dspread[:, 0:1], dspread[:, 0:1], dspread[:, 1:2], ALU.max))
            for h in range(2):
                ins = dve.tensor_scalar(loc_f[:, h, :], dst_f[:, h, :], dlow[:, h:h + 1], None, ALU.subtract)
            ins.then_inc(edge_rows_ready, 1)
            dve.wait_ge(edge_rows_ready, 1)

            def cols(bank):
                return bank[:, 0:NT].rearrange("p (c j) -> p j c", j=PAIRS)

            def rows(tab):
                return tab.rearrange("p (j c) -> p j c", c=NC6)

            banks = [ps2[:, 0, 0:512], ps2[:, 0, 512:1024], ps2[:, 1, 0:512], ps2[:, 1, 512:1024], ps3[:, 0, :], ps3[:, 1, :]]
            dests = [edge_dst[:, :], edge_loc[:, :], edge_src[:, :]] + [edge_tmp[:, :, m] for m in range(3)]
            for k, (bank, tab) in enumerate(zip(banks, dests)):
                dve.wait_ge(edge_cols_ready, k + 1)
                dve.tensor_copy(rows(tab), cols(bank)).then_inc(edge_cols_taken, 1)
            dve.wait_ge(spread_col, 1)
            for h in range(2):
                ins = dve.tensor_copy(base_i[:, :, h], ps1[0:1, 1, h * PAIRS:(h + 1) * PAIRS])
            ins.then_inc(base_ready, 1)
            own(dve.tensor_reduce(spread_row[:, :], ps1[0:1, 1, 2 * PAIRS:3 * PAIRS], AX.X, ALU.max))
            dve.tensor_scalar(spread_i[:, :], spread_row[:, :], float(WIN), None, ALU.is_ge).then_inc(flag_ready, 1)
            dve.wait_ge(edge_cols_taken, 6)
            own(dve.tensor_tensor(edge_r[:, :, :], edge_tmp[:, :, :], edge_tmp[:, :, :], ALU.mult))
            dve.tensor_reduce(edge_len[:, 0, :], edge_r[:, :, :], AX.X, ALU.add).then_inc(edge_sq_ready, 1)
            dve.wait_ge(edge_len_ready, 1)
            own(dve.tensor_scalar(edge_len[:, 0, :], edge_len[:, 1, :], 1e-12, None, ALU.add))
            own(dve.reciprocal(edge_len[:, 2, :], edge_len[:, 0, :]))
            own(dve.tensor_tensor(edge_len[:, 0, :], edge_len[:, 1, :], edge_len[:, 2, :], ALU.mult))
            own(dve.tensor_tensor(edge_rr[:, :], edge_len[:, 0, :], edge_len[:, 0, :], ALU.mult))
            dve.tensor_tensor(edge_r[:, :, :], edge_tmp[:, :, :], edge_len[:, 2, :].unsqueeze(2).to_broadcast([128, NT, 3]),
                              ALU.mult).then_inc(edges_ready, 1)
            dve.wait_ge(edges_ready, 1)

            dve.wait_ge(consts_ready, 11)
            for c in range(2):
                ins = dve.tensor_reduce(pick_m[:, c, :], pick[:, c, :, :].rearrange("p u m -> p m u"), AX.X, ALU.add)
            own(ins)
            dve.wait_ge(w_mm, 5)
            for c in range(2):
                ins = dve.tensor_tensor(w_vec[:, c, :, :], ps1[:, 0, 256 + c * M:256 + (c + 1) * M].unsqueeze(2).to_broadcast([128, M, 3]),
                                        pick_m[:, c, :].unsqueeze(1).to_broadcast([128, M, 3]), ALU.mult)
            own(ins)
            for c in range(2):
                ins = dve.memset(ps2[:, c, 0:129], 0.0)
            ins.then_inc(banks_cleared, 1)

            dve.wait_ge(xn_ready, NB)
            own.open(1)

            def heads(b):
                own.enter(b)
                xh = xn_sb[:, bass.ds(b * JB, JB), :].rearrange("p j (h c) -> p (j h) c", c=HC)
                total = hstat[:, 0, bass.ds(b * JB * H, JB * H)]
                own(dve.tensor_reduce(total, xh, AX.X, ALU.add))
                dve.scalar_tensor_tensor(out=dev[:, bass.ds(b * JB, JB), :].rearrange("p j (h c) -> p (j h) c", c=HC),
                                         in0=total.unsqueeze(2).to_broadcast([P, JB * H, HC]), scalar=-1.0 / HC, in1=xh,
                                         op0=ALU.mult, op1=ALU.add).then_inc(head_dev, 1)

            def mean_squares(b):
                dve.wait_ge(head_sq, b + 1)
                dve.tensor_reduce(hstat[:, 1, bass.ds(b * JB * H, JB * H)], sq[:, :, :], AX.X, ALU.add).then_inc(head_var, 1)

            heads(0)
            with dve.Fori(1, NB) as b:
                heads(b)
                mean_squares(b - 1)
            own.leave(NB)
            mean_squares(NB - 1)
            dve.wait_ge(head_std, 1)
            own(dve.tensor_scalar(hstat[:, 0, :], hstat[:, 2, :], EPS, None, ALU.add))
            own(dve.reciprocal(hstat[:, 1, :], hstat[:, 0, :]))

            def quotients(b):
                for k, (j0, j1) in enumerate(PARTS):
                    if past(b):
                        dve.wait_ge(head_used[k], b)
                    n = j1 - j0
                    dve.tensor_tensor(hx[:, j0:j1, :, 0:128].rearrange("p j c (h f) -> p (j c) h f", f=HC),
                                      dev[:, bass.ds(b * JB + j0, n), :].rearrange("p j (c h f) -> p (j c) h f", c=2, f=HC),
                                      hstat[:, 1, bass.ds((b * JB + j0) * H, n * H)].rearrange("p (a h) -> p a h", h=H // 2)
                                      .unsqueeze(3).to_broadcast([P, n * 2, H // 2, HC]),
                                      ALU.mult).then_inc(head_ready[k], 1)

            batches(dve, quotients)

            for k in (0, 1):
                dve.wait_ge(head_used[k], NB)
            dve.wait_ge(mixw_loaded, 64)
            for c in range(2):
                ins = dve.tensor_scalar(sum_diag[:, c, :], ident[:, :], ps2[:, c, 128:129], None, ALU.mult)
            ins.then_inc(sums_ready, 1)
            dve.wait_ge(rows_ready, 1)
            for c in range(2):
                cs = slice(c * 128, (c + 1) * 128)
                own(dve.tensor_scalar(kv_col[:, 0:1], kb_col[:, c:c + 1], float(N), None, ALU.mult))
                own(dve.scalar_tensor_tensor(out=kv_col[:, 1:2], in0=ps2[:, c, 128:129], scalar=kw_col[:, c:c + 1],
                                             in1=kv_col[:, 0:1], op0=ALU.mult, op1=ALU.add))
                own(dve.scalar_tensor_tensor(out=kv_tmp[:, 0, :], in0=ps2[:, c, 0:128], scalar=kw_col[:, c:c + 1],
                                             in1=vw_bc[:, cs], op0=ALU.mult, op1=ALU.mult))
                own(dve.scalar_tensor_tensor(out=kv_tmp[:, 1, :], in0=vb_bc[:, cs], scalar=kv_col[:, 1:2],
                                             in1=kv_tmp[:, 0, :], op0=ALU.mult, op1=ALU.add))
                own(dve.scalar_tensor_tensor(out=kv_tmp[:, 2, :], in0=ps3[:, 0, cs], scalar=kb_col[:, c:c + 1],
                                             in1=vw_bc[:, cs], op0=ALU.mult, op1=ALU.mult))
                own(dve.tensor_tensor(kv_tmp[:, 0, :], kv_tmp[:, 1, :], kv_tmp[:, 2, :], ALU.add))
                own(dve.tensor_tensor(kv_tmp[:, 1, :], kv_tmp[:, 0, :], head_block[:, :], ALU.mult))
                dve.scalar_tensor_tensor(out=kv[:, c, :], in0=ident[:, :], scalar=2.0, in1=kv_tmp[:, 1, :],
                                         op0=ALU.mult, op1=ALU.add).then_inc(kv_ready, 1)
                dve.wait_ge(kv_ready, c + 1)

            def products(i, o):
                if not group(i, o):
                    return
                s = o % RING
                dve.wait_ge(main.gathered[s], 16 * TG * (i + o // RING + 1))
                if not isinstance(i, int) or o >= 1:
                    dve.wait_ge(main.dot, RING * i + o)
                products_of(s, RING * i + o).then_inc(main.prod, 1)

            def products_of(s, g):
                r = edge_r[:, bass.ds(TG * g, TG), :].unsqueeze(2).to_broadcast([128, TG, M, 3])
                return dve.tensor_tensor(prod[:, :, :, :], xg[:, s, :, 128:320].rearrange("p t (u m) -> p t u m", m=3), r,
                                         ALU.mult)

            def dots(i, o):
                if not group(i, o):
                    return
                dve.wait_ge(main.prod, RING * i + o + 1)
                dve.tensor_reduce(xg[:, o % RING, :, 0:M], prod[:, :, :, :], AX.X, ALU.add).then_inc(main.dot, 1)

            def maxima(i, o):
                if not group(i, o):
                    return
                s = o % 2
                dve.wait_ge(main.scores, RING * i + o + 1)
                if not isinstance(i, int) or o >= 2:
                    dve.wait_ge(main.exp, RING * i + o - 1)
                maxima_of(s).then_inc(main.neg_top, 1)

            def maxima_of(s):
                return dve.tensor_reduce(neg_top[:, s, :], score_ps(s).rearrange("p (t f) -> p t f", f=96)[:, :, 0:M + 1], AX.X,
                                         ALU.max, negate=True)

            def hots(i, o):
                if not group(i, o):
                    return
                if not isinstance(i, int) or o >= 2:
                    dve.wait_ge(main.sel, RING * i + o - 1)
                loc = edge_loc[:, bass.ds(TG * (RING * i + o), TG)].unsqueeze(2).to_broadcast([128, TG, WIN])
                dve.tensor_tensor(hot[:, o % 2, :, :], iota_w[:, :].unsqueeze(1).to_broadcast([128, TG, WIN]), loc,
                                  ALU.is_equal).then_inc(main.hot, 1)

            def out0(i, o):
                if not group(i, o):
                    return
                dve.wait_ge(main.q_sb, RING * i + o + 1)
                out0_of(o % 4, o % 2).then_inc(main.o0, 1)

            def out0_of(q, s):
                return dve.tensor_tensor(o0[:, q, :, :], o0[:, q, :, :],
                                         pq_ps(s).rearrange("p (t f) -> p t f", f=128)[:, :, 0:M], ALU.add)

            def norm_of(s):
                return dve.scalar_tensor_tensor(out=norm[:, :], in0=exp_neg[:, s, :], scalar=float(V), in1=exp_sum[:, s, :],
                                                op0=ALU.mult, op1=ALU.add)

            def norms(i, o):
                if not group(i, o):
                    return
                g = RING * i + o
                dve.wait_ge(main.exp, g + 1)
                if not isinstance(i, int) or o >= 1:
                    dve.wait_ge(main.norm, 3 * g)
                norm_of(o % 2).then_inc(main.norm, 1)

            def inverses(i, o):
                if not group(i, o):
                    return
                dve.wait_ge(main.norm, 3 * (RING * i + o) + 1)
                dve.reciprocal(coef[:, o % 2, :, 4], norm[:, :]).then_inc(main.norm, 1)

            def weights(i, o):
                if not group(i, o):
                    return
                dve.wait_ge(main.norm, 3 * (RING * i + o) + 2)
                dve.tensor_tensor(coef[:, o % 2, :, 3], exp_neg[:, o % 2, :], coef[:, o % 2, :, 4],
                                  ALU.mult).then_inc(main.norm, 1)

            def vector_weights(i, o):
                if not group(i, o):
                    return
                g = RING * i + o
                dve.wait_ge(main.norm, 3 * g + 3)
                vector_weights_of(o % 2, g).then_inc(main.coef, 1)

            def vector_weights_of(s, g):
                return dve.tensor_tensor(coef[:, s, :, 0:3], edge_r[:, bass.ds(TG * g, TG), :],
                                         coef[:, s, :, 3].unsqueeze(2).to_broadcast([128, TG, 3]), ALU.mult)

            def messages(i, o):
                if not group(i, o):
                    return
                dve.wait_ge(main.o0, RING * i + o + 1)
                messages_of(o % RING, o % 2, o % 4).then_inc(main.eo, 1)

            def messages_of(r, s, q):
                return dve.tensor_tensor(xg[:, r, :, M + D:2 * M + D], e0[:, s, :, :], o0[:, q, :, :], ALU.mult)

            def weigh(i, o):
                if not group(i, o):
                    return
                g = RING * i + o
                if not isinstance(i, int) or o >= 2:
                    dve.wait_ge(main.scattered, g - 1)
                dve.wait_ge(main.hot, g + 1)
                dve.wait_ge(main.coef, g + 1)
                weigh_of(o % 2).then_inc(main.sel, 1)

            def weigh_of(s):
                return dve.tensor_tensor(sel[:, s, 0:TG * 5 * WIN].rearrange("p (t k w) -> p t k w", t=TG, k=5),
                                         hot[:, s, :, :].unsqueeze(2).to_broadcast([128, TG, 5, WIN]),
                                         coef[:, s, :, :].unsqueeze(3).to_broadcast([128, TG, 5, WIN]), ALU.mult)

            def add(i, o):
                if not group(i, o):
                    return
                g = RING * i + o
                base = dve.value_load(base_i[0:1, :, :].rearrange("p a b -> p (a b)")[:, bass.ds(g, 1)], min_val=0, max_val=N)
                dve.wait_ge(main.scattered, g + 1)
                if not isinstance(i, int) or o >= 1:
                    dve.wait_ge(main.added, g)
                add_to(agg[:, :, bass.ds(base, WIN)], o % 2).then_inc(main.added, 1)

            def add_to(win, s):
                return dve.tensor_tensor(win, win, ps3[:, s, WIN:7 * WIN].rearrange("p (k w) -> p k w", w=WIN), ALU.add)

            dve.wait_ge(kv_ready, 2)
            dve.wait_ge(base_ready, 1)
            dve.wait_ge(agg_zeroed, 2)
            dve.memset(sel[:, :, TG * 5 * WIN:], 0.0).then_inc(sel_padded, 1)

            def step(i, k):
                products(i, k + 1)
                norms(i, k - 3)
                hots(i, k - 3)
                inverses(i, k - 3)
                dots(i, k + 1)
                weights(i, k - 3)
                out0(i, k - 1)
                vector_weights(i, k - 3)
                messages(i, k - 3)
                weigh(i, k - 3)
                maxima(i, k - 1)
                add(i, k - 5)

            steps(dve, step, -1, FIRST, TURNS, G + 5)
            dve.wait_ge(main.added, G)

            far = dve.value_load(spread_i[0:1, 0:1], min_val=0, max_val=1)
            with dve.If(far > 0):
                dve.memset(agg[:, :, :], 0.0).then_inc(wide.added, 1)
                dve.wait_ge(wide.added, 1)
                with dve.Fori(0, G) as g:
                    dve.wait_ge(wide.gathered[0], 16 * TG * (g + 1))
                    products_of(0, g).then_inc(wide.prod, 1)
                    dve.wait_ge(wide.prod, g + 1)
                    dve.tensor_reduce(xg[:, 0, :, 0:M], prod[:, :, :, :], AX.X, ALU.add).then_inc(wide.dot, 1)
                    dve.wait_ge(wide.q_sb, g + 1)
                    out0_of(0, 0).then_inc(wide.o0, 1)
                    dve.wait_ge(wide.scores, g + 1)
                    maxima_of(0).then_inc(wide.neg_top, 1)
                    dve.wait_ge(wide.exp, g + 1)
                    norm_of(0).then_inc(wide.norm, 1)
                    dve.wait_ge(wide.norm, 3 * g + 1)
                    dve.reciprocal(coef[:, 0, :, 4], norm[:, :]).then_inc(wide.norm, 1)
                    dve.wait_ge(wide.norm, 3 * g + 2)
                    dve.tensor_tensor(coef[:, 0, :, 3], exp_neg[:, 0, :], coef[:, 0, :, 4], ALU.mult).then_inc(wide.norm, 1)
                    dve.wait_ge(wide.norm, 3 * g + 3)
                    vector_weights_of(0, g).then_inc(wide.coef, 1)
                    dve.wait_ge(wide.o0, g + 1)
                    messages_of(0, 0, 0).then_inc(wide.eo, 1)
                    dve.wait_ge(wide.eo, g + 1)
                    dve.wait_ge(wide.coef, g + 1)
                    dve.tensor_scalar(loc_w[:, :], edge_dst[:, bass.ds(TG * g, TG)], 1.0, None, ALU.mult).then_inc(loc_ready, 1)
                    with dve.Fori(0, NWIN) as w:
                        n = g * NWIN + w
                        dve.wait_ge(loc_ready, n + g + 1)
                        dve.tensor_tensor(hot[:, 0, :, :], iota_w[:, :].unsqueeze(1).to_broadcast([128, TG, WIN]),
                                          loc_w[:, :].unsqueeze(2).to_broadcast([128, TG, WIN]), ALU.is_equal).then_inc(wide.hot, 1)
                        dve.wait_ge(wide.hot, n + 1)
                        weigh_of(0).then_inc(wide.sel, 1)
                        dve.tensor_scalar(loc_w[:, :], loc_w[:, :], float(WIN), None, ALU.subtract).then_inc(loc_ready, 1)
                        dve.wait_ge(wide.scattered, n + 1)
                        add_to(agg[:, :, bass.ds(w * WIN, WIN)], 0).then_inc(wide.added, 1)
                dve.wait_ge(wide.added, G * NWIN + 1)
            dve.tensor_scalar(agg[:, :, N:NW], agg[:, :, N:NW], 0.0, None, ALU.mult).then_inc(agg_final, 1)

            def sums(b):
                own.enter(b)
                xb = x_sb[:, bass.ds(b * JB, JB), :]

                def row(jj):
                    return x_sb[:, bass.ds(b * JB + jj, 1), :].rearrange("p j d -> p (j d)")

                dve.wait_ge(epi_out, (b + 1) * JB)
                dve.tensor_tensor(xb, xb, out_ps, ALU.add).then_inc(epi_res, 1)
                summed_up = count(dve, b + 1)
                dve.wait_ge(x_loaded[0], 32)
                dve.wait_ge(epi_res, summed_up)
                for jj in range(JB):
                    ins = dve.bn_stats(ln_stats[:, jj, :], row(jj))
                own.apart(ins, (x_loaded[0], 32))
                for jj in range(JB):
                    ins = dve.bn_aggr(ln_mv[:, jj, :], ln_stats[:, jj, :])
                own(ins)
                dve.tensor_scalar(ln_var[:, :], ln_mv[:, :, 1], EPS, None, ALU.add).then_inc(epi_var, 1)
                dve.tensor_copy(mean2[:, bass.ds(b * JB, JB)], ln_mv[:, :, 0])
                dve.wait_ge(epi_std, b + 1)
                own(dve.reciprocal(ln_rstd[:, :], ln_std[:, :]))
                dve.tensor_scalar(rstd2[:, bass.ds(b * JB, JB)], ln_rstd[:, :], 1.0, None, ALU.mult)
                if past(b):
                    dve.wait_ge(epi_ft_ps, b * JB)
                for jj in range(JB):
                    dve.tensor_scalar(xf_sb[:, jj, :], row(jj), ln_mv[:, jj, 0:1], ln_rstd[:, jj:jj + 1],
                                      ALU.subtract, ALU.mult).then_inc(epi_xf, 1)

            def choose(b):
                dve.wait_ge(epi_logit, (b + 1) * JB)
                own.apart(dve.tensor_tensor(logit[:, :, :], ps3[0:P, 0, 0:JB * 96].rearrange("p (j e) -> p j e", e=96)[:, :, 0:NE],
                                            bg_bc[:, :].unsqueeze(1).to_broadcast([P, JB, NE]), ALU.add), (x_loaded[0], 32))
                for jj in range(JB):
                    ins = dve.max(top8[:, jj, :], logit[:, jj, :])
                own(ins)
                dve.tensor_scalar(top_w[:, bass.ds(b * JB, JB), :], top8[:, :, 0:K2], 1.0, None, ALU.mult)
                for jj in range(JB):
                    ins = dve.max_index(top8_i[:, jj, :], top8[:, jj, :], logit[:, jj, :])
                own(ins)
                dve.tensor_scalar(top_i[:, bass.ds(b * JB, JB), :], top8_i[:, :, 0:K2], 1.0, None, ALU.mult).then_inc(epi_done, 1)
                dve.wait_ge(epi_done, b + 1)

            def step(b):
                sums(b)
                choose(b - 1)

            own.open(3)
            sums(0)
            own.leave(1)
            own.open(6)
            own.first -= 6
            step(1)
            with dve.Fori(2, NB) as b:
                step(b)
            own.leave(NB)
            choose(NB - 1)

            dve.tensor_tensor(gap[:, 0, :], top_w[:, :, 1], top_w[:, :, 0], ALU.subtract).then_inc(gap_ready, 1)
            for k in range(K2):
                ins = dve.tensor_tensor(picked[:, k, :, :], top_i[:, :, k].unsqueeze(2).to_broadcast([P, J, NE]),
                                        iota_e[:, :].unsqueeze(1).to_broadcast([P, J, NE]), ALU.is_equal)
            own(ins)
            own(dve.tensor_tensor(both[:, :, :], picked[:, 0, :, :], picked[:, 1, :, :], ALU.add))
            for e in range(NE):
                ins = dve.tensor_tensor_scan(ranks[:, :, e], ones[0:P, 0:J], both[:, :, e], 0.0, ALU.mult, ALU.add)
            own(ins)
            dve.tensor_copy(tot[:, :], ranks[:, J - 1, :]).then_inc(tot_ready, 1)
            dve.wait_ge(tot_ready, 1)
            own(dve.tensor_tensor(ranks[:, :, :], ranks[:, :, :], both[:, :, :], ALU.subtract))
            dve.wait_ge(rank0_ps, 1)
            own(dve.tensor_scalar(n_tiles_i[:, 0, :], ps1[:, 0, 128:128 + NE], 127.0, None, ALU.add))
            own(dve.tensor_scalar(n_tiles_i[:, 1, :], n_tiles_i[:, 0, :], 7, None, ALU.arith_shift_right))
            own(dve.tensor_copy(n_tiles[:, 0, :], n_tiles_i[:, 1, :]))
            own(dve.tensor_tensor_scan(n_tiles[:, 1, :], ones[:, 0:NE], n_tiles[:, 0, :], 0.0, ALU.mult, ALU.add))
            own(dve.tensor_tensor(n_tiles[:, 2, :], n_tiles[:, 1, :], n_tiles[:, 0, :], ALU.subtract))
            own(dve.scalar_tensor_tensor(out=row0[:, :], in0=n_tiles[0:P, 2, :], scalar=128.0, in1=ps1[0:P, 0, 0:NE],
                                         op0=ALU.mult, op1=ALU.add))
            own(dve.tensor_tensor(ranks[:, :, :], ranks[:, :, :], row0[:, :].unsqueeze(1).to_broadcast([P, J, NE]), ALU.add))
            for k in range(K2):
                own(dve.tensor_tensor(both[:, :, :], ranks[:, :, :], picked[:, k, :, :], ALU.mult))
                own(dve.tensor_reduce(slot_f[:, k, :], both[:, :, :], AX.X, ALU.add))
            dve.tensor_copy(slot_i[:, :, :].rearrange("p j k -> p k j"), slot_f[:, :, :]).then_inc(slots_ready, 1)
            own(dve.tensor_tensor(ended[:, :, :], iota_tile[:, :].unsqueeze(2).to_broadcast([1, TILES, NE]),
                                  n_tiles[0:1, 1, :].unsqueeze(1).to_broadcast([1, TILES, NE]), ALU.is_ge))
            own(dve.tensor_reduce(etile_f[:, :], ended[:, :, :], AX.X, ALU.add))
            dve.tensor_scalar(etile[:, :], etile_f[:, :], float(NE - 1), None, ALU.min).then_inc(etile_ready, 1)
            dve.wait_ge(gap_exp, 1)
            own(dve.tensor_scalar(gap[:, 0, :], gap[:, 1, :], 1.0, None, ALU.add))
            own(dve.reciprocal(top_w[:, :, 0], gap[:, 0, :]))
            own(dve.tensor_tensor(top_w[:, :, 1], gap[:, 1, :], top_w[:, :, 0], ALU.mult))

            def stage_rows(b):
                for k, (j0, j1) in enumerate(PARTS):
                    if past(b):
                        dve.wait_ge(rows_sent[k], b * K2 * (j1 - j0) * 16)
                    for jj in range(j0, j1):
                        j = b * JB + jj
                        dve.tensor_scalar(row_st[:, jj, :], x_sb[:, bass.ds(j, 1), :].rearrange("p j d -> p (j d)"),
                                          mean2[:, bass.ds(j, 1)], rstd2[:, bass.ds(j, 1)], ALU.subtract,
                                          ALU.mult).then_inc(row_staged[k], 1)

            batches(dve, stage_rows)

            for k, (j0, j1) in enumerate(PARTS):
                dve.wait_ge(rows_sent[k], 16 * K2 * (j1 - j0) * NB)
            dve.wait_ge(etile_ready, 1)
            dve.wait_ge(b_loaded, 32)

            def rows_t(i, o):
                dve.wait_ge(xst_ps, 2 * i + o + 1)
                if not isinstance(i, int) or o >= 2:
                    dve.wait_ge(h_ps, 2 * (2 * i + o) - 2)
                dve.tensor_copy(xst[:, o % 2, :, :].rearrange("p c s -> p (c s)"), ps1[:, 0, 0:256]).then_inc(xst_sb, 1)

            rows_t(0, 0)

            def stage_w1(i, o):
                s = o % 2
                k = 2 * i + o
                e = dve.value_load(etile[0:1, bass.ds(k, 1)], min_val=0, max_val=NE - 1)
                dve.wait_ge(ew_loaded, 32 * e + 32)
                if not isinstance(i, int) or o >= 2:
                    dve.wait_ge(h_ps, 2 * k - 2)
                dve.tensor_scalar(w1_st[:, s, 0, :, :], w1_columns(e, 0), 1.0, None, ALU.mult).then_inc(w1_half0, 1)
                if not isinstance(i, int) or o >= 2:
                    dve.wait_ge(ht_ready, k - 1)
                dve.tensor_scalar(b1_cur[:, s, :], b1_sb[:, bass.ds(e, 1), :].rearrange("p e c -> p (e c)"), 1.0, None,
                                  ALU.mult).then_inc(b1_ready, 1)

            def finish(i, o):
                s = o % 2
                k = 2 * i + o
                e = dve.value_load(etile[0:1, bass.ds(k, 1)], min_val=0, max_val=NE - 1)
                dve.wait_ge(y_ps, k + 1)
                if not isinstance(i, int) or o >= 2:
                    dve.wait_ge(ys_written[s], 16 * (i + o // 2))
                dve.tensor_tensor(y_sb[:, s, :], ps1[:, 1, 0:D], b2_bc[:, bass.ds(e, 1), :].rearrange("p e d -> p (e d)"),
                                  ALU.add).then_inc(y_ready, 1)

            def expert_step(i, o):
                stage_w1(i, o + 1)
                rows_t(i, o + 1)
                finish(i, o - 1)

            stage_w1(0, 0)
            stage_w1(0, 1)
            rows_t(0, 1)
            for k in (1, 2):
                expert_step(0, k)
            with dve.Fori(0, (TILES - 4) // 2) as i:
                expert_step(i, 3)
                expert_step(i, 4)
            finish(0, TILES - 2)
            finish(0, TILES - 1)

            with dve.Fori(0, NB) as b:
                w = top_w[:, :, :].rearrange("p j k -> p (j k)")
                for k, (j0, j1) in enumerate(PARTS):
                    dve.wait_ge(y_taken[k], (b + 1) * K2 * (j1 - j0) * 16)
                    for c, done in ((0, y_first), (1, summed)):
                        for jj in range(j0, j1):
                            j = b * JB + jj
                            xj = x_sb[:, bass.ds(j, 1), :].rearrange("p j d -> p (j d)")
                            if c:
                                dve.wait_ge(y_first, j + 1)
                            dve.scalar_tensor_tensor(out=xj, in0=y_st[:, jj, c, :], scalar=w[:, bass.ds(K2 * j + c, 1)], in1=xj,
                                                     op0=ALU.mult, op1=ALU.add).then_inc(done, 1)


_INS = ["x", "src", "dst", "edge_attr_3"] + ["L0_gnn_" + n for n in (
    "lin_src_w0", "lin_src_w1", "tp1_w00", "tp1_w11", "tp1_w01", "tp1_w10", "tp2_w00", "tp2_w11", "tp2_w01", "tp2_w10",
    "lin_hidden_w0", "lin_hidden_w1", "lin_scalar_w")] + ["L0_mix_" + n for n in (
    "kln_weight", "kln_bias", "vln_weight", "vln_bias")] + ["L0_ffn_" + n for n in ("Wg", "bg", "W1", "b1", "W2", "b2")]


def kernel(**inputs):
    import numpy as _np
    import concourse.bacc as _bacc
    from concourse import mybir as _mybir
    from concourse.bass_utils import run_bass_kernel_spmd as _run

    nc = _bacc.Bacc("TRN2", target_bir_lowering=False, num_devices=1)
    arrays, args = {}, {}
    for name in _INS:
        a = _np.ascontiguousarray(inputs[name])
        arrays[f"in_{name}"] = a
        args[name] = nc.dram_tensor(f"in_{name}", a.shape, _mybir.dt.from_np(a.dtype), kind="ExternalInput").ap()
    shape = inputs["x"].shape
    out = nc.dram_tensor("out_0", shape, _mybir.dt.float32, kind="ExternalOutput").ap()
    gps_layer_kernel(nc, args, out)
    r = _run(nc, [arrays], core_ids=[0])
    return r.results[0]["out_0"]
```
